# Optimizing a Trainium2 kernel written in Bass

```python
import numpy as np
import jax
import jax.numpy as jnp

def _softmax(x, axis=-1):
    return jax.nn.softmax(x, axis=axis)

def _gelu(x):
    return jax.nn.gelu(x, approximate=True)

def _silu(x):
    return jax.nn.silu(x)

def _sigmoid(x):
    return jax.nn.sigmoid(x)

def _layernorm(x, axis=-1, eps=1e-05):
    m = jnp.mean(x, axis=axis, keepdims=True)
    v = jnp.var(x, axis=axis, keepdims=True)
    return (x - m) / jnp.sqrt(v + eps)

def _scatter_add(tgt, idx, src, axis=0):
    return tgt.at[idx].add(src)

def _segment_sum(src, seg, n):
    return jax.ops.segment_sum(src, seg, n)
kernel_name = 'mk_xattn_ffn_d2_seqx_r8_2ce5c8'

def setup_inputs(seed: int=0):
    np.random.seed(seed)
    _w = jnp.asarray

    def _rec_inputs():
        import jax
        import jax.numpy as jnp
        _rk = jax.random.key(seed)
        x = -0.0005207 + 1.001 * jax.random.normal(jax.random.fold_in(_rk, 1), (32, 64, 256), jnp.float32)
        _lenS = 64 - jax.random.randint(jax.random.fold_in(_rk, 7), (32,), 0, max(1, 64 // 4) + 1, jnp.int32)
        _lenS2 = 64 - jax.random.randint(jax.random.fold_in(_rk, 8), (32,), 0, max(1, 64 // 4) + 1, jnp.int32)
        _ctx_2048P = jax.random.normal(jax.random.fold_in(_rk, 12), (32, 16, 256), jnp.float32)
        _ctx_2048c = jax.random.dirichlet(jax.random.fold_in(_rk, 512), 0.3 * jnp.ones((16,), jnp.float32), (32, 64))
        _ctx_2048t = jnp.einsum('bsk,bkd->bsd', _ctx_2048c, _ctx_2048P)
        _ctx_2048t = _ctx_2048t * jax.lax.rsqrt(jnp.mean(jnp.square(_ctx_2048t)) + 1e-12) * 0.953939
        ctx_2048 = -5.72187e-05 + 0.999849 * (_ctx_2048t + 0.3 * jax.random.normal(jax.random.fold_in(_rk, 612), (32, 64, 256), jnp.float32))
        _validS = jnp.arange(64)[None, :] < _lenS[:, None]
        _validS2 = jnp.arange(64)[None, :] < _lenS2[:, None]
        _causal = jnp.tril(jnp.ones((64, 64), dtype=bool))
        mask_BxSx4224_bf0 = jnp.logical_not(jnp.ones((32, 64, 528), dtype=bool))
        return (x, ctx_2048, mask_BxSx4224_bf0)
    x, ctx_2048, mask_BxSx4224_bf0 = _rec_inputs()

    def _L0_xattn_setup():
        import jax, jax.numpy as jnp
        import numpy as np
        import math
        DIM = 256
        B, Q_LEN, KV_LEN = (8, 128, 512)
        key = jax.random.key(seed)
        ks = jax.random.split(key, 8)
        x = jax.random.normal(ks[0], (B, Q_LEN, DIM), dtype=jnp.float32)
        mask = jnp.zeros((B, Q_LEN, KV_LEN + Q_LEN), dtype=bool)
        k_cache = jax.random.normal(ks[1], (B, KV_LEN, DIM), dtype=jnp.float32)
        v_cache = jax.random.normal(ks[2], (B, KV_LEN, DIM), dtype=jnp.float32)
        scale = 1.0 / math.sqrt(DIM)
        wq = jax.random.normal(ks[3], (DIM, DIM), dtype=jnp.float32) * scale
        wk = jax.random.normal(ks[4], (DIM, DIM), dtype=jnp.float32) * scale
        wv = jax.random.normal(ks[5], (DIM, DIM), dtype=jnp.float32) * scale
        wo = jax.random.normal(ks[6], (DIM, DIM), dtype=jnp.float32) * scale
        return {'x': x, 'mask': mask, 'k_cache': k_cache, 'v_cache': v_cache, 'wq': wq, 'wk': wk, 'wv': wv, 'wo': wo}
    _L0_xattn_all = _L0_xattn_setup()
    _L0_xattn_in = {k: v for k, v in _L0_xattn_all.items() if k in ('wq', 'wk', 'wv', 'wo')}
    del _L0_xattn_all

    def _L0_ffn_setup():
        import jax, jax.numpy as jnp
        import numpy as np
        EPS = 1e-05

        def weight_quant(w):
            scale = 1.0 / jnp.clip(jnp.mean(jnp.abs(w)), EPS, None)
            return jnp.clip(jnp.round(w * scale), -1.0, 1.0) / scale

        def act_quant(x):
            scale = 127.0 / jnp.clip(jnp.max(jnp.abs(x), axis=-1, keepdims=True), EPS, None)
            return jnp.clip(jnp.round(x * scale), -128.0, 127.0) / scale

        def bitlinear(x, w):
            return jnp.einsum('bsd,od->bso', act_quant(x), weight_quant(w))
        key = jax.random.key(seed)
        k1, k2, k3, k4 = jax.random.split(key, 4)
        B, S, D = (4, 256, 256)
        I = int(np.ceil(D * np.pi / 64) * 64)
        x = jax.random.normal(k1, (B, S, D), dtype=jnp.float32)
        w_gate = jax.random.normal(k2, (I, D), dtype=jnp.float32) * 0.02
        w_up = jax.random.normal(k3, (I, D), dtype=jnp.float32) * 0.02
        w_down = jax.random.normal(k4, (D, I), dtype=jnp.float32) * 0.02
        return {'x': x, 'w_gate': w_gate, 'w_up': w_up, 'w_down': w_down}
    _L0_ffn_all = _L0_ffn_setup()
    _L0_ffn_in = {k: v for k, v in _L0_ffn_all.items() if k in ('w_gate', 'w_up', 'w_down')}
    del _L0_ffn_all

    def _L1_xattn_setup():
        import math
        import jax, jax.numpy as jnp
        import numpy as np
        N_HEADS = 8
        CHANNELS = 64
        K_CH = CHANNELS // N_HEADS
        THETA = 10000.0

        def _rope_freqs(length, dim):
            inv_freq = 1.0 / THETA ** (jnp.arange(0, dim, 2, dtype=jnp.float32) / dim)
            f = jnp.arange(length, dtype=jnp.float32)[:, None] * inv_freq[None, :]
            return jnp.concatenate([f, f], axis=-1)

        def _apply_rotary(pos, t):
            half = t.shape[-1] // 2
            rot = jnp.concatenate([-t[..., half:], t[..., :half]], axis=-1)
            return t * jnp.cos(pos) + rot * jnp.sin(pos)

        def _proj(inp, W, b):
            return jnp.einsum('oc,bct->bot', W, inp) + b[None, :, None]
        key = jax.random.key(seed)
        ks = jax.random.split(key, 10)
        B, C, T = (4, CHANNELS, 256)
        bound = math.sqrt(6.0 / (C + C))

        def w(k):
            return jax.random.uniform(k, (C, C), jnp.float32, -bound, bound)
        return {'x': jax.random.normal(ks[0], (B, C, T), jnp.float32), 'c': jax.random.normal(ks[1], (B, C, T), jnp.float32), 'Wq': w(ks[2]), 'bq': jnp.zeros((C,), jnp.float32), 'Wk': w(ks[3]), 'bk': jnp.zeros((C,), jnp.float32), 'Wv': w(ks[4]), 'bv': jnp.zeros((C,), jnp.float32), 'Wo': w(ks[5]), 'bo': jnp.zeros((C,), jnp.float32)}
    _L1_xattn_all = _L1_xattn_setup()
    _L1_xattn_in = {k: v for k, v in _L1_xattn_all.items() if k in ('Wq', 'bq', 'Wk', 'bk', 'Wv', 'bv', 'Wo', 'bo')}
    del _L1_xattn_all

    def _L1_ffn_setup():
        import jax, jax.numpy as jnp
        import numpy as np
        D_MODEL = 256
        NUM_TILES = 64
        D_SLICE = D_MODEL // NUM_TILES
        TILES_PER_CLUSTER = 8
        NUM_CLUSTERS = NUM_TILES // TILES_PER_CLUSTER
        GRID = 16
        LN_EPS = 1e-05
        DIMS = (np.arange(NUM_TILES)[:, None] * D_SLICE + np.arange(D_SLICE)[None, :]) % D_MODEL
        DIMS = jnp.asarray(DIMS, dtype=jnp.int32)

        def _forward(x, ln_gamma, ln_beta, spline_bases, spline_slopes, output_scale):
            B, S, D = x.shape
            N = B * S
            mu = jnp.mean(x, axis=-1, keepdims=True)
            var = jnp.mean(jnp.square(x - mu), axis=-1, keepdims=True)
            xn = (x - mu) * jax.lax.rsqrt(var + LN_EPS) * ln_gamma + ln_beta
            xf = xn.reshape(N, D)
            slope_sign = jnp.sign(jnp.mean(spline_slopes, axis=-1))
            tile_sigs = jnp.zeros((NUM_TILES, D), dtype=x.dtype)
            tile_sigs = tile_sigs.at[jnp.arange(NUM_TILES)[:, None], DIMS].set(slope_sign)
            cluster_sigs = jnp.sign(tile_sigs.reshape(NUM_CLUSTERS, TILES_PER_CLUSTER, D).mean(axis=1))
            cluster_assign = jnp.arange(NUM_TILES, dtype=jnp.int32) // TILES_PER_CLUSTER
            input_sigs = jnp.sign(xf)
            cluster_scores = input_sigs @ cluster_sigs.T
            best_cluster = jnp.argmax(cluster_scores, axis=-1)
            tile_scores = input_sigs @ tile_sigs.T
            in_cluster = cluster_assign[None, :] == best_cluster[:, None]
            tile_idx = jnp.argmax(jnp.where(in_cluster, tile_scores, -jnp.inf), axis=-1)
            tok_dims = DIMS[tile_idx]
            x_slice = jnp.take_along_axis(xf, tok_dims, axis=1)
            tok_min = x_slice.min(axis=1)
            tok_max = x_slice.max(axis=1)
            onehot = tile_idx[None, :] == jnp.arange(NUM_TILES)[:, None]
            tile_min = jnp.where(onehot, tok_min[None, :], jnp.inf).min(axis=1)
            tile_max = jnp.where(onehot, tok_max[None, :], -jnp.inf).max(axis=1)
            mn = tile_min[tile_idx][:, None]
            mx = tile_max[tile_idx][:, None]
            u = jnp.clip((x_slice - mn) / (mx - mn + 1e-08), 0.0, 1.0 - 1e-06)
            gi = jnp.clip((u * GRID).astype(jnp.int32), 0, GRID - 1)
            j = jnp.arange(D_SLICE)[None, :]
            b = spline_bases[tile_idx[:, None], j, gi]
            s = spline_slopes[tile_idx[:, None], j, gi]
            x_local = (u - gi.astype(u.dtype) / GRID) * GRID
            delta = (b + s * x_local) * output_scale[tile_idx][:, None]
            out = jnp.zeros_like(xf).at[jnp.arange(N)[:, None], tok_dims].set(delta)
            return x + out.reshape(B, S, D)
        key = jax.random.key(seed)
        k1, k2, k3, k4, k5, k6 = jax.random.split(key, 6)
        x = jax.random.normal(k1, (4, 512, D_MODEL), dtype=jnp.float32)
        ln_gamma = 1.0 + 0.1 * jax.random.normal(k2, (D_MODEL,), dtype=jnp.float32)
        ln_beta = 0.1 * jax.random.normal(k3, (D_MODEL,), dtype=jnp.float32)
        spline_bases = 0.1 * jax.random.normal(k4, (NUM_TILES, D_SLICE, GRID), dtype=jnp.float32)
        spline_slopes = 0.1 + 0.1 * jax.random.normal(k5, (NUM_TILES, D_SLICE, GRID), dtype=jnp.float32)
        output_scale = 1.0 + 0.1 * jax.random.normal(k6, (NUM_TILES,), dtype=jnp.float32)
        return {'x': x, 'ln_gamma': ln_gamma, 'ln_beta': ln_beta, 'spline_bases': spline_bases, 'spline_slopes': spline_slopes, 'output_scale': output_scale}
    _L1_ffn_all = _L1_ffn_setup()
    _L1_ffn_in = {k: v for k, v in _L1_ffn_all.items() if k in ('ln_gamma', 'ln_beta', 'spline_bases', 'spline_slopes', 'output_scale')}
    del _L1_ffn_all
    return {'x': x, 'ctx_2048': ctx_2048, 'mask_BxSx4224_bf0': mask_BxSx4224_bf0, 'L0_xattn_wq': _L0_xattn_in['wq'], 'L0_xattn_wk': _L0_xattn_in['wk'], 'L0_xattn_wv': _L0_xattn_in['wv'], 'L0_xattn_wo': _L0_xattn_in['wo'], 'L0_ffn_w_gate': _L0_ffn_in['w_gate'], 'L0_ffn_w_up': _L0_ffn_in['w_up'], 'L0_ffn_w_down': _L0_ffn_in['w_down'], 'L1_xattn_Wq': _L1_xattn_in['Wq'], 'L1_xattn_bq': _L1_xattn_in['bq'], 'L1_xattn_Wk': _L1_xattn_in['Wk'], 'L1_xattn_bk': _L1_xattn_in['bk'], 'L1_xattn_Wv': _L1_xattn_in['Wv'], 'L1_xattn_bv': _L1_xattn_in['bv'], 'L1_xattn_Wo': _L1_xattn_in['Wo'], 'L1_xattn_bo': _L1_xattn_in['bo'], 'L1_ffn_ln_gamma': _L1_ffn_in['ln_gamma'], 'L1_ffn_ln_beta': _L1_ffn_in['ln_beta'], 'L1_ffn_spline_bases': _L1_ffn_in['spline_bases'], 'L1_ffn_spline_slopes': _L1_ffn_in['spline_slopes'], 'L1_ffn_output_scale': _L1_ffn_in['output_scale']}

def reference(x, ctx_2048, mask_BxSx4224_bf0, L0_xattn_wq, L0_xattn_wk, L0_xattn_wv, L0_xattn_wo, L0_ffn_w_gate, L0_ffn_w_up, L0_ffn_w_down, L1_xattn_Wq, L1_xattn_bq, L1_xattn_Wk, L1_xattn_bk, L1_xattn_Wv, L1_xattn_bv, L1_xattn_Wo, L1_xattn_bo, L1_ffn_ln_gamma, L1_ffn_ln_beta, L1_ffn_spline_bases, L1_ffn_spline_slopes, L1_ffn_output_scale):
    import jax
    import jax.numpy as jnp

    def _L0_xattn_ref(x, mask, k_cache, v_cache, wq, wk, wv, wo):
        import jax, jax.numpy as jnp
        import numpy as np
        import math
        DIM = 256
        B, Q_LEN, KV_LEN = (8, 128, 512)
        q = jnp.einsum('bsd,ed->bse', x, wq)
        k_new = jnp.einsum('bsd,ed->bse', x, wk)
        v_new = jnp.einsum('bsd,ed->bse', x, wv)
        k = jnp.concatenate([k_cache, k_new], axis=1)
        v = jnp.concatenate([v_cache, v_new], axis=1)
        scale = 1.0 / math.sqrt(q.shape[-1])
        scores = jnp.einsum('bqd,bkd->bqk', q, k) * scale
        attn = jax.nn.softmax(scores, axis=-1)
        out = jnp.einsum('bqk,bkd->bqd', attn, v)
        return jnp.einsum('bqd,ed->bqe', out, wo)

    def _L0_ffn_ref(x, w_gate, w_up, w_down):
        import jax, jax.numpy as jnp
        import numpy as np
        EPS = 1e-05

        def weight_quant(w):
            scale = 1.0 / jnp.clip(jnp.mean(jnp.abs(w)), EPS, None)
            return jnp.clip(jnp.round(w * scale), -1.0, 1.0) / scale

        def act_quant(x):
            scale = 127.0 / jnp.clip(jnp.max(jnp.abs(x), axis=-1, keepdims=True), EPS, None)
            return jnp.clip(jnp.round(x * scale), -128.0, 127.0) / scale

        def bitlinear(x, w):
            return jnp.einsum('bsd,od->bso', act_quant(x), weight_quant(w))
        gate = jax.nn.silu(bitlinear(x, w_gate))
        up = bitlinear(x, w_up)
        return bitlinear(gate * up, w_down)

    def _L1_xattn_ref(x, c, Wq, bq, Wk, bk, Wv, bv, Wo, bo):
        import math
        import jax, jax.numpy as jnp
        import numpy as np
        N_HEADS = 8
        CHANNELS = 64
        K_CH = CHANNELS // N_HEADS
        THETA = 10000.0

        def _rope_freqs(length, dim):
            inv_freq = 1.0 / THETA ** (jnp.arange(0, dim, 2, dtype=jnp.float32) / dim)
            f = jnp.arange(length, dtype=jnp.float32)[:, None] * inv_freq[None, :]
            return jnp.concatenate([f, f], axis=-1)

        def _apply_rotary(pos, t):
            half = t.shape[-1] // 2
            rot = jnp.concatenate([-t[..., half:], t[..., :half]], axis=-1)
            return t * jnp.cos(pos) + rot * jnp.sin(pos)

        def _proj(inp, W, b):
            return jnp.einsum('oc,bct->bot', W, inp) + b[None, :, None]
        b, _, t_t = x.shape
        t_s = c.shape[2]
        q_emb = _rope_freqs(t_t, K_CH)
        k_emb = _rope_freqs(t_s, K_CH)

        def split_heads(t):
            return t.reshape(b, N_HEADS, K_CH, t.shape[2]).transpose(0, 1, 3, 2)
        q = split_heads(_proj(x, Wq, bq))
        k = split_heads(_proj(c, Wk, bk))
        v = split_heads(_proj(c, Wv, bv))
        q = _apply_rotary(q_emb, q)
        k = _apply_rotary(k_emb, k)
        scores = jnp.einsum('bhtc,bhsc->bhts', q, k) / math.sqrt(K_CH)
        p_attn = jax.nn.softmax(scores, axis=-1)
        out = jnp.einsum('bhts,bhsc->bhtc', p_attn, v)
        out = out.transpose(0, 1, 3, 2).reshape(b, N_HEADS * K_CH, t_t)
        return _proj(out, Wo, bo)

    def _L1_ffn_ref(x, ln_gamma, ln_beta, spline_bases, spline_slopes, output_scale):
        import jax, jax.numpy as jnp
        import numpy as np
        D_MODEL = 256
        NUM_TILES = 64
        D_SLICE = D_MODEL // NUM_TILES
        TILES_PER_CLUSTER = 8
        NUM_CLUSTERS = NUM_TILES // TILES_PER_CLUSTER
        GRID = 16
        LN_EPS = 1e-05
        DIMS = (np.arange(NUM_TILES)[:, None] * D_SLICE + np.arange(D_SLICE)[None, :]) % D_MODEL
        DIMS = jnp.asarray(DIMS, dtype=jnp.int32)

        def _forward(x, ln_gamma, ln_beta, spline_bases, spline_slopes, output_scale):
            B, S, D = x.shape
            N = B * S
            mu = jnp.mean(x, axis=-1, keepdims=True)
            var = jnp.mean(jnp.square(x - mu), axis=-1, keepdims=True)
            xn = (x - mu) * jax.lax.rsqrt(var + LN_EPS) * ln_gamma + ln_beta
            xf = xn.reshape(N, D)
            slope_sign = jnp.sign(jnp.mean(spline_slopes, axis=-1))
            tile_sigs = jnp.zeros((NUM_TILES, D), dtype=x.dtype)
            tile_sigs = tile_sigs.at[jnp.arange(NUM_TILES)[:, None], DIMS].set(slope_sign)
            cluster_sigs = jnp.sign(tile_sigs.reshape(NUM_CLUSTERS, TILES_PER_CLUSTER, D).mean(axis=1))
            cluster_assign = jnp.arange(NUM_TILES, dtype=jnp.int32) // TILES_PER_CLUSTER
            input_sigs = jnp.sign(xf)
            cluster_scores = input_sigs @ cluster_sigs.T
            best_cluster = jnp.argmax(cluster_scores, axis=-1)
            tile_scores = input_sigs @ tile_sigs.T
            in_cluster = cluster_assign[None, :] == best_cluster[:, None]
            tile_idx = jnp.argmax(jnp.where(in_cluster, tile_scores, -jnp.inf), axis=-1)
            tok_dims = DIMS[tile_idx]
            x_slice = jnp.take_along_axis(xf, tok_dims, axis=1)
            tok_min = x_slice.min(axis=1)
            tok_max = x_slice.max(axis=1)
            onehot = tile_idx[None, :] == jnp.arange(NUM_TILES)[:, None]
            tile_min = jnp.where(onehot, tok_min[None, :], jnp.inf).min(axis=1)
            tile_max = jnp.where(onehot, tok_max[None, :], -jnp.inf).max(axis=1)
            mn = tile_min[tile_idx][:, None]
            mx = tile_max[tile_idx][:, None]
            u = jnp.clip((x_slice - mn) / (mx - mn + 1e-08), 0.0, 1.0 - 1e-06)
            gi = jnp.clip((u * GRID).astype(jnp.int32), 0, GRID - 1)
            j = jnp.arange(D_SLICE)[None, :]
            b = spline_bases[tile_idx[:, None], j, gi]
            s = spline_slopes[tile_idx[:, None], j, gi]
            x_local = (u - gi.astype(u.dtype) / GRID) * GRID
            delta = (b + s * x_local) * output_scale[tile_idx][:, None]
            out = jnp.zeros_like(xf).at[jnp.arange(N)[:, None], tok_dims].set(delta)
            return x + out.reshape(B, S, D)
        return _forward(x, ln_gamma, ln_beta, spline_bases, spline_slopes, output_scale)
    x = x + _L0_xattn_ref(_layernorm(x, axis=-1), mask_BxSx4224_bf0, ctx_2048, ctx_2048, L0_xattn_wq, L0_xattn_wk, L0_xattn_wv, L0_xattn_wo)
    x = x + _L0_ffn_ref(_layernorm(x, axis=-1), L0_ffn_w_gate, L0_ffn_w_up, L0_ffn_w_down)
    x = x + _L1_xattn_ref(_layernorm(x, axis=-1), ctx_2048, L1_xattn_Wq, L1_xattn_bq, L1_xattn_Wk, L1_xattn_bk, L1_xattn_Wv, L1_xattn_bv, L1_xattn_Wo, L1_xattn_bo)
    x = x + _L1_ffn_ref(_layernorm(x, axis=-1), L1_ffn_ln_gamma, L1_ffn_ln_beta, L1_ffn_spline_bases, L1_ffn_spline_slopes, L1_ffn_output_scale)
    return x

_drawn_inputs = setup_inputs


def setup_inputs(seed=0):
    import zlib

    import numpy as np

    out = dict(_drawn_inputs(seed))
    spreads = {'L1_xattn_bq': (0.0, 0.425),
     'L1_xattn_bk': (0.0, 0.739),
     'L1_xattn_bv': (0.0, 0.29),
     'L1_xattn_bo': (0.0, 0.318)}
    factors = {'L0_ffn_w_gate': 5.936,
     'L0_ffn_w_up': 5.537,
     'L0_ffn_w_down': 5.515,
     'L1_ffn_ln_gamma': 8.0,
     'L1_ffn_ln_beta': 8.0,
     'L1_ffn_spline_bases': 8.0,
     'L1_ffn_spline_slopes': 8.0,
     'L1_ffn_output_scale': 8.0}
    for name, (base, spread) in spreads.items():
        noise = np.random.default_rng([zlib.crc32(name.encode()), seed]).standard_normal(out[name].shape)
        drawn = base * np.exp(spread * noise) if base else spread * noise
        out[name] = jnp.asarray(drawn.astype(out[name].dtype))
    for name, factor in factors.items():
        out[name] = (out[name] * factor).astype(out[name].dtype)
    return out
```

```python
from contextlib import ExitStack

import concourse.bass as bass
from concourse import mybir

F32 = mybir.dt.float32
BF16 = mybir.dt.bfloat16
ALU = mybir.AluOpType
ACT = mybir.ActivationFunctionType
AX = mybir.AxisListType.X

P = 128
B, S, D = 32, 64, 256
NT = B * S // P
DC = D // P
UNITS = NT // 2
FF = 832
FH = FF // 2
FK, FP = 8, FF // 8
HEADS, HC = 8, 8
PAIRS = HEADS // 2
NTILE, SLICE, GRID, CLUSTERS = 64, 4, 16, 8
LN_EPS = 1e-5
Q_EPS = 1e-5
MAGIC = 12582912.0
BIG = 3.0e38
NBUF = 3
GRANULES = 8
MAXG = 16
SPREADS = 14

SEMS = """
x_loaded attn_w_loaded wo_loaded chan_w_loaded ffn_w_loaded ident_loaded ctxT_loaded ctxV_loaded ffn2_loaded
const_ready ident_ready ones_row_placed oz_ready
wsum_ready wtot_ready wmean_ready winv_ready w_clip w_round w_ready
bo_sum_ready bo_ready
ln1_steps ln1_var ln1_rstd xn_ready
xT_psum xT_ready q_psum q_ready k_psum k_ready v_psum v_ready
s_psum s_max nmax_ready probs_ready pT_psum pT_ready rsum_ready oT_psum oT_ready y_psum x1_ready
ln2_steps ln2_var ln2_rstd xn2_ready amax_ready amaxc_ready arec_ready ascale_ready
a_round xq_ready act_scale1 act_scale2 act_scale3
xqT_psum xqT_ready xh_ready xhT_psum xhT_ready gateup_psum gate_ready up_ready
h_half h_ready hamax_ready hamaxc_ready hrec_ready hscale_ready h_round hq_ready dscale_ready
hT_psum hT_ready down_psum x2_ready
ln3_steps ln3_var ln3_rstd xn3_ready
qproj_psum kproj_psum vproj_psum rope_q rope_k qk_sum part1 rest1 part2 parts_ready
parts_stored vz_ready
max_psum max_ready maxT_psum maxT_ready maxrow_done
sT_psum exp_ready av_psum den_inv o_ready yc_psum x3_ready
ln4_steps ln4_var ln4_rstd xn4_ready
ln5_steps ln5_var ln5_rstd xn5_ready gamma_done xf_ready
sgn_prod sgn_neg sgn_ready tile_score clus_score key_c key_ready key_max onehot_ready
xf_masked x4_ready slice_ready
slope_sum slope_neg sig_ready
min_part max_part
spline_step mm_psum mm_ready ohT_psum ohT_ready look_psum look_ready

delta_ready place_dve place_pool out_pool out_dve out_stored
""".split()


def decoder_kernel(nc, A, out):
    with ExitStack() as ctx:
        def sb(name, shape, dt=F32):
            return ctx.enter_context(nc.sbuf_tensor(name, shape, dt))

        sem = {name: ctx.enter_context(nc.semaphore(name)) for name in SEMS}
        ctx_loaded = [ctx.enter_context(nc.semaphore(f"ctx_loaded{i}")) for i in range(NBUF)]
        spread_done = [ctx.enter_context(nc.semaphore(f"spread_done{i}")) for i in range(NBUF)]

        def tile(turn, off):
            return turn * NBUF + off, off % NBUF, turn + off // NBUF

        xall = sb("xall", [P, NT, D])
        ident = sb("ident", [P, P])
        identb = sb("identb", [P, P], BF16)
        ones = sb("ones", [P, P])
        halfneg = sb("halfneg", [P, 2])
        wattn = sb("wattn", [P, 4 * DC * D])
        wqT, wkT, wvT, woT = (wattn[:, i * DC * D:(i + 1) * DC * D].rearrange("p (c d) -> p c d", c=DC) for i in range(4))
        PB = sb("PB", [P, GRANULES, 4 * D])
        pbf = PB[:, :, :].rearrange("p g n -> p (g n)")
        slopes = pbf[:, 0:D * GRID].rearrange("p (d g) -> p d g", g=GRID)
        wffn = pbf[:, 4096:4096 + 2 * DC * FF].rearrange("p (a n) -> p a n", a=2)
        lookf = sb("lookf", [P, NT * 131])
        look = lookf[:, :].rearrange("p (n c) -> p n c", n=NT)
        wdn = lookf[0:FP, 0:FK * D]
        outf = sb("outf", [P, NT * D])
        outb = outf[:, :].rearrange("p (n d) -> p n d", n=NT)
        wgT = sb("wgT", [P, DC, FF], BF16)
        wuT = wffn[:, 1, :].rearrange("p (c f) -> p c f", c=DC)
        wdT = sb("wdT", [FP, FK, D], BF16)
        wsum = sb("wsum", [P, 4])
        wmean = sb("wmean", [P, 4])
        winv = sb("winv", [P, 4])
        wm127 = sb("wm127", [P, 4])
        st1 = sb("st1", [P, 2, 6])
        mv1 = sb("mv1", [P, 2, 2])
        ve1 = sb("ve1", [P, 2])
        rs1 = sb("rs1", [P, 2])
        xn = sb("xn", [P, 2, D])
        xnT = sb("xnT", [P, DC, 2 * P])
        qT = sb("qT", [P, DC, 2 * P])
        kT = sb("kT", [P, DC, 2, 4 * S])
        vb = sb("vb", [P, 2, 2, D])
        nmax = sb("nmax", [P, 2])
        nmaxs = sb("nmaxs", [P, 2])
        probs = sb("probs", [P, 2, P])
        psums = sb("psums", [P, 2])
        pinv = sb("pinv", [P, 2])
        pT = sb("pT", [P, 2, P])
        oT = sb("oT", [P, DC, 2 * P])
        st2 = sb("st2", [P, 2, 6])
        mv2 = sb("mv2", [P, 2, 2])
        ve2 = sb("ve2", [P, 2])
        rs2 = sb("rs2", [P, 2])
        hold = sb("hold", [P, 2])
        hold2 = sb("hold2", [P, 2])
        xn2 = sb("xn2", [P, 2, D])
        amax = sb("amax", [P, 2])
        amaxc = sb("amaxc", [P, 2])
        arec = sb("arec", [P, 2])
        ascale = sb("ascale", [P, 2])
        xq = sb("xq", [P, 2, D], BF16)
        xh = sb("xh", [P, 2, D])
        xhT = sb("xhT", [P, DC, 2 * P])
        ainv = sb("ainv", [P, 2])
        aG = sb("aG", [P, 2])
        aGh = sb("aGh", [P, 2])
        xqT = sb("xqT", [P, DC, 2 * P], BF16)
        th = outf[:, 0 * FF:1 * FF]
        us = outf[:, 1 * FF:2 * FF]
        h1 = outf[:, 2 * FF:3 * FF]
        h2 = outf[:, 3 * FF:4 * FF]
        hm = sb("hm", [P, 4])
        hq = sb("hq", [P, FF], BF16)
        bD = sb("bD", [P, 1])
        hqT = sb("hqT", [FP, FK, P], BF16)
        wqb = sb("wqb", [P, 2, P])
        wkb = sb("wkb", [P, 2, P])
        wvb = sb("wvb", [P, P])
        wob = sb("wob", [P, P])
        bias = sb("bias", [P, 8])
        boe = sb("boe", [P, 1])
        cos = sb("cos", [P, D])
        sin = sb("sin", [P, D])
        cst = [sb(f"cst{i}", [P, D]) for i in range(NBUF)]
        st3 = sb("st3", [P, 6])
        mv3 = sb("mv3", [P, 2])
        ve3 = sb("ve3", [P, 1])
        rs3 = sb("rs3", [P, 1])
        xn3 = sb("xn3", [P, D])
        rope = wattn[:, 0:4 * D].rearrange("p (a i d) -> p a i d", a=2, i=2)
        qk = wattn[:, 4 * D:6 * D].rearrange("p (a d) -> p a d", a=2)
        qkr = wattn[:, 6 * D:8 * D].rearrange("p (a d) -> p a d", a=2)
        parts = sb("parts", [P, 2, 3, D], BF16)
        QS = [sb(f"QS{i}", [P, 2, 2, PAIRS, D], BF16) for i in range(NBUF)]
        KS = [sb(f"KS{i}", [P, 2, PAIRS, D], BF16) for i in range(NBUF)]
        VZ = [sb(f"VZ{i}", [P, 8, 160]) for i in range(NBUF)]
        OZ = sb("OZ", [P, 160])
        rows = sb("rows", [33, 2 * PAIRS * D], BF16)
        row1, row0 = rows[0:1, :], rows[32:33, :]
        mx = sb("mx", [P, 2, 16])
        mxT = sb("mxT", [16, D], BF16)
        dinv = sb("dinv", [P, D])
        ob = sb("ob", [P, D])
        gam = sb("gam", [P, D])
        bet = sb("bet", [P, D])
        ssum = pbf[:, 7424:7424 + D]
        sneg = pbf[:, 7424 + D:7424 + 2 * D]
        sig = sb("sig", [P, D])
        ckey = sb("ckey", [P, NTILE])
        giota = sb("giota", [P, GRID])
        table = sb("table", [NTILE, 2 * SLICE * GRID + 3])
        st4 = sb("st4", [P, 6])
        mv4 = sb("mv4", [P, 2])
        ve4 = sb("ve4", [P, 2])
        rs4 = sb("rs4", [P, 2])
        st5 = sb("st5", [P, 6])
        mv5 = sb("mv5", [P, 2])
        kTf = kT[:, :, :, :].rearrange("p c j n -> p (c j n)")
        xn4, xn5, xf, wk1 = (kTf[:, i * D:(i + 1) * D] for i in range(4))
        wk2 = sb("wk2", [P, D])
        wk3 = sb("wk3", [P, D])
        tsc = sb("tsc", [P, NTILE])
        csc = sb("csc", [P, CLUSTERS])
        key1 = sb("key1", [P, NTILE])
        key2 = sb("key2", [P, NTILE])
        kmax = sb("kmax", [P, 1])
        oh = vb[:, :, :, :].rearrange("p a b (c t) -> p (a b c) t", t=NTILE)
        xs = sb("xs", [P, NT, SLICE])
        tmm = sb("tmm", [P, NT, 2])
        bigm = pbf[:, 0:1024].rearrange("p (n t) -> p n t", n=NT)
        cand = pbf[:, 1024:2048].rearrange("p (n t) -> p n t", n=NT)
        mpart = pbf[:, 2048:2048 + 2 * NTILE].rearrange("p (a t) -> p a t", a=2)
        gmask = pbf[:, 2304:3328]
        gprod = pbf[:, 3328:4352]
        ohT = pbf[0:NTILE, 6144:6144 + NT * P].rearrange("p (n t) -> p n t", n=NT)
        u0, u1, u2, u3, u4, u5 = [sb(f"u{i}", [P, NT, SLICE]) for i in range(6)]
        span = sb("span", [P, 4, NT])
        bsel = sb("bsel", [P, NT, SLICE])
        ssel = sb("ssel", [P, NT, SLICE])
        delta = sb("delta", [P, NT, SLICE])

        bk = [ctx.enter_context(nc.psum_tensor(f"bank{i}", [P, 512], F32)) for i in range(4)]
        big = ctx.enter_context(nc.psum_tensor("big", [P, 4, 512], F32))
        bankA, bankB, bankC, bankD = bk
        G = big[:, 0:2, 0:FH]
        U = big[:, 2:4, 0:FH]
        bankDb = bankD[:, :].bitcast(BF16)
        EX = [big[:, 2 * i:2 * i + 2, :].rearrange("p s n -> p (s n)") for i in range(2)]
        MXB = [bankA, bankB]
        AV = bankC
        MISC = bankD

        scr = [nc.dram_tensor(f"scr{i}", [6, P, D], BF16).ap() for i in range(NBUF)]

        block = ctx.enter_context(nc.Block())

        @block.sync
        def _(sp):
            sp.dma_start(ident[:, :], A["ident"]).then_inc(sem["ident_loaded"], 16)
            xin = A["x"].rearrange("(n two) s d -> (two s) n d", two=2)
            for j in range(4):
                sp.dma_start(xall[:, 4 * j:4 * j + 4, :], xin[:, 4 * j:4 * j + 4, :]).then_inc(sem["x_loaded"], 16)
            for dst, name in ((wqT, "wq"), (wkT, "wk"), (wvT, "wv")):
                sp.dma_start(dst[:, :, :], A[name].rearrange("(c p) e -> p c e", p=P)).then_inc(sem["attn_w_loaded"], 16)

            sp.dma_start(woT[:, :, :], A["wo"].rearrange("(c p) e -> p c e", p=P)).then_inc(sem["wo_loaded"], 16)
            for i, name in enumerate(("wg", "wu")):
                sp.dma_start(wffn[:, i, :].rearrange("p (c f) -> p c f", c=DC),
                             A[name].rearrange("(c p) f -> p c f", p=P)).then_inc(sem["ffn_w_loaded"], 16)
            sp.dma_start(wdn.rearrange("p (k d) -> p k d", k=FK),
                         A["wd"].rearrange("(k p) d -> p k d", p=FP)).then_inc(sem["ffn_w_loaded"], 16)
            for dst, name in ((wqb[:, :, :], "wqb"), (wkb[:, :, :], "wkb"), (wvb[:, :], "wvb"),
                              (wob[:, :], "wob"), (bias[:, 0:6], "bias"), (cos[:, :], "cos"), (sin[:, :], "sin")):
                sp.dma_start(dst, A[name]).then_inc(sem["chan_w_loaded"], 16)
            sp.dma_start(gam[:, :], A["gamma"].to_broadcast([P, D])).then_inc(sem["ffn2_loaded"], 16)
            sp.dma_start(bet[:, :], A["beta"].to_broadcast([P, D])).then_inc(sem["ffn2_loaded"], 16)
            sp.dma_start(pbf[:, 0:D * GRID],
                         A["slopes_row"].to_broadcast([P, D * GRID])).then_inc(sem["ffn2_loaded"], 16)
            sp.dma_start(table[:, 0:64], A["bases"]).then_inc(sem["ffn2_loaded"], 16)
            sp.dma_start(table[:, 64:128], A["slopes"]).then_inc(sem["ffn2_loaded"], 16)
            sp.dma_start(table[:, 130:131], A["oscale"]).then_inc(sem["ffn2_loaded"], 16)
            sp.dma_start(ckey[:, :], A["ckey"].to_broadcast([P, NTILE])).then_inc(sem["ffn2_loaded"], 16)
            sp.dma_start(giota[:, :], A["giota"].to_broadcast([P, GRID])).then_inc(sem["ffn2_loaded"], 16)
            sp.wait_ge(sem["const_ready"], 3)
            for i in range(NBUF):
                for par in range(2):
                    r = 64 * par + 48
                    sp.dma_start(KS[i][r:r + 1, :, :, :].rearrange("p b k t -> p (b k t)"),
                                 row1).then_inc(sem["ones_row_placed"], 16)
            def spread(t, u, w):
                sp.wait_ge(sem["parts_ready"], t + 1)
                sp.dma_start(scr[u].rearrange("r p t -> p r t"),
                             parts[:, :, :, :].rearrange("p a r t -> p (a r) t")).then_inc(sem["parts_stored"], 16)
                sp.wait_ge(sem["parts_stored"], (t + 1) * 16)
                sv = scr[u].rearrange("(a r) (par c g) t -> a par r c (g t)", a=2, par=2, c=HC)
                for par in range(2):
                    q0 = 64 * par
                    for at, n, piece in ((0, 3, 0), (3, 2, 1), (5, 1, 2)):
                        rows = slice(q0 + 8 * at, q0 + 8 * (at + n))
                        sp.dma_start(QS[u][rows, par, :, :, :].rearrange("p b k t -> p (b k t)"),
                                     sv[0, par, 0:n, :, :]).then_inc(spread_done[u], 16)
                        sp.dma_start(KS[u][rows, :, :, :].rearrange("p b k t -> p (b k t)"),
                                     sv[1, par, piece:piece + 1, :, :].to_broadcast([n, HC, 2048])
                                     ).then_inc(spread_done[u], 16)
                    sp.dma_start(QS[u][q0 + 48:q0 + 49, par, :, :, :].rearrange("p b k t -> p (b k t)"),
                                 row0).then_inc(spread_done[u], 16)

            def max_rows(t, u, w):
                sp.wait_ge(sem["maxT_ready"], t + 1)
                for par in range(2):
                    r = 64 * par + 48
                    sp.dma_start(QS[u][r:r + 1, par, :, :, :].rearrange("p b k t -> p (b k t)"),
                                 mxT[8 * par:8 * par + 8, :]).then_inc(sem["maxrow_done"], 16)

            spread(*tile(0, 0))
            spread(*tile(0, 1))
            max_rows(*tile(0, 0))

            def slot(turn, off):
                spread(*tile(turn, off + 2))
                max_rows(*tile(turn, off + 1))

            slot(0, 0)
            with sp.Fori(0, 4) as i:
                for r in range(1, 4):
                    slot(i, r)
            slot(0, 13)
            max_rows(*tile(0, 15))
            ov = out.rearrange("(n two) s d -> (two s) n d", two=2)
            for q in range(4):
                sp.wait_ge(sem["out_dve" if q % 2 == 0 else "out_pool"], q // 2 + 1)
                sp.dma_start(ov[:, 4 * q:4 * q + 4, :], outb[:, 4 * q:4 * q + 4, :]).then_inc(sem["out_stored"], 16)
            sp.wait_ge(sem["out_stored"], 64)

        @block.gpsimd
        def _(pool):
            nc.gpsimd.memset(row1, 1.0).then_inc(sem["const_ready"], 1)
            nc.gpsimd.memset(row0, 0.0).then_inc(sem["const_ready"], 1)
            pool.wait_ge(sem["const_ready"], 2)
            for i in range(NBUF):
                nc.gpsimd.memset(QS[i][:, :, :, :, :], 0.0)
                nc.gpsimd.memset(VZ[i][:, :, :], 0.0)
                last = nc.gpsimd.memset(KS[i][:, :, :, :], 0.0)
            last.then_inc(sem["const_ready"], 1)

            def rstd(name, ve, rs, t):
                pool.wait_ge(sem[name + "_var"], t + 1)
                w = ve.shape[1]
                nc.gpsimd.tensor_tensor(rs, ve, halfneg[:, 0:w], ALU.pow).then_inc(sem[name + "_rstd"], 1)

            pool.wait_ge(sem["ident_ready"], 1)
            rstd("ln1", ve1[:, :], rs1[:, :], 0)
            with pool.Fori(1, UNITS) as t:
                rstd("ln1", ve1[:, :], rs1[:, :], t)
                rstd("ln2", ve2[:, :], rs2[:, :], t - 1)
            rstd("ln2", ve2[:, :], rs2[:, :], UNITS - 1)

            def split(t):
                pool.wait_ge(sem["rope_k"], t + 1)
                nc.gpsimd.tensor_tensor(qk[:, :, :], rope[:, :, 0, :], rope[:, :, 1, :], ALU.add).then_inc(sem["qk_sum"], 1)
                pool.wait_ge(sem["qk_sum"], t + 1)
                pool.wait_ge(sem["parts_stored"], t * 16)
                nc.gpsimd.tensor_tensor(hold2[:, 0:1], halfneg[:, 0:1], halfneg[:, 1:2], ALU.add)
                nc.gpsimd.tensor_scalar(parts[:, :, 0, :], qk[:, :, :], 1.0, None, ALU.mult).then_inc(sem["part1"], 1)
                pool.wait_ge(sem["part1"], t + 1)
                nc.gpsimd.tensor_tensor(qkr[:, :, :], qk[:, :, :], parts[:, :, 0, :], ALU.subtract).then_inc(sem["rest1"], 1)
                pool.wait_ge(sem["rest1"], t + 1)
                nc.gpsimd.tensor_tensor(hold2[:, 1:2], halfneg[:, 0:1], halfneg[:, 1:2], ALU.add)
                nc.gpsimd.tensor_scalar(parts[:, :, 1, :], qkr[:, :, :], 1.0, None, ALU.mult).then_inc(sem["part2"], 1)
                pool.wait_ge(sem["part2"], t + 1)
                nc.gpsimd.tensor_tensor(parts[:, :, 2, :], qkr[:, :, :], parts[:, :, 1, :],
                                        ALU.subtract).then_inc(sem["parts_ready"], 1)

            def affine(t):
                pool.wait_ge(sem["xn5_ready"], t + 1)
                nc.gpsimd.tensor_tensor(wk3[:, :], xn5, gam[:, :], ALU.mult).then_inc(sem["gamma_done"], 1)
                pool.wait_ge(sem["gamma_done"], t + 1)
                pool.wait_ge(sem["xf_masked"], t)
                nc.gpsimd.tensor_tensor(xf, wk3[:, :], bet[:, :], ALU.add).then_inc(sem["xf_ready"], 1)

            rstd("ln3", ve3[:, :], rs3[:, :], 0)
            split(0)
            rstd("ln3", ve3[:, :], rs3[:, :], 1)
            split(1)
            pool.wait_ge(sem["ffn2_loaded"], 8 * 16)

            def slot(s, front=True, back=True):
                if front:
                    rstd("ln3", ve3[:, :], rs3[:, :], s + 2)
                if back:
                    rstd("ln4", ve4[:, 0:1], rs4[:, 0:1], s - 1)
                    rstd("ln5", ve4[:, 1:2], rs4[:, 1:2], s - 1)
                if front:
                    split(s + 2)
                if back:
                    affine(s - 1)

            slot(0, back=False)
            with pool.Fori(1, 14) as s:
                slot(s)
            slot(14, front=False)
            slot(15, front=False)
            slot(16, front=False)
            pool.wait_ge(sem["delta_ready"], 1)
            for q in (1, 3):
                for n in range(4 * q, 4 * q + 4):
                    nc.gpsimd.tensor_tensor(
                        outb[:, n, :].rearrange("p (t j) -> p t j", j=SLICE),
                        oh[:, n, :].unsqueeze(2).to_broadcast([P, NTILE, SLICE]),
                        delta[:, n, :].unsqueeze(1).to_broadcast([P, NTILE, SLICE]), ALU.mult).then_inc(sem["place_pool"], 1)
                pool.wait_ge(sem["place_pool"], 4 * (q // 2 + 1))
                nc.gpsimd.tensor_tensor(outb[:, 4 * q:4 * q + 4, :], outb[:, 4 * q:4 * q + 4, :],
                                        xall[:, 4 * q:4 * q + 4, :], ALU.add).then_inc(sem["out_pool"], 1)

        @block.scalar
        def _(act):
            def load_unit(t):
                act.wait_ge(sem["s_psum"], t)
                act.dma_start(kT[:, 0, :, S:3 * S], A["ctxT"][0:P, t, :, :]).then_inc(sem["ctxT_loaded"], 16)
                act.dma_start(kT[:, 1, :, S:3 * S], A["ctxT"][P:D, t, :, :]).then_inc(sem["ctxT_loaded"], 16)
                act.wait_ge(sem["oT_psum"], t)
                cv = A["ctx"].rearrange("(t j b) s d -> t b s j d", j=2, b=2)
                act.dma_start(vb[S:P, :, 0, :], cv[t, 0, :, :, :]).then_inc(sem["ctxV_loaded"], 16)
                act.dma_start(vb[0:S, :, 1, :], cv[t, 1, :, :, :]).then_inc(sem["ctxV_loaded"], 16)

            def a1_head(t):
                act.wait_ge(sem["xT_psum"], t + 1)
                nc.scalar.copy(xnT[:, :, :].rearrange("p c n -> p (c n)"), bankA[:, :]).then_inc(sem["xT_ready"], 1)

            def a1_qkv(t):
                act.wait_ge(sem["q_psum"], t + 1)
                nc.scalar.copy(qT[:, :, :].rearrange("p c n -> p (c n)"), bankA[:, :]).then_inc(sem["q_ready"], 1)
                act.wait_ge(sem["k_psum"], t + 1)
                nc.scalar.copy(kT[:, :, :, 0:S],
                               bankB[:, :].rearrange("p (c j n) -> p c j n", c=2, j=2)[:, :, :, 0:S])
                nc.scalar.copy(kT[:, :, :, 3 * S:4 * S],
                               bankB[:, :].rearrange("p (c j n) -> p c j n", c=2, j=2)[:, :, :, S:P]).then_inc(sem["k_ready"], 1)
                act.wait_ge(sem["v_psum"], t + 1)
                nc.scalar.copy(vb[0:S, :, 0, :], bankC[0:S, :].rearrange("p (j d) -> p j d", j=2))
                nc.scalar.copy(vb[S:P, :, 1, :], bankC[S:P, :].rearrange("p (j d) -> p j d", j=2)).then_inc(sem["v_ready"], 1)

            def a1_exp(t):
                act.wait_ge(sem["nmax_ready"], t + 1)
                for j in range(2):
                    last = nc.scalar.activation(probs[:, j, :], bankC[:, j * P:(j + 1) * P], ACT.Exp,
                                                bias=nmaxs[:, j:j + 1], scale=1.0 / 16.0, accum_out=psums[:, j:j + 1])
                last.then_inc(sem["probs_ready"], 1)

            def a1_pT(t):
                act.wait_ge(sem["pT_psum"], t + 1)
                nc.scalar.copy(pT[:, :, :].rearrange("p j n -> p (j n)"), bankC[:, 0:2 * P]).then_inc(sem["pT_ready"], 1)

            def a1_oT(t):
                act.wait_ge(sem["oT_psum"], t + 1)
                nc.scalar.copy(oT[:, :, :].rearrange("p c n -> p (c n)"), bankA[:, :]).then_inc(sem["oT_ready"], 1)

            def a2_xqT(t):
                act.wait_ge(sem["xqT_psum"], t + 1)
                nc.scalar.copy(xqT[:, :, :].rearrange("p c n -> p (c n)"), bankDb[:, 0:512]).then_inc(sem["xqT_ready"], 1)

            def a2_xhT(t):
                act.wait_ge(sem["xhT_psum"], t + 1)
                nc.scalar.copy(xhT[:, :, :].rearrange("p c n -> p (c n)"), big[:, 3, :]).then_inc(sem["xhT_ready"], 1)

            def a2_silu(t, j):
                act.wait_ge(sem["act_scale3"], t + 1)
                act.wait_ge(sem["gateup_psum"], 2 * t + j + 1)
                nc.scalar.activation(th.rearrange("p (a n) -> p a n", a=2), G, ACT.Tanh,
                                     scale=aGh[:, j:j + 1]).then_inc(sem["gate_ready"], 1)
                nc.scalar.activation(us.rearrange("p (a n) -> p a n", a=2), U, ACT.Copy,
                                     scale=aGh[:, j:j + 1]).then_inc(sem["up_ready"], 1)

            def a2_hT(t, j):
                act.wait_ge(sem["hT_psum"], 2 * t + j + 1)
                nc.scalar.copy(hqT[:, :, :].rearrange("p k n -> p (k n)"), bankDb[0:FP, :]).then_inc(sem["hT_ready"], 1)

            def a1(t):
                a1_head(t)
                a1_qkv(t)
                a1_exp(t)
                a1_pT(t)
                a1_oT(t)

            load_unit(0)
            a1(0)
            load_unit(1)
            def unit(t):
                a1_head(t)
                a2_xqT(t - 1)
                a1_qkv(t)
                a2_xhT(t - 1)
                a1_exp(t)
                a2_silu(t - 1, 0)
                a1_pT(t)
                a1_oT(t)
                a2_hT(t - 1, 0)
                a2_silu(t - 1, 1)
                a2_hT(t - 1, 1)

            with act.Fori(1, UNITS - 1) as t:
                unit(t)
                load_unit(t + 1)
            unit(UNITS - 1)
            a2_xqT(UNITS - 1)
            a2_xhT(UNITS - 1)
            for j in range(2):
                a2_silu(UNITS - 1, j)
                a2_hT(UNITS - 1, j)

            act.wait_ge(sem["const_ready"], 3)

            ctile = A["ctx"].rearrange("(n two) s d -> n (two s) d", two=2)

            def load_ctx(t, u, w):
                if not (isinstance(t, int) and t < NBUF):
                    act.wait_ge(sem["vproj_psum"], t - (NBUF - 1))
                act.dma_start(cst[u][:, :], ctile[t, :, :]).then_inc(ctx_loaded[u], 16)

            def v_out(t, u, w):
                act.wait_ge(sem["vproj_psum"], t + 1)
                nc.scalar.copy(VZ[u][:, :, :].rearrange("p k (a b) -> p k a b", b=40)[:, :, :, 0:HC],
                               MISC[:, 0:256].rearrange("p (k a c) -> p k a c", k=8, a=4)).then_inc(sem["vz_ready"], 1)

            def max_out(t):
                act.wait_ge(sem["maxT_psum"], t + 1)
                act.wait_ge(sem["maxrow_done"], t * 32)
                nc.scalar.activation(mxT[:, :], MISC[0:16, 0:256], ACT.Copy, scale=-1.0).then_inc(sem["maxT_ready"], 1)

            def exp(t, k, first=False):
                act.wait_ge(sem["sT_psum"], t * GRANULES + (k + 1))
                if not first:
                    act.wait_ge(sem["av_psum"], t * 2 + (k // 4 - 1))
                nc.scalar.activation(PB[:, k, :], EX[k % 2], ACT.Exp, scale=float(HC) ** -0.5).then_inc(sem["exp_ready"], 1)

            for t in range(NBUF):
                load_ctx(t, t, 0)
            v_out(*tile(0, 0))
            v_out(*tile(0, 1))
            max_out(0)

            def slot(turn, off, load=True, front=True, mid=True):
                s, first = tile(turn, off)[0], off == 0
                for k in range(GRANULES):
                    if k == 5 and front:
                        v_out(*tile(turn, off + 2))
                    exp(s, k, first)
                    if k == 1 and load:
                        load_ctx(*tile(turn, off + 3))
                if mid:
                    max_out(s + 1)

            slot(0, 0)
            with act.Fori(0, 4) as i:
                for r in range(1, 4):
                    slot(i, r)
            slot(0, 13, load=False)
            slot(0, 14, load=False, front=False)
            slot(0, 15, load=False, front=False, mid=False)
            for g in range(4):
                act.wait_ge(sem["ohT_psum"], g + 1)
                nc.scalar.copy(ohT[:, 4 * g:4 * g + 4, :].rearrange("p n t -> p (n t)"),
                               (bankA if g % 2 == 0 else bankB)[0:NTILE, :]).then_inc(sem["ohT_ready"], 1)
            for g in range(6):
                w = min(3, NT - 3 * g)
                act.wait_ge(sem["look_psum"], g + 1)
                nc.scalar.copy(look[:, 3 * g:3 * g + w, :].rearrange("p n c -> p (n c)"),
                               big[:, g % 4, 0:w * 131]).then_inc(sem["look_ready"], 1)

        @block.tensor
        def _(pe):
            mm = nc.tensor.matmul

            def a1_s1(t):
                pe.wait_ge(sem["xn_ready"], t + 1)
                pe.wait_ge(sem["oT_ready"], t)
                for c in range(DC):
                    for j in range(2):
                        last = nc.tensor.transpose(bankA[:, c * 256 + j * P:c * 256 + (j + 1) * P],
                                                   xn[:, j, c * P:(c + 1) * P], ident[:, :])
                last.then_inc(sem["xT_psum"], 1)

            def a1_s2(t):
                pe.wait_ge(sem["xT_ready"], t + 1)
                pe.wait_ge(sem["attn_w_loaded"], 48)
                for e in range(DC):
                    for c in range(DC):
                        last = mm(bankA[:, e * 256:(e + 1) * 256], wqT[:, c, e * P:(e + 1) * P], xnT[:, c, :],
                                  start=c == 0, stop=c == DC - 1)
                last.then_inc(sem["q_psum"], 1)
                pe.wait_ge(sem["x1_ready"], t)
                for e in range(DC):
                    for c in range(DC):
                        last = mm(bankB[:, e * 256:(e + 1) * 256], wkT[:, c, e * P:(e + 1) * P], xnT[:, c, :],
                                  start=c == 0, stop=c == DC - 1)
                last.then_inc(sem["k_psum"], 1)
                pe.wait_ge(sem["pT_ready"], t)
                for j in range(2):
                    for c in range(DC):
                        last = mm(bankC[:, j * 256:(j + 1) * 256], xnT[:, c, j * P:(j + 1) * P], wvT[:, c, :],
                                  start=c == 0, stop=c == DC - 1)
                last.then_inc(sem["v_psum"], 1)

            def a1_s3(t):
                pe.wait_ge(sem["k_ready"], t + 1)
                pe.wait_ge(sem["v_ready"], t + 1)
                pe.wait_ge(sem["ctxT_loaded"], (t + 1) * 32)
                for j in range(2):
                    for b in range(2):
                        for c in range(DC):
                            last = mm(bankC[b * S:(b + 1) * S, j * P:(j + 1) * P],
                                      qT[:, c, j * P + b * S:j * P + (b + 1) * S], kT[:, c, j, b * P:(b + 1) * P],
                                      start=c == 0, stop=c == DC - 1)
                last.then_inc(sem["s_psum"], 1)

            def a1_s4(t):
                pe.wait_ge(sem["probs_ready"], t + 1)
                for j in range(2):
                    last = nc.tensor.transpose(bankC[:, j * P:(j + 1) * P], probs[:, j, :], ident[:, :])
                last.then_inc(sem["pT_psum"], 1)

            def a1_s5(t):
                pe.wait_ge(sem["pT_ready"], t + 1)
                pe.wait_ge(sem["ctxV_loaded"], (t + 1) * 32)
                for c in range(DC):
                    for j in range(2):
                        for b in range(2):
                            at = c * 256 + j * P + b * S
                            last = mm(bankA[:, at:at + S], vb[:, j, b, c * P:(c + 1) * P], pT[:, j, b * S:(b + 1) * S],
                                      start=True, stop=True)
                last.then_inc(sem["oT_psum"], 1)

            def a1_s6(t):
                pe.wait_ge(sem["oT_ready"], t + 1)
                pe.wait_ge(sem["wo_loaded"], 16)
                for j in range(2):
                    for c in range(DC):
                        last = mm(bankB[:, j * 256:(j + 1) * 256], oT[:, c, j * P:(j + 1) * P], woT[:, c, :],
                                  start=c == 0, stop=c == DC - 1)
                last.then_inc(sem["y_psum"], 1)

            def a2_r1(t):
                pe.wait_ge(sem["xq_ready"], t + 1)
                pe.wait_ge(sem["hT_ready"], t * 2)
                for c in range(DC):
                    for j in range(2):
                        last = nc.tensor.transpose(bankDb[:, c * 256 + j * P:c * 256 + (j + 1) * P],
                                                   xq[:, j, c * P:(c + 1) * P], identb[:, :])
                last.then_inc(sem["xqT_psum"], 1)

            def a2_r1h(t):
                pe.wait_ge(sem["xh_ready"], t + 1)
                pe.wait_ge(sem["x2_ready"], t * 2)
                for c in range(DC):
                    for j in range(2):
                        last = nc.tensor.transpose(big[:, 3, c * 256 + j * P:c * 256 + (j + 1) * P],
                                                   xh[:, j, c * P:(c + 1) * P], ident[:, :])
                last.then_inc(sem["xhT_psum"], 1)

            def a2_r2(t, j):
                pe.wait_ge(sem["xqT_ready"], t + 1)
                pe.wait_ge(sem["w_ready"], 3)
                pe.wait_ge(sem["x2_ready"], t * 2 + j)
                pe.wait_ge(sem["xhT_ready"], t + 1)
                for w, src, dst in ((wgT, xqT, G), (wuT, xhT, U)):
                    for f in range(2):
                        for c in range(DC):
                            last = mm(dst[:, f, :], src[:, c, j * P:(j + 1) * P], w[:, c, f * FH:(f + 1) * FH],
                                      start=c == 0, stop=c == DC - 1)
                last.then_inc(sem["gateup_psum"], 1)

            def a2_r4(t, j):
                pe.wait_ge(sem["hq_ready"], t * 2 + (j + 1))
                for k in range(FK):
                    last = nc.tensor.transpose(bankDb[0:FP, k * P:(k + 1) * P], hq[:, k * FP:(k + 1) * FP], identb[:, :])
                last.then_inc(sem["hT_psum"], 1)
                pe.wait_ge(sem["hT_ready"], t * 2 + (j + 1))
                for k in range(FK):
                    last = mm(big[:, 0, 0:D], hqT[:, k, :], wdT[:, k, :], start=k == 0, stop=k == FK - 1)
                last.then_inc(sem["down_psum"], 1)

            pe.wait_ge(sem["ident_ready"], 1)
            a1_s1(0)
            a1_s2(0)
            a1_s3(0)
            pe.wait_ge(sem["wsum_ready"], 3)
            for i in range(3):
                n = P if i < 2 else FP
                last = mm(bankD[:, i:i + 1], ones[0:n, :], wsum[0:n, i:i + 1], start=True, stop=True)
            last.then_inc(sem["wtot_ready"], 1)
            pe.wait_ge(sem["wmean_ready"], 1)
            pe.wait_ge(sem["chan_w_loaded"], 7 * 16)
            mm(bankD[:, 8:9], wob[:, :], bias[:, 4:5], start=True, stop=True).then_inc(sem["bo_sum_ready"], 1)
            a1_s4(0)
            a1_s5(0)
            a1_s6(0)
            pe.wait_ge(sem["bo_ready"], 1)
            with pe.Fori(1, UNITS) as t:
                a1_s1(t)
                a2_r1(t - 1)
                a1_s2(t)
                a2_r1h(t - 1)
                a1_s3(t)
                a2_r2(t - 1, 0)
                a1_s4(t)
                a1_s5(t)
                a2_r4(t - 1, 0)
                a2_r2(t - 1, 1)
                a1_s6(t)
                a2_r4(t - 1, 1)
            a2_r1(UNITS - 1)
            a2_r1h(UNITS - 1)
            for j in range(2):
                a2_r2(UNITS - 1, j)
                a2_r4(UNITS - 1, j)

            pe.wait_ge(sem["x2_ready"], NT)
            pe.wait_ge(sem["ones_row_placed"], 2 * NBUF * 16)

            def proj_q(t):
                pe.wait_ge(sem["xn3_ready"], t + 1)
                for i in range(2):
                    last = mm(MISC[:, i * D:(i + 1) * D], wqb[:, i, :], xn3[:, :], start=True, stop=True)
                last.then_inc(sem["qproj_psum"], 1)

            def proj_k(t, u, w):
                pe.wait_ge(sem["rope_q"], t + 1)
                pe.wait_ge(ctx_loaded[u], (w + 1) * 16)
                for i in range(2):
                    last = mm(MISC[:, i * D:(i + 1) * D], wkb[:, i, :], cst[u][:, :], start=True, stop=True)
                last.then_inc(sem["kproj_psum"], 1)

            def proj_v(t, u, w):
                pe.wait_ge(sem["rope_k"], t + 1)
                for st in range(2):
                    last = mm(MISC[:, st * P:(st + 1) * P], cst[u][:, st * P:(st + 1) * P], wvb[:, :],
                              start=True, stop=True)
                last.then_inc(sem["vproj_psum"], 1)

            def score_max(t, u, w, m, first=False):
                if m == 0:
                    pe.wait_ge(spread_done[u], (w + 1) * (16 * SPREADS))
                if not (first and m < 2):
                    pe.wait_ge(sem["max_ready"], t * MAXG + (m - 1))
                b, tt, pair = m // 8, m // 4 % 2, m % 4
                for par in range(2):
                    last = mm(MXB[m % 2][:, par * D:(par + 1) * D], QS[u][:, par, b, pair, tt * P:(tt + 1) * P],
                              KS[u][:, b, pair, :], start=True, stop=True)
                last.then_inc(sem["max_psum"], 1)

            def max_turn(t):
                pe.wait_ge(sem["max_ready"], (t + 1) * MAXG)
                for tt in range(2):
                    last = nc.tensor.transpose(MISC[0:16, tt * P:(tt + 1) * P], mx[:, tt, :], ident[:, :])
                last.then_inc(sem["maxT_psum"], 1)

            def score(t, u, w, k, first=False):
                if k == 0:
                    pe.wait_ge(sem["maxrow_done"], (t + 1) * 32)
                if not (first and k < 2):
                    pe.wait_ge(sem["exp_ready"], t * GRANULES + (k - 1))
                b, pair = k % 4 // 2, 2 * (k % 2) + k // 4
                for st in range(2):
                    last = mm(EX[k % 2][:, st * 512:(st + 1) * 512], KS[u][:, b, pair, st * P:(st + 1) * P],
                              QS[u][:, :, b, pair, :], start=True, stop=True)
                last.then_inc(sem["sT_psum"], 1)

            def values(t, u, w, half):
                pe.wait_ge(sem["exp_ready"], t * GRANULES + (4 * half + 4))
                if half == 0:
                    pe.wait_ge(sem["vz_ready"], t + 1)
                    pe.wait_ge(sem["o_ready"], t)
                for par in range(2):
                    for st in range(2):
                        for den in range(2):
                            for g in range(4):
                                slot = 2 * half + par
                                w = OZ[:, 32 * slot:32 * slot + 32] if den else \
                                    VZ[u][:, st * 4 + g, 32 * slot:32 * slot + 32]
                                last = mm(AV[32 * g:32 * g + 32, den * D:(den + 1) * D], w,
                                          PB[:, 4 * half + g, st * 512 + par * D:st * 512 + (par + 1) * D],
                                          start=(half == 0 and par == 0 and st == 0 and den == 0),
                                          stop=(half == 1 and par == 1 and st == 1), skip_group_check=True)
                last.then_inc(sem["av_psum"], 1)

            def out_proj(t):
                if not (isinstance(t, int) and t >= NT - 1):
                    pe.wait_ge(sem["maxT_ready"], t + 2)
                pe.wait_ge(sem["o_ready"], t + 1)
                mm(MISC[:, 0:D], wob[:, :], ob[:, :], start=True, stop=True).then_inc(sem["yc_psum"], 1)

            proj_q(0)
            proj_k(*tile(0, 0))
            proj_v(*tile(0, 0))
            pe.wait_ge(sem["vz_ready"], 1)
            proj_q(1)
            proj_k(*tile(0, 1))
            proj_v(*tile(0, 1))
            for m in range(MAXG):
                score_max(*tile(0, 0), m, first=True)
            pe.wait_ge(sem["vz_ready"], 2)
            max_turn(0)

            def slot(turn, off, front=True, mid=True):
                s, first = tile(turn, off)[0], off == 0
                for k in range(GRANULES):
                    if k == 1 and not first:
                        out_proj(s - 1)
                    if k == 2 and front:
                        pe.wait_ge(sem["maxT_ready" if first else "x3_ready"], 1 if first else s)
                        proj_q(s + 2)
                    if k == 3 and front:
                        proj_k(*tile(turn, off + 2))
                    if k == 4 and front:
                        proj_v(*tile(turn, off + 2))
                    score(*tile(turn, off), k, first)
                    if mid:
                        score_max(*tile(turn, off + 1), 2 * k)
                        score_max(*tile(turn, off + 1), 2 * k + 1)
                    if k == 5:
                        values(*tile(turn, off), 0)
                values(*tile(turn, off), 1)
                if mid:
                    pe.wait_ge(sem["vz_ready" if front else "x3_ready"], s + 3 if front else s)
                    max_turn(s + 1)

            slot(0, 0)
            with pe.Fori(0, 4) as i:
                for r in range(1, 4):
                    slot(i, r)
            slot(0, 13)
            slot(0, 14, front=False)
            slot(0, 15, front=False, mid=False)
            pe.wait_ge(sem["x3_ready"], 15)
            out_proj(15)
            pe.wait_ge(sem["onehot_ready"], NT)
            for g in range(4):
                if g >= 2:
                    pe.wait_ge(sem["ohT_ready"], g - 1)
                for i in range(4):
                    last = nc.tensor.transpose((bankA if g % 2 == 0 else bankB)[0:NTILE, i * P:(i + 1) * P],
                                               oh[:, 4 * g + i, :], ident[:, :])
                last.then_inc(sem["ohT_psum"], 1)
            pe.wait_ge(sem["max_part"], 1)
            for i in range(2):
                last = nc.tensor.transpose(bankC[0:NTILE, i * P:(i + 1) * P], mpart[:, i, :], ident[:, :])
            last.then_inc(sem["mm_psum"], 1)
            pe.wait_ge(sem["mm_ready"], 1)
            pe.wait_ge(sem["ohT_ready"], 4)
            for g in range(6):
                if g >= 4:
                    pe.wait_ge(sem["look_ready"], g - 3)
                for i in range(min(3, NT - 3 * g)):
                    last = mm(big[:, g % 4, i * 131:(i + 1) * 131], ohT[:, 3 * g + i, :], table[:, :],
                              start=True, stop=True)
                last.then_inc(sem["look_psum"], 1)

        @block.vector
        def _(v):
            V = nc.vector

            def stats(name, srcs, stt, mv, ve, t):
                for j, src in enumerate(srcs):
                    last = V.bn_stats(stt[j], src)
                last.then_inc(sem[name + "_steps"], 1)
                v.wait_ge(sem[name + "_steps"], t * 2 + 1)
                V.memset(hold[:, 0:1], 0.0)
                for j in range(len(srcs)):
                    last = V.bn_aggr(mv[j], stt[j])
                last.then_inc(sem[name + "_steps"], 1)
                v.wait_ge(sem[name + "_steps"], t * 2 + 2)
                for j in range(len(srcs)):
                    last = V.tensor_scalar(ve[j], mv[j][:, 1:2], LN_EPS, None, ALU.add)
                last.then_inc(sem[name + "_var"], 1)

            def ln1_stats(t):
                stats("ln1", [xall[:, t * 2 + j, :] for j in range(2)], [st1[:, j, :] for j in range(2)],
                      [mv1[:, j, :] for j in range(2)], [ve1[:, j:j + 1] for j in range(2)], t)

            def ln1_apply(t):
                v.wait_ge(sem["ln1_rstd"], t + 1)
                v.wait_ge(sem["xT_psum"], t)
                for j in range(2):
                    last = V.tensor_scalar(xn[:, j, :], xall[:, t * 2 + j, :], mv1[:, j, 0:1], rs1[:, j:j + 1],
                                           ALU.subtract, ALU.mult)
                last.then_inc(sem["xn_ready"], 1)

            def a1_max(t):
                v.wait_ge(sem["s_psum"], t + 1)
                V.tensor_reduce(nmax[:, :], bankC[:, 0:2 * P].rearrange("p (j n) -> p j n", j=2), AX,
                                ALU.max).then_inc(sem["s_max"], 1)
                v.wait_ge(sem["s_max"], t + 1)
                V.tensor_scalar(nmaxs[:, :], nmax[:, :], -1.0 / 16.0, None, ALU.mult).then_inc(sem["nmax_ready"], 1)

            def a1_out(t):
                v.wait_ge(sem["probs_ready"], t + 1)
                V.reciprocal(pinv[:, :], psums[:, :]).then_inc(sem["rsum_ready"], 1)
                v.wait_ge(sem["rsum_ready"], t + 1)
                v.wait_ge(sem["y_psum"], t + 1)
                for j in range(2):
                    last = V.scalar_tensor_tensor(out=xall[:, t * 2 + j, :], in0=bankB[:, j * D:(j + 1) * D],
                                                  scalar=pinv[:, j:j + 1], in1=xall[:, t * 2 + j, :],
                                                  op0=ALU.mult, op1=ALU.add)
                last.then_inc(sem["x1_ready"], 1)

            def ln2_stats(t):
                stats("ln2", [xall[:, t * 2 + j, :] for j in range(2)], [st2[:, j, :] for j in range(2)],
                      [mv2[:, j, :] for j in range(2)], [ve2[:, j:j + 1] for j in range(2)], t)

            def a2_quant(t):
                v.wait_ge(sem["ln2_rstd"], t + 1)
                for j in range(2):
                    last = V.tensor_scalar(xn2[:, j, :], xall[:, t * 2 + j, :], mv2[:, j, 0:1], rs2[:, j:j + 1],
                                           ALU.subtract, ALU.mult)
                last.then_inc(sem["xn2_ready"], 1)
                v.wait_ge(sem["xn2_ready"], t + 1)
                V.tensor_reduce(amax[:, :], xn2[:, :, :], AX, ALU.max,
                                apply_absolute_value=True).then_inc(sem["amax_ready"], 1)
                v.wait_ge(sem["amax_ready"], t + 1)
                V.tensor_scalar(amaxc[:, :], amax[:, :], Q_EPS, None, ALU.max).then_inc(sem["amaxc_ready"], 1)
                v.wait_ge(sem["amaxc_ready"], t + 1)
                V.reciprocal(arec[:, :], amaxc[:, :]).then_inc(sem["arec_ready"], 1)
                v.wait_ge(sem["gate_ready"], t * 2)
                v.wait_ge(sem["up_ready"], t * 2)
                V.tensor_scalar(aG[:, :], amaxc[:, :], wm127[:, 0:1], None, ALU.mult).then_inc(sem["act_scale1"], 1)
                V.tensor_scalar(ainv[:, :], amaxc[:, :], 1.0 / 127.0, None, ALU.mult).then_inc(sem["act_scale2"], 1)
                v.wait_ge(sem["arec_ready"], t + 1)
                V.tensor_scalar(ascale[:, :], arec[:, :], 127.0, None, ALU.mult).then_inc(sem["ascale_ready"], 1)
                v.wait_ge(sem["act_scale1"], t + 1)
                V.tensor_scalar(aGh[:, :], aG[:, :], 0.5, None, ALU.mult).then_inc(sem["act_scale3"], 1)
                v.wait_ge(sem["ascale_ready"], t + 1)
                for j in range(2):
                    last = V.tensor_scalar(xn2[:, j, :], xn2[:, j, :], ascale[:, j:j + 1], MAGIC, ALU.mult, ALU.add)
                last.then_inc(sem["a_round"], 1)
                v.wait_ge(sem["a_round"], t + 1)
                v.wait_ge(sem["xqT_psum"], t)
                V.tensor_scalar(xq[:, :, :].rearrange("p j d -> p (j d)"), xn2[:, :, :].rearrange("p j d -> p (j d)"),
                                MAGIC, None, ALU.subtract).then_inc(sem["xq_ready"], 1)
                v.wait_ge(sem["act_scale2"], t + 1)
                for j in range(2):
                    last = V.tensor_scalar(xh[:, j, :].rearrange("p (b a) -> p a b", a=16),
                                           xn2[:, j, :].rearrange("p (a b) -> p a b", b=16),
                                           MAGIC, ainv[:, j:j + 1], ALU.subtract, ALU.mult)
                last.then_inc(sem["xh_ready"], 1)

            def a2_h(t, j):
                n = t * 2 + j
                v.wait_ge(sem["up_ready"], n + 1)
                V.scalar_tensor_tensor(out=h1, in0=th, scalar=1.0, in1=us, op0=ALU.add,
                                       op1=ALU.mult).then_inc(sem["h_half"], 1)
                v.wait_ge(sem["h_half"], n + 1)
                V.tensor_tensor(h2.rearrange("p (a n) -> p a n", a=2), G,
                                h1.rearrange("p (a n) -> p a n", a=2), ALU.mult).then_inc(sem["h_ready"], 1)
                v.wait_ge(sem["h_ready"], n + 1)
                V.tensor_reduce(hm[:, 0:1], h2, AX, ALU.max, apply_absolute_value=True).then_inc(sem["hamax_ready"], 1)
                v.wait_ge(sem["hamax_ready"], n + 1)
                V.tensor_scalar(hm[:, 1:2], hm[:, 0:1], Q_EPS, None, ALU.max).then_inc(sem["hamaxc_ready"], 1)
                v.wait_ge(sem["hamaxc_ready"], n + 1)
                V.reciprocal(hm[:, 2:3], hm[:, 1:2]).then_inc(sem["hrec_ready"], 1)
                V.tensor_scalar(bD[:, :], hm[:, 1:2], wm127[:, 2:3], None, ALU.mult).then_inc(sem["dscale_ready"], 1)
                v.wait_ge(sem["hrec_ready"], n + 1)
                V.tensor_scalar(hm[:, 3:4], hm[:, 2:3], 127.0, None, ALU.mult).then_inc(sem["hscale_ready"], 1)
                v.wait_ge(sem["hscale_ready"], n + 1)
                V.tensor_scalar(h1, h2, hm[:, 3:4], MAGIC, ALU.mult, ALU.add).then_inc(sem["h_round"], 1)
                v.wait_ge(sem["h_round"], n + 1)
                v.wait_ge(sem["hT_psum"], n)
                V.tensor_scalar(hq[:, :], h1, MAGIC, None, ALU.subtract).then_inc(sem["hq_ready"], 1)

            def a2_out(t, j):
                n = t * 2 + j
                v.wait_ge(sem["dscale_ready"], n + 1)
                v.wait_ge(sem["down_psum"], n + 1)
                V.scalar_tensor_tensor(out=xall[:, n, :], in0=big[:, 0, 0:D], scalar=bD[:, 0:1],
                                       in1=xall[:, n, :], op0=ALU.mult, op1=ALU.add).then_inc(sem["x2_ready"], 1)

            V.memset(halfneg[:, :], -0.5)
            V.memset(ones[:, :], 1.0)
            V.memset(OZ[:, :], 0.0).then_inc(sem["oz_ready"], 1)
            v.wait_ge(sem["oz_ready"], 1)
            V.memset(OZ[:, :].rearrange("p (a b) -> p a b", b=40)[:, :, 0:HC], 1.0).then_inc(sem["oz_ready"], 1)
            v.wait_ge(sem["ident_loaded"], 16)
            V.tensor_copy(identb[:, :], ident[:, :]).then_inc(sem["ident_ready"], 1)
            v.wait_ge(sem["x_loaded"], 64)
            ln1_stats(0)
            ln1_apply(0)
            v.wait_ge(sem["ffn_w_loaded"], 48)
            V.tensor_reduce(wsum[:, 0:2], wffn, AX, ALU.add, apply_absolute_value=True).then_inc(sem["wsum_ready"], 2)
            V.tensor_reduce(wsum[0:FP, 2:3], wdn, AX, ALU.add, apply_absolute_value=True).then_inc(sem["wsum_ready"], 1)
            a1_max(0)
            v.wait_ge(sem["wtot_ready"], 1)
            V.tensor_scalar(wmean[:, 0:3], bankD[:, 0:3], 1.0 / (FF * D), Q_EPS, ALU.mult, ALU.max).then_inc(sem["wmean_ready"], 1)
            v.wait_ge(sem["wmean_ready"], 1)
            V.reciprocal(winv[:, 0:3], wmean[:, 0:3])
            V.tensor_scalar(wm127[:, 0:3], wmean[:, 0:3], 1.0 / 127.0, None, ALU.mult).then_inc(sem["winv_ready"], 1)
            v.wait_ge(sem["winv_ready"], 1)
            for i, (src, dst, n) in enumerate(((wffn[:, 0, :], wgT[:, :, :], P), (wffn[:, 1, :], wuT, P), (wdn, wdT[:, :, :], FP))):
                V.tensor_scalar(src, src, winv[0:n, i:i + 1], 1.0, ALU.mult, ALU.min).then_inc(sem["w_clip"], 1)
                v.wait_ge(sem["w_clip"], i + 1)
                V.tensor_scalar(src, src, -1.0, MAGIC, ALU.max, ALU.add).then_inc(sem["w_round"], 1)
                v.wait_ge(sem["w_round"], i + 1)
                V.tensor_scalar(dst.rearrange("p a b -> p (a b)"), src, MAGIC, wmean[:, 1:2] if i == 1 else 1.0,
                                ALU.subtract, ALU.mult).then_inc(sem["w_ready"], 1)
            v.wait_ge(sem["bo_sum_ready"], 1)
            V.tensor_tensor(boe[:, :], bankD[:, 8:9], bias[:, 5:6], ALU.add).then_inc(sem["bo_ready"], 1)
            a1_out(0)
            v.wait_ge(sem["ffn2_loaded"], 8 * 16)
            V.tensor_reduce(ssum, slopes, AX, ALU.add).then_inc(sem["slope_sum"], 1)
            v.wait_ge(sem["slope_sum"], 1)
            V.tensor_scalar(sneg, ssum, 0.0, None, ALU.is_lt).then_inc(sem["slope_neg"], 1)
            v.wait_ge(sem["slope_neg"], 1)
            V.scalar_tensor_tensor(out=sig[:, :], in0=ssum, scalar=0.0, in1=sneg, op0=ALU.is_gt,
                                   op1=ALU.subtract).then_inc(sem["sig_ready"], 1)

            with v.Fori(1, UNITS) as t:
                ln1_stats(t)
                v.wait_ge(sem["x1_ready"], t)
                ln1_apply(t)
                ln2_stats(t - 1)
                a2_quant(t - 1)
                a1_max(t)
                a2_h(t - 1, 0)
                a2_out(t - 1, 0)
                a1_out(t)
                a2_h(t - 1, 1)
                a2_out(t - 1, 1)
            v.wait_ge(sem["x1_ready"], UNITS)
            ln2_stats(UNITS - 1)
            a2_quant(UNITS - 1)
            for j in range(2):
                a2_h(UNITS - 1, j)
                a2_out(UNITS - 1, j)

            v.wait_ge(sem["x2_ready"], NT)
            v.wait_ge(sem["chan_w_loaded"], 7 * 16)

            def ln3_stats(t):
                stats("ln3", [xall[:, t, :]], [st3[:, :]], [mv3[:, :]], [ve3[:, :]], t)

            def ln3_apply(t):
                v.wait_ge(sem["ln3_rstd"], t + 1)
                v.wait_ge(sem["qproj_psum"], t)
                V.tensor_scalar(xn3[:, :], xall[:, t, :], mv3[:, 0:1], rs3[:, 0:1],
                                ALU.subtract, ALU.mult).then_inc(sem["xn3_ready"], 1)

            def rope_part(t, a, name, psum):
                v.wait_ge(sem[psum], t + 1)
                v.wait_ge(sem["qk_sum"], t)
                for i, tab in enumerate((cos, sin)):
                    last = V.scalar_tensor_tensor(out=rope[:, a, i, :], in0=MISC[:, i * D:(i + 1) * D],
                                                  scalar=bias[:, 2 * a + i:2 * a + i + 1], in1=tab[:, :],
                                                  op0=ALU.add, op1=ALU.mult)
                last.then_inc(sem[name], 1)

            def reduce_max(t, m):
                b, tt, pair = m // 8, m // 4 % 2, m % 4
                if m == 0:
                    v.wait_ge(sem["maxT_psum"], t)
                v.wait_ge(sem["max_psum"], t * MAXG + (m + 1))
                col = mx[:, tt, :].rearrange("p (a c) -> p a c", a=2)[:, :, b * 4 + pair]
                V.tensor_reduce(col, MXB[m % 2][:, :].rearrange("p (a n) -> p a n", a=2), AX,
                                ALU.max).then_inc(sem["max_ready"], 1)

            def normalize(t):
                v.wait_ge(sem["av_psum"], t * 2 + 2)
                V.reciprocal(dinv[:, :], AV[:, D:2 * D]).then_inc(sem["den_inv"], 1)
                v.wait_ge(sem["den_inv"], t + 1)
                v.wait_ge(sem["yc_psum"], t)
                V.tensor_tensor(ob[:, :], AV[:, 0:D], dinv[:, :], ALU.mult).then_inc(sem["o_ready"], 1)

            def residual(t):
                v.wait_ge(sem["yc_psum"], t + 1)
                V.scalar_tensor_tensor(out=xall[:, t, :], in0=MISC[:, 0:D], scalar=boe[:, 0:1],
                                       in1=xall[:, t, :], op0=ALU.add, op1=ALU.add).then_inc(sem["x3_ready"], 1)

            def ln4_stats(t):
                stats("ln4", [xall[:, t, :]], [st4[:, :]], [mv4[:, :]], [ve4[:, 0:1]], t)

            def ln4_apply(t):
                v.wait_ge(sem["ln4_rstd"], t + 1)
                V.tensor_scalar(xn4, xall[:, t, :], mv4[:, 0:1], rs4[:, 0:1],
                                ALU.subtract, ALU.mult).then_inc(sem["xn4_ready"], 1)
                v.wait_ge(sem["xn4_ready"], t + 1)
                stats("ln5", [xn4], [st5[:, :]], [mv5[:, :]], [ve4[:, 1:2]], t)

            def ln5_apply(t):
                v.wait_ge(sem["ln5_rstd"], t + 1)
                v.wait_ge(sem["gamma_done"], t)
                V.tensor_scalar(xn5, xn4, mv5[:, 0:1], rs4[:, 1:2],
                                ALU.subtract, ALU.mult).then_inc(sem["xn5_ready"], 1)
                V.tensor_tensor(xall[:, t, :], xall[:, t, :], xn4, ALU.add).then_inc(sem["x4_ready"], 1)

            def route_scores(t):
                v.wait_ge(sem["xf_ready"], t + 1)
                V.tensor_tensor(wk1, xf, sig[:, :], ALU.mult).then_inc(sem["sgn_prod"], 1)
                v.wait_ge(sem["sgn_prod"], t + 1)
                V.tensor_scalar(wk2[:, :], wk1, 0.0, None, ALU.is_lt).then_inc(sem["sgn_neg"], 1)
                v.wait_ge(sem["sgn_neg"], t + 1)
                V.scalar_tensor_tensor(out=wk1, in0=wk1, scalar=0.0, in1=wk2[:, :], op0=ALU.is_gt,
                                       op1=ALU.subtract).then_inc(sem["sgn_ready"], 1)
                v.wait_ge(sem["sgn_ready"], t + 1)
                V.tensor_reduce(tsc[:, :], wk1.rearrange("p (n j) -> p n j", j=SLICE), AX,
                                ALU.add).then_inc(sem["tile_score"], 1)
                V.tensor_reduce(csc[:, :], wk1.rearrange("p (c n) -> p c n", c=CLUSTERS), AX,
                                ALU.add).then_inc(sem["clus_score"], 1)

            def route_pick(t):
                v.wait_ge(sem["clus_score"], t + 1)
                V.scalar_tensor_tensor(out=key1[:, :].rearrange("p (c n) -> p c n", c=CLUSTERS),
                                       in0=csc[:, :].unsqueeze(2).to_broadcast([P, CLUSTERS, CLUSTERS]),
                                       scalar=1024.0, in1=ckey[:, :].rearrange("p (c n) -> p c n", c=CLUSTERS),
                                       op0=ALU.mult, op1=ALU.add).then_inc(sem["key_c"], 1)
                v.wait_ge(sem["key_c"], t + 1)
                V.scalar_tensor_tensor(out=key2[:, :], in0=tsc[:, :], scalar=8.0, in1=key1[:, :], op0=ALU.mult,
                                       op1=ALU.add).then_inc(sem["key_ready"], 1)
                v.wait_ge(sem["key_ready"], t + 1)
                V.tensor_reduce(kmax[:, :], key2[:, :], AX, ALU.max).then_inc(sem["key_max"], 1)
                v.wait_ge(sem["key_max"], t + 1)
                V.tensor_scalar(oh[:, t, :], key2[:, :], kmax[:, 0:1], None, ALU.is_equal).then_inc(sem["onehot_ready"], 1)

            def route_slice(t):
                v.wait_ge(sem["onehot_ready"], t + 1)
                V.tensor_tensor(wk2[:, :].rearrange("p (n j) -> p n j", j=SLICE),
                                xf.rearrange("p (n j) -> p n j", j=SLICE),
                                oh[:, t, :].unsqueeze(2).to_broadcast([P, NTILE, SLICE]),
                                ALU.mult).then_inc(sem["xf_masked"], 1)
                v.wait_ge(sem["xf_masked"], t + 1)
                V.tensor_reduce(xs[:, t, :], wk2[:, :].rearrange("p (n j) -> p j n", j=SLICE), AX,
                                ALU.add).then_inc(sem["slice_ready"], 1)

            ln3_stats(0)
            ln3_apply(0)
            rope_part(0, 0, "rope_q", "qproj_psum")
            rope_part(0, 1, "rope_k", "kproj_psum")
            ln3_stats(1)
            ln3_apply(1)
            rope_part(1, 0, "rope_q", "qproj_psum")
            rope_part(1, 1, "rope_k", "kproj_psum")
            for m in range(MAXG):
                reduce_max(0, m)

            def slot(s, front=True, mid=True, back=True, route=True):
                for k in range(GRANULES):
                    if mid:
                        reduce_max(s + 1, 2 * k)
                        reduce_max(s + 1, 2 * k + 1)
                    if k == 0:
                        if back:
                            normalize(s - 1)
                        if front:
                            ln3_stats(s + 2)
                    if k == 1:
                        if back:
                            residual(s - 1)
                            v.wait_ge(sem["x3_ready"], s)
                        if front:
                            ln3_apply(s + 2)
                        if back:
                            ln4_stats(s - 1)
                    if k == 2:
                        if front:
                            rope_part(s + 2, 0, "rope_q", "qproj_psum")
                        if back:
                            ln4_apply(s - 1)
                    if k == 3:
                        if front:
                            rope_part(s + 2, 1, "rope_k", "kproj_psum")
                        if back:
                            ln5_apply(s - 1)
                    if k == 4 and route:
                        route_scores(s - 2)
                    if k == 5 and route:
                        route_pick(s - 2)
                    if k == 6 and route:
                        route_slice(s - 2)

            slot(0, back=False, route=False)
            slot(1, route=False)
            with v.Fori(2, 14) as s:
                slot(s)
            slot(14, front=False)
            slot(15, front=False, mid=False)
            slot(16, front=False, mid=False)
            route_scores(15)
            route_pick(15)
            route_slice(15)

            links = [0]

            def link(ins):
                links[0] += 1
                ins.then_inc(sem["spline_step"], 1)
                v.wait_ge(sem["spline_step"], links[0])

            v.wait_ge(sem["slice_ready"], NT)
            v.wait_ge(sem["x4_ready"], NT)
            link(V.tensor_reduce(tmm[:, :, 0], xs[:, :, :], AX, ALU.min))
            link(V.tensor_reduce(tmm[:, :, 1], xs[:, :, :], AX, ALU.max))
            link(V.tensor_scalar(bigm, oh[:, :, :], -BIG, BIG, ALU.mult, ALU.add))
            for i, (name, op, edge) in enumerate((("min", ALU.min, ALU.add), ("max", ALU.max, ALU.subtract))):
                link(V.tensor_tensor(cand, oh[:, :, :], tmm[:, :, i:i + 1].to_broadcast([P, NT, NTILE]),
                                ALU.mult))
                link(V.tensor_tensor(cand, cand, bigm, edge))
                V.tensor_reduce(mpart[:, i, :], cand.rearrange("p n t -> p t n"), AX, op).then_inc(sem[name + "_part"], 1)
                v.wait_ge(sem[name + "_part"], 1)
            v.wait_ge(sem["mm_psum"], 1)
            V.tensor_reduce(table[:, 128:129], bankC[0:NTILE, 0:P], AX, ALU.min)
            V.tensor_reduce(table[:, 129:130], bankC[0:NTILE, P:2 * P], AX, ALU.max).then_inc(sem["mm_ready"], 1)
            v.wait_ge(sem["look_ready"], 6)
            mnb = look[:, :, 128:129].to_broadcast([P, NT, SLICE])
            link(V.tensor_tensor(u0[:, :, :], xs[:, :, :], mnb, ALU.subtract))
            link(V.tensor_tensor(span[:, 0, :], look[:, :, 129], look[:, :, 128], ALU.subtract))
            link(V.tensor_scalar(span[:, 1, :], span[:, 0, :], 1e-8, None, ALU.add))
            link(V.reciprocal(span[:, 2, :], span[:, 1, :]))
            link(V.tensor_tensor(u1[:, :, :], u0[:, :, :], span[:, 2, :].unsqueeze(2).to_broadcast([P, NT, SLICE]),
                            ALU.mult))
            link(V.tensor_scalar(u2[:, :, :], u1[:, :, :], 0.0, 1.0 - 1e-6, ALU.max, ALU.min))
            link(V.tensor_scalar(u3[:, :, :], u2[:, :, :], float(GRID), None, ALU.mult))
            link(V.tensor_scalar(u4[:, :, :], u3[:, :, :], MAGIC, None, ALU.add))
            link(V.tensor_scalar(u5[:, :, :], u4[:, :, :], MAGIC, None, ALU.subtract))
            link(V.tensor_tensor(u0[:, :, :], u5[:, :, :], u3[:, :, :], ALU.is_gt))
            link(V.tensor_tensor(u1[:, :, :], u5[:, :, :], u0[:, :, :], ALU.subtract))
            link(V.tensor_scalar(u2[:, :, :], u1[:, :, :], 0.0, float(GRID - 1), ALU.max, ALU.min))
            link(V.tensor_tensor(u4[:, :, :], u3[:, :, :], u2[:, :, :], ALU.subtract))
            u2m = u2[:, :, :].rearrange("p n j -> p (n j)")
            link(V.tensor_tensor(gmask.rearrange("p (m g) -> p m g", g=GRID),
                            giota[:, :].unsqueeze(1).to_broadcast([P, NT * SLICE, GRID]),
                            u2m.unsqueeze(2).to_broadcast([P, NT * SLICE, GRID]),
                            ALU.is_equal))
            for i, (name, dst) in enumerate((("base", bsel), ("slope", ssel))):
                link(V.tensor_tensor(gprod.rearrange("p (n c) -> p n c", n=NT), gmask.rearrange("p (n c) -> p n c", n=NT),
                                look[:, :, 64 * i:64 * i + 64], ALU.mult))
                link(V.tensor_reduce(dst[:, :, :].rearrange("p n j -> p (n j)"), gprod.rearrange("p (m g) -> p m g", g=GRID),
                                AX, ALU.add))
            link(V.tensor_tensor(u5[:, :, :], ssel[:, :, :], u4[:, :, :], ALU.mult))
            link(V.tensor_tensor(u3[:, :, :], u5[:, :, :], bsel[:, :, :], ALU.add))
            V.tensor_tensor(delta[:, :, :], u3[:, :, :], look[:, :, 130:131].to_broadcast([P, NT, SLICE]),
                            ALU.mult).then_inc(sem["delta_ready"], 1)
            v.wait_ge(sem["delta_ready"], 1)
            for i, q in enumerate((0, 2)):
                for n in range(4 * q, 4 * q + 4):
                    last = V.tensor_tensor(outb[:, n, :].rearrange("p (t j) -> p t j", j=SLICE),
                                           oh[:, n, :].unsqueeze(2).to_broadcast([P, NTILE, SLICE]),
                                           delta[:, n, :].unsqueeze(1).to_broadcast([P, NTILE, SLICE]), ALU.mult)
                last.then_inc(sem["place_dve"], 1)
                v.wait_ge(sem["place_dve"], i + 1)
                V.tensor_tensor(outb[:, 4 * q:4 * q + 4, :], outb[:, 4 * q:4 * q + 4, :], xall[:, 4 * q:4 * q + 4, :],
                                ALU.add).then_inc(sem["out_dve"], 1)


def kernel(**inputs):
    import numpy as np
    import concourse.bacc as bacc
    from concourse.bass_utils import run_bass_kernel_spmd

    a = {k: np.asarray(v) for k, v in inputs.items()}
    f = np.float32

    def turned(w):
        return np.ascontiguousarray(w.T)

    def twice(w):
        z = np.zeros((2 * w.shape[0], 2 * w.shape[1]), f)
        z[:w.shape[0], :w.shape[1]] = w
        z[w.shape[0]:, w.shape[1]:] = w
        return z

    order = [(b, (2 * g + par) * HC + c) for par in range(2) for c in range(HC) for b in range(2) for g in range(PAIRS)]
    rolled = [(b, o // HC * HC + (o % HC + HC // 2) % HC) for b, o in order]
    cols = np.array([b * 64 + o for b, o in order])
    colr = np.array([b * 64 + o for b, o in rolled])

    def stacked(w):
        z = twice(turned(w))
        return np.ascontiguousarray(np.stack([z[:, cols], z[:, colr]], 1))

    def both(v):
        return np.concatenate([v, v])

    bq, bk = both(a["L1_xattn_bq"]), both(a["L1_xattn_bk"])
    bias = np.stack([bq[cols], bq[colr], bk[cols], bk[colr], both(a["L1_xattn_bv"]), both(a["L1_xattn_bo"])], 1)
    inv_freq = f(1.0) / f(10000.0) ** (np.arange(0, HC, 2, dtype=f) / f(HC))
    angle = np.arange(D, dtype=f)[:, None] * inv_freq[None, :]
    ch = np.array([o % HC for _, o in order])
    cos = np.cos(angle)[:, ch % 4].T
    sin = np.sin(angle)[:, ch % 4].T * np.where(ch < HC // 2, f(-1), f(1))[:, None]
    n = np.arange(NTILE)
    ctx = a["ctx_2048"]
    arrays = {
        "x": a["x"], "ctx": ctx,
        "ctxT": np.ascontiguousarray(ctx.reshape(UNITS, 2, 2 * S, D).transpose(3, 0, 1, 2)),
        "wq": turned(a["L0_xattn_wq"]), "wk": turned(a["L0_xattn_wk"]),
        "wv": turned(a["L0_xattn_wv"]), "wo": turned(a["L0_xattn_wo"]),
        "wg": turned(a["L0_ffn_w_gate"]), "wu": np.ascontiguousarray(turned(a["L0_ffn_w_up"]).reshape(16, 16, FF).swapaxes(0, 1)).reshape(D, FF), "wd": turned(a["L0_ffn_w_down"]),
        "wqb": stacked(a["L1_xattn_Wq"]), "wkb": stacked(a["L1_xattn_Wk"]),
        "wvb": twice(turned(a["L1_xattn_Wv"])), "wob": twice(turned(a["L1_xattn_Wo"])),
        "bias": bias, "cos": np.ascontiguousarray(cos, f), "sin": np.ascontiguousarray(sin, f),
        "gamma": a["L1_ffn_ln_gamma"][None, :], "beta": a["L1_ffn_ln_beta"][None, :],
        "bases": a["L1_ffn_spline_bases"].reshape(NTILE, 64), "slopes": a["L1_ffn_spline_slopes"].reshape(NTILE, 64),
        "slopes_row": a["L1_ffn_spline_slopes"].reshape(1, NTILE * 64),
        "oscale": a["L1_ffn_output_scale"][:, None],
        "ident": np.eye(P, dtype=f),
        "ckey": (-(n // 8) * 128 - n % 8).astype(f)[None, :], "giota": np.arange(GRID, dtype=f)[None, :],
    }
    nc = bacc.Bacc("TRN2", target_bir_lowering=False, num_devices=1)
    feed, A = {}, {}
    for name, v in arrays.items():
        v = np.ascontiguousarray(v)
        feed["in_" + name] = v
        A[name] = nc.dram_tensor("in_" + name, v.shape, mybir.dt.from_np(v.dtype), kind="ExternalInput").ap()
    out = nc.dram_tensor("out_x", (B, S, D), F32, kind="ExternalOutput").ap()
    decoder_kernel(nc, A, out)
    r = run_bass_kernel_spmd(nc, [feed], core_ids=[0])
    return r.results[0]["out_x"]
```

```python
from contextlib import ExitStack

import concourse.bass as bass
from concourse import mybir

F32 = mybir.dt.float32
BF16 = mybir.dt.bfloat16
ALU = mybir.AluOpType
ACT = mybir.ActivationFunctionType
AX = mybir.AxisListType.X

P = 128
B, S, D = 32, 64, 256
NT = B * S // P
DC = D // P
UNITS = NT // 2
FF = 832
FH = FF // 2
FK, FP = 8, FF // 8
HEADS, HC = 8, 8
PAIRS = HEADS // 2
NTILE, SLICE, GRID, CLUSTERS = 64, 4, 16, 8
LN_EPS = 1e-5
Q_EPS = 1e-5
MAGIC = 12582912.0
BIG = 3.0e38
NBUF = 3
GRANULES = 8
MAXG = 16
SPREADS = 14
LAG = 3

SEMS = """
x0_loaded x_loaded attn_w_loaded wo_loaded chan_w_loaded ffn_w_loaded ident_loaded ctxT_loaded ctxV_loaded ffn2_loaded
const_ready ident_ready ones_row_placed oz_ready
wsum_ready wtot_ready wmean_ready winv_ready w_clip w_round w_ready
bo_sum_ready bo_ready
ln1_steps ln1_var ln1_rstd xn_ready
xT_psum xT_ready q_psum q_ready k_psum k_ready v_psum v_ready
s_psum s_max nmax_ready probs_ready pT_psum pT_ready rsum_ready oT_psum oT_ready y_psum x1_ready
ln2_steps ln2_var ln2_rstd xn2_ready amax_ready amaxc_ready arec_ready ascale_ready
a_round xq_ready act_scale1 act_scale2 act_scale3
xqT_psum xqT_ready xh_ready xhT_psum xhT_ready gateup_psum gate_ready up_ready
h_half h_ready hamax_ready hamaxc_ready hrec_ready hscale_ready h_round hq_ready dscale_ready
hT_psum hT_ready down_psum x2_ready
ln3_steps ln3_var ln3_rstd xn3_ready
qproj_psum kproj_psum vproj_psum rope_q rope_k qk_sum part1 rest1 part2 parts_ready
parts_stored vz_ready
max_psum max_ready maxT_psum maxT_ready maxrow_done
sT_psum exp_ready av_psum den_inv o_ready yc_psum x3_ready
ln4_steps ln4_var ln4_rstd xn4_ready
ln5_steps ln5_var ln5_rstd xn5_ready gamma_done xf_ready
sgn_prod sgn_neg sgn_ready tile_score clus_score key_c key_ready key_max onehot_ready
xf_masked x4_ready slice_ready
slope_sum slope_neg sig_ready
min_part max_part
spline_step mm_psum mm_ready ohT_psum ohT_ready look_psum look_ready

delta_ready place_dve place_pool out_pool out_dve out_stored
""".split()


def decoder_kernel(nc, A, out):
    with ExitStack() as ctx:
        def sb(name, shape, dt=F32):
            return ctx.enter_context(nc.sbuf_tensor(name, shape, dt))

        sem = {name: ctx.enter_context(nc.semaphore(name)) for name in SEMS}
        ctx_loaded = [ctx.enter_context(nc.semaphore(f"ctx_loaded{i}")) for i in range(NBUF)]
        spread_done = [ctx.enter_context(nc.semaphore(f"spread_done{i}")) for i in range(NBUF)]

        def tile(turn, off):
            return turn * NBUF + off, off % NBUF, turn + off // NBUF

        def live(t):
            return not isinstance(t, int) or 0 <= t < NT

        def proj_bank(t):
            return (bankA, bankC)[t] if isinstance(t, int) and t < 2 else MISC

        def on(t):
            return not isinstance(t, int) or 0 <= t < UNITS

        xall = sb("xall", [P, NT, D])
        ident = sb("ident", [P, P])
        identb = sb("identb", [P, P], BF16)
        ones = sb("ones", [P, P])
        halfneg = sb("halfneg", [P, 2])
        wattn = sb("wattn", [P, 4 * DC * D])
        wqT, wkT, wvT, woT = (wattn[:, i * DC * D:(i + 1) * DC * D].rearrange("p (c d) -> p c d", c=DC) for i in range(4))
        PB = sb("PB", [P, GRANULES, 4 * D])
        pbf = PB[:, :, :].rearrange("p g n -> p (g n)")
        slopes = pbf[:, 0:D * GRID].rearrange("p (d g) -> p d g", g=GRID)
        wffn = pbf[:, 4096:4096 + 2 * DC * FF].rearrange("p (a n) -> p a n", a=2)
        lookf = sb("lookf", [P, NT * 131])
        look = lookf[:, :].rearrange("p (n c) -> p n c", n=NT)
        wdn = lookf[0:FP, 0:FK * D]
        outf = sb("outf", [P, NT * D])
        outb = outf[:, :].rearrange("p (n d) -> p n d", n=NT)
        wgT = sb("wgT", [P, DC, FF], BF16)
        wuT = wffn[:, 1, :].rearrange("p (c f) -> p c f", c=DC)
        wdT = sb("wdT", [FP, FK, D], BF16)
        wsum = sb("wsum", [P, 4])
        wmean = sb("wmean", [P, 4])
        winv = sb("winv", [P, 4])
        wm127 = sb("wm127", [P, 4])
        st1 = sb("st1", [P, 2, 6])
        mv1 = sb("mv1", [P, 2, 2])
        ve1 = sb("ve1", [P, 2])
        rs1 = sb("rs1", [P, 2])
        xn = sb("xn", [P, 2, D])
        xnT = sb("xnT", [P, DC, 2 * P])
        qT = sb("qT", [P, DC, 2 * P])
        kT = sb("kT", [P, DC, 2, 4 * S])
        vb = sb("vb", [P, 2, 2, D])
        nmax = sb("nmax", [P, 2])
        nmaxs = sb("nmaxs", [P, 2])
        probs = sb("probs", [P, 2, P])
        psums = sb("psums", [P, 2])
        pinv = sb("pinv", [P, 2])
        pT = sb("pT", [P, 2, P])
        oT = sb("oT", [P, DC, 2 * P])
        st2 = sb("st2", [P, 2, 6])
        mv2 = sb("mv2", [P, 2, 2])
        ve2 = sb("ve2", [P, 2])
        rs2 = sb("rs2", [P, 2])
        hold = sb("hold", [P, 2])
        hold2 = sb("hold2", [P, 2])
        xn2 = sb("xn2", [P, 2, D])
        amax = sb("amax", [P, 2])
        amaxc = sb("amaxc", [P, 2])
        arec = sb("arec", [P, 2])
        ascale = sb("ascale", [P, 2])
        xq = sb("xq", [P, 2, D], BF16)
        xh = sb("xh", [P, 2, D])
        xhT = sb("xhT", [P, DC, 2 * P])
        ainv = sb("ainv", [P, 2])
        aG = sb("aG", [P, 2])
        aGh = sb("aGh", [P, 2])
        xqT = sb("xqT", [P, DC, 2 * P], BF16)
        th = outf[:, 0 * FF:1 * FF]
        us = outf[:, 1 * FF:2 * FF]
        h1 = outf[:, 2 * FF:3 * FF]
        h2 = outf[:, 3 * FF:4 * FF]
        hm = sb("hm", [P, 4])
        hq = sb("hq", [P, FF], BF16)
        bD = sb("bD", [P, 2])
        hqT = sb("hqT", [FP, FK, P], BF16)
        wqb = sb("wqb", [P, 2, P])
        wkb = sb("wkb", [P, 2, P])
        wvb = sb("wvb", [P, P])
        wob = sb("wob", [P, P])
        bias = sb("bias", [P, 8])
        boe = sb("boe", [P, 1])
        cos = sb("cos", [P, D])
        sin = sb("sin", [P, D])
        cst = [sb(f"cst{i}", [P, D]) for i in range(NBUF)]
        st3 = sb("st3", [P, 6])
        mv3 = sb("mv3", [P, 2])
        ve3 = sb("ve3", [P, 1])
        rs3 = sb("rs3", [P, 1])
        xn3 = sb("xn3", [P, D])
        rope = wattn[:, 0:4 * D].rearrange("p (a i d) -> p a i d", a=2, i=2)
        qk = wattn[:, 4 * D:6 * D].rearrange("p (a d) -> p a d", a=2)
        qkr = wattn[:, 6 * D:8 * D].rearrange("p (a d) -> p a d", a=2)
        parts = sb("parts", [P, 2, 3, D], BF16)
        QS = [sb(f"QS{i}", [P, 2, 2, PAIRS, D], BF16) for i in range(NBUF)]
        KS = [sb(f"KS{i}", [P, 2, PAIRS, D], BF16) for i in range(NBUF)]
        VZ = [sb(f"VZ{i}", [P, 8, 160]) for i in range(NBUF)]
        OZ = sb("OZ", [P, 160])
        rows = sb("rows", [33, 2 * PAIRS * D], BF16)
        row1, row0 = rows[0:1, :], rows[32:33, :]
        mx = sb("mx", [P, 2, 16])
        mxT = sb("mxT", [16, D], BF16)
        dinv = sb("dinv", [P, D])
        ob = sb("ob", [P, D])
        gam = sb("gam", [P, D])
        bet = sb("bet", [P, D])
        ssum = pbf[:, 7424:7424 + D]
        sneg = pbf[:, 7424 + D:7424 + 2 * D]
        sig = sb("sig", [P, D])
        ckey = sb("ckey", [P, NTILE])
        giota = sb("giota", [P, GRID])
        table = sb("table", [NTILE, 2 * SLICE * GRID + 3])
        st4 = sb("st4", [P, 6])
        mv4 = sb("mv4", [P, 2])
        ve4 = sb("ve4", [P, 2])
        rs4 = sb("rs4", [P, 2])
        st5 = sb("st5", [P, 6])
        mv5 = sb("mv5", [P, 2])
        kTf = kT[:, :, :, :].rearrange("p c j n -> p (c j n)")
        xn4, xn5, xf, wk1 = (kTf[:, i * D:(i + 1) * D] for i in range(4))
        wk2 = sb("wk2", [P, D])
        wk3 = sb("wk3", [P, D])
        tsc = sb("tsc", [P, NTILE])
        csc = sb("csc", [P, CLUSTERS])
        key1 = sb("key1", [P, NTILE])
        key2 = sb("key2", [P, NTILE])
        kmax = sb("kmax", [P, 1])
        oh = vb[:, :, :, :].rearrange("p a b (c t) -> p (a b c) t", t=NTILE)
        xs = sb("xs", [P, NT, SLICE])
        tmm = sb("tmm", [P, NT, 2])
        bigm = pbf[:, 0:1024].rearrange("p (n t) -> p n t", n=NT)
        cand = pbf[:, 1024:2048].rearrange("p (n t) -> p n t", n=NT)
        mpart = pbf[:, 2048:2048 + 2 * NTILE].rearrange("p (a t) -> p a t", a=2)
        gmask = pbf[:, 2304:3328]
        gprod = pbf[:, 3328:4352]
        ohT = pbf[0:NTILE, 6144:6144 + NT * P].rearrange("p (n t) -> p n t", n=NT)
        u0, u1, u2, u3, u4, u5 = [sb(f"u{i}", [P, NT, SLICE]) for i in range(6)]
        span = sb("span", [P, 4, NT])
        bsel = sb("bsel", [P, NT, SLICE])
        ssel = sb("ssel", [P, NT, SLICE])
        delta = sb("delta", [P, NT, SLICE])

        bk = [ctx.enter_context(nc.psum_tensor(f"bank{i}", [P, 512], F32)) for i in range(4)]
        big = ctx.enter_context(nc.psum_tensor("big", [P, 4, 512], F32))
        bankA, bankB, bankC, bankD = bk
        G = big[:, 0:2, 0:FH]
        U = big[:, 2:4, 0:FH]
        bankDb = bankD[:, :].bitcast(BF16)
        EX = [big[:, 2 * i:2 * i + 2, :].rearrange("p s n -> p (s n)") for i in range(2)]
        MXB = [bankA, bankB]
        AV = bankC
        MISC = bankD

        scr = [nc.dram_tensor(f"scr{i}", [6, P, D], BF16).ap() for i in range(NBUF)]

        block = ctx.enter_context(nc.Block())

        @block.sync
        def _(sp):
            sp.dma_start(ident[:, :], A["ident"]).then_inc(sem["ident_loaded"], 16)
            xin = A["x"].rearrange("(n two) s d -> (two s) n d", two=2)
            sp.dma_start(xall[:, 0:2, :], xin[:, 0:2, :]).then_inc(sem["x0_loaded"], 16)
            for dst, name in ((wqT, "wq"), (wkT, "wk"), (wvT, "wv")):
                sp.dma_start(dst[:, :, :], A[name].rearrange("(c p) e -> p c e", p=P)).then_inc(sem["attn_w_loaded"], 16)

            sp.dma_start(xall[:, 2:6, :], xin[:, 2:6, :]).then_inc(sem["x_loaded"], 16)
            sp.dma_start(woT[:, :, :], A["wo"].rearrange("(c p) e -> p c e", p=P)).then_inc(sem["wo_loaded"], 16)
            for i, name in enumerate(("wg", "wu")):
                sp.dma_start(wffn[:, i, :].rearrange("p (c f) -> p c f", c=DC),
                             A[name].rearrange("(c p) f -> p c f", p=P)).then_inc(sem["ffn_w_loaded"], 16)
            sp.dma_start(wdn.rearrange("p (k d) -> p k d", k=FK),
                         A["wd"].rearrange("(k p) d -> p k d", p=FP)).then_inc(sem["ffn_w_loaded"], 16)
            sp.dma_start(xall[:, 6:NT, :], xin[:, 6:NT, :]).then_inc(sem["x_loaded"], 16)
            for dst, name in ((wqb[:, :, :], "wqb"), (wkb[:, :, :], "wkb"), (wvb[:, :], "wvb"),
                              (wob[:, :], "wob"), (bias[:, 0:6], "bias"), (cos[:, :], "cos"), (sin[:, :], "sin")):
                sp.dma_start(dst, A[name]).then_inc(sem["chan_w_loaded"], 16)
            sp.dma_start(gam[:, :], A["gamma"].to_broadcast([P, D])).then_inc(sem["ffn2_loaded"], 16)
            sp.dma_start(bet[:, :], A["beta"].to_broadcast([P, D])).then_inc(sem["ffn2_loaded"], 16)
            sp.dma_start(pbf[:, 0:D * GRID],
                         A["slopes_row"].to_broadcast([P, D * GRID])).then_inc(sem["ffn2_loaded"], 16)
            sp.dma_start(table[:, 0:64], A["bases"]).then_inc(sem["ffn2_loaded"], 16)
            sp.dma_start(table[:, 64:128], A["slopes"]).then_inc(sem["ffn2_loaded"], 16)
            sp.dma_start(table[:, 130:131], A["oscale"]).then_inc(sem["ffn2_loaded"], 16)
            sp.dma_start(ckey[:, :], A["ckey"].to_broadcast([P, NTILE])).then_inc(sem["ffn2_loaded"], 16)
            sp.dma_start(giota[:, :], A["giota"].to_broadcast([P, GRID])).then_inc(sem["ffn2_loaded"], 16)
            sp.wait_ge(sem["const_ready"], 3)
            for i in range(NBUF):
                for par in range(2):
                    r = 64 * par + 48
                    sp.dma_start(KS[i][r:r + 1, :, :, :].rearrange("p b k t -> p (b k t)"),
                                 row1).then_inc(sem["ones_row_placed"], 16)
            def spread(t, u, w):
                sv = scr[u].rearrange("(a r) (par c g) t -> a par r c (g t)", a=2, par=2, c=HC)
                for a in range(2):
                    n = t * 2 + a
                    sp.wait_ge(sem["parts_ready"], n + 1)
                    sp.dma_start(scr[u][3 * a:3 * a + 3].rearrange("r p t -> p r t"),
                                 parts[:, a, :, :]).then_inc(sem["parts_stored"], 16)
                    if a == 0:
                        if not (isinstance(t, int) and t < NBUF):
                            sp.wait_ge(sem["sT_psum"], (t - (NBUF - 1)) * GRANULES)
                        for par in range(2):
                            r = 64 * par + 48
                            sp.dma_start(QS[u][r:r + 1, par, :, :, :].rearrange("p b k t -> p (b k t)"),
                                         row0).then_inc(spread_done[u], 16)
                    sp.wait_ge(sem["parts_stored"], (n + 1) * 16)
                    for par in range(2):
                        q0 = 64 * par
                        for at, m, piece in ((0, 3, 0), (3, 2, 1), (5, 1, 2)):
                            rows = slice(q0 + 8 * at, q0 + 8 * (at + m))
                            if a == 0:
                                sp.dma_start(QS[u][rows, par, :, :, :].rearrange("p b k t -> p (b k t)"),
                                             sv[0, par, 0:m, :, :]).then_inc(spread_done[u], 16)
                            else:
                                sp.dma_start(KS[u][rows, :, :, :].rearrange("p b k t -> p (b k t)"),
                                             sv[1, par, piece:piece + 1, :, :].to_broadcast([m, HC, 2048])
                                             ).then_inc(spread_done[u], 16)

            def max_rows(t, u, w):
                sp.wait_ge(sem["maxT_ready"], t + 1)
                for par in range(2):
                    r = 64 * par + 48
                    sp.dma_start(QS[u][r:r + 1, par, :, :, :].rearrange("p b k t -> p (b k t)"),
                                 mxT[8 * par:8 * par + 8, :]).then_inc(sem["maxrow_done"], 16)

            spread(*tile(0, 0))
            spread(*tile(0, 1))

            def slot(turn, off):
                if live(tile(turn, off)[0]):
                    max_rows(*tile(turn, off))
                if live(tile(turn, off + 2)[0]):
                    spread(*tile(turn, off + 2))

            for s in range(4):
                slot(0, s)
            with sp.Fori(1, 4) as i:
                for r in range(1, 4):
                    slot(i, r)
            for s in range(13, NT):
                slot(0, s)
            ov = out.rearrange("(n two) s d -> (two s) n d", two=2)
            for q in range(4):
                sp.wait_ge(sem["out_dve" if q % 2 == 0 else "out_pool"], q // 2 + 1)
                sp.dma_start(ov[:, 4 * q:4 * q + 4, :], outb[:, 4 * q:4 * q + 4, :]).then_inc(sem["out_stored"], 16)
            sp.wait_ge(sem["out_stored"], 64)

        @block.gpsimd
        def _(pool):
            nc.gpsimd.memset(row1, 1.0).then_inc(sem["const_ready"], 1)
            nc.gpsimd.memset(row0, 0.0).then_inc(sem["const_ready"], 1)
            pool.wait_ge(sem["const_ready"], 2)
            def rstd(name, ve, rs, t):
                pool.wait_ge(sem[name + "_var"], t + 1)
                w = ve.shape[1]
                nc.gpsimd.tensor_tensor(rs, ve, halfneg[:, 0:w], ALU.pow).then_inc(sem[name + "_rstd"], 1)

            pool.wait_ge(sem["ident_ready"], 1)
            rstd("ln1", ve1[:, :], rs1[:, :], 0)
            rstd("ln1", ve1[:, :], rs1[:, :], 1)
            def split(t, a):
                n = t * 2 + a
                pool.wait_ge(sem["rope_k" if a else "rope_q"], t + 1)
                nc.gpsimd.tensor_tensor(qk[:, a, :], rope[:, a, 0, :], rope[:, a, 1, :], ALU.add).then_inc(sem["qk_sum"], 1)
                pool.wait_ge(sem["qk_sum"], n + 1)
                if not (isinstance(t, int) and t == 0):
                    pool.wait_ge(sem["parts_stored"], (n - 1) * 16)
                nc.gpsimd.tensor_tensor(hold2[:, 0:1], halfneg[:, 0:1], halfneg[:, 1:2], ALU.add)
                nc.gpsimd.tensor_scalar(parts[:, a, 0, :], qk[:, a, :], 1.0, None, ALU.mult).then_inc(sem["part1"], 1)
                pool.wait_ge(sem["part1"], n + 1)
                nc.gpsimd.tensor_tensor(qkr[:, a, :], qk[:, a, :], parts[:, a, 0, :], ALU.subtract).then_inc(sem["rest1"], 1)
                pool.wait_ge(sem["rest1"], n + 1)
                nc.gpsimd.tensor_tensor(hold2[:, 1:2], halfneg[:, 0:1], halfneg[:, 1:2], ALU.add)
                nc.gpsimd.tensor_scalar(parts[:, a, 1, :], qkr[:, a, :], 1.0, None, ALU.mult).then_inc(sem["part2"], 1)
                pool.wait_ge(sem["part2"], n + 1)
                nc.gpsimd.tensor_tensor(parts[:, a, 2, :], qkr[:, a, :], parts[:, a, 1, :],
                                        ALU.subtract).then_inc(sem["parts_ready"], 1)

            def affine(t):
                pool.wait_ge(sem["xn5_ready"], t + 1)
                nc.gpsimd.tensor_tensor(wk3[:, :], xn5, gam[:, :], ALU.mult).then_inc(sem["gamma_done"], 1)
                pool.wait_ge(sem["gamma_done"], t + 1)
                pool.wait_ge(sem["xf_masked"], t)
                nc.gpsimd.tensor_tensor(xf, wk3[:, :], bet[:, :], ALU.add).then_inc(sem["xf_ready"], 1)
                nc.gpsimd.tensor_tensor(xall[:, t, :], xall[:, t, :], xn4, ALU.add).then_inc(sem["x4_ready"], 1)

            def unit(t):
                if on(t + 1):
                    rstd("ln1", ve1[:, :], rs1[:, :], t + 1)
                if on(t - 1):
                    rstd("ln2", ve2[:, :], rs2[:, :], t - 1)

            for i in range(NBUF):
                nc.gpsimd.memset(QS[i][:, :, :, :, :], 0.0)
                nc.gpsimd.memset(VZ[i][:, :, :], 0.0)
                last = nc.gpsimd.memset(KS[i][:, :, :, :], 0.0)
                if i < 2:
                    unit(i + 1)
            last.then_inc(sem["const_ready"], 1)
            with pool.Fori(3, UNITS - 1) as t:
                unit(t)
            unit(UNITS - 1)
            unit(UNITS)

            rstd("ln3", ve3[:, :], rs3[:, :], 0)
            split(0, 0)
            split(0, 1)
            rstd("ln3", ve3[:, :], rs3[:, :], 1)
            split(1, 0)
            split(1, 1)
            pool.wait_ge(sem["ffn2_loaded"], 8 * 16)

            rstd("ln3", ve3[:, :], rs3[:, :], 2)

            def slot(s):
                if live(s + 2):
                    split(s + 2, 0)
                if live(s - 2):
                    rstd("ln4", ve4[:, 0:1], rs4[:, 0:1], s - 2)
                if live(s + 2):
                    split(s + 2, 1)
                if live(s - 2):
                    rstd("ln5", ve4[:, 1:2], rs4[:, 1:2], s - 2)
                if live(s + 3):
                    rstd("ln3", ve3[:, :], rs3[:, :], s + 3)
                if live(s - 2):
                    affine(s - 2)

            for s in range(4):
                slot(s)
            with pool.Fori(4, 13) as s:
                slot(s)
            for s in range(13, NT + 2):
                slot(s)
            pool.wait_ge(sem["delta_ready"], 1)
            for q in (1, 3):
                for n in range(4 * q, 4 * q + 4):
                    nc.gpsimd.tensor_tensor(
                        outb[:, n, :].rearrange("p (t j) -> p t j", j=SLICE),
                        oh[:, n, :].unsqueeze(2).to_broadcast([P, NTILE, SLICE]),
                        delta[:, n, :].unsqueeze(1).to_broadcast([P, NTILE, SLICE]), ALU.mult).then_inc(sem["place_pool"], 1)
                pool.wait_ge(sem["place_pool"], 4 * (q // 2 + 1))
                nc.gpsimd.tensor_tensor(outb[:, 4 * q:4 * q + 4, :], outb[:, 4 * q:4 * q + 4, :],
                                        xall[:, 4 * q:4 * q + 4, :], ALU.add).then_inc(sem["out_pool"], 1)

        @block.scalar
        def _(act):
            def load_unit(t):
                if not (isinstance(t, int) and t == 0):
                    act.wait_ge(sem["s_psum"], t)
                act.dma_start(kT[:, 0, :, S:3 * S], A["ctxT"][0:P, t, :, :]).then_inc(sem["ctxT_loaded"], 16)
                act.dma_start(kT[:, 1, :, S:3 * S], A["ctxT"][P:D, t, :, :]).then_inc(sem["ctxT_loaded"], 16)
                if not (isinstance(t, int) and t == 0):
                    act.wait_ge(sem["oT_psum"], t)
                cv = A["ctx"].rearrange("(t j b) s d -> t b s j d", j=2, b=2)
                act.dma_start(vb[S:P, :, 0, :], cv[t, 0, :, :, :]).then_inc(sem["ctxV_loaded"], 16)
                act.dma_start(vb[0:S, :, 1, :], cv[t, 1, :, :, :]).then_inc(sem["ctxV_loaded"], 16)

            def a1_head(t):
                act.wait_ge(sem["xT_psum"], t + 1)
                nc.scalar.copy(xnT[:, :, :].rearrange("p c n -> p (c n)"), bankA[:, :]).then_inc(sem["xT_ready"], 1)

            def a1_qkv(t):
                act.wait_ge(sem["q_psum"], t + 1)
                nc.scalar.copy(qT[:, :, :].rearrange("p c n -> p (c n)"), bankA[:, :]).then_inc(sem["q_ready"], 1)
                act.wait_ge(sem["k_psum"], t + 1)
                nc.scalar.copy(kT[:, :, :, 0:S],
                               bankB[:, :].rearrange("p (c j n) -> p c j n", c=2, j=2)[:, :, :, 0:S])
                nc.scalar.copy(kT[:, :, :, 3 * S:4 * S],
                               bankB[:, :].rearrange("p (c j n) -> p c j n", c=2, j=2)[:, :, :, S:P]).then_inc(sem["k_ready"], 1)
                act.wait_ge(sem["v_psum"], t + 1)
                nc.scalar.copy(vb[0:S, :, 0, :], bankC[0:S, :].rearrange("p (j d) -> p j d", j=2))
                nc.scalar.copy(vb[S:P, :, 1, :], bankC[S:P, :].rearrange("p (j d) -> p j d", j=2)).then_inc(sem["v_ready"], 1)

            def a1_exp(t):
                act.wait_ge(sem["nmax_ready"], t + 1)
                for j in range(2):
                    last = nc.scalar.activation(probs[:, j, :], bankC[:, j * P:(j + 1) * P], ACT.Exp,
                                                bias=nmaxs[:, j:j + 1], scale=1.0 / 16.0, accum_out=psums[:, j:j + 1])
                last.then_inc(sem["probs_ready"], 1)

            def a1_pT(t):
                act.wait_ge(sem["pT_psum"], t + 1)
                nc.scalar.copy(pT[:, :, :].rearrange("p j n -> p (j n)"), bankC[:, 0:2 * P]).then_inc(sem["pT_ready"], 1)

            def a1_oT(t):
                act.wait_ge(sem["oT_psum"], t + 1)
                nc.scalar.copy(oT[:, :, :].rearrange("p c n -> p (c n)"), bankA[:, :]).then_inc(sem["oT_ready"], 1)

            def a2_xqT(t):
                act.wait_ge(sem["xqT_psum"], t + 1)
                nc.scalar.copy(xqT[:, :, :].rearrange("p c n -> p (c n)"), bankDb[:, 0:512]).then_inc(sem["xqT_ready"], 1)

            def a2_xhT(t):
                act.wait_ge(sem["xhT_psum"], t + 1)
                nc.scalar.copy(xhT[:, :, :].rearrange("p c n -> p (c n)"), bankC[:, :]).then_inc(sem["xhT_ready"], 1)

            def a2_silu(t, j):
                act.wait_ge(sem["act_scale3"], t + 1)
                act.wait_ge(sem["gateup_psum"], t * 2 + (j + 1))
                if not (isinstance(t, int) and t == 0 and j == 0):
                    act.wait_ge(sem["h_half"], t * 2 + j)
                nc.scalar.activation(th.rearrange("p (a n) -> p a n", a=2), G, ACT.Tanh,
                                     scale=aGh[:, j:j + 1]).then_inc(sem["gate_ready"], 1)
                nc.scalar.activation(us.rearrange("p (a n) -> p a n", a=2), U, ACT.Copy,
                                     scale=aGh[:, j:j + 1]).then_inc(sem["up_ready"], 1)

            def a2_hT(t, j):
                act.wait_ge(sem["hT_psum"], t * 2 + (j + 1))
                nc.scalar.copy(hqT[:, :, :].rearrange("p k n -> p (k n)"), bankDb[0:FP, :]).then_inc(sem["hT_ready"], 1)

            ctile = A["ctx"].rearrange("(n two) s d -> n (two s) d", two=2)

            def load_ctx(t, u, w):
                if not (isinstance(t, int) and t < NBUF):
                    act.wait_ge(sem["vproj_psum"], t - (NBUF - 1))
                act.dma_start(cst[u][:, :], ctile[t, :, :]).then_inc(ctx_loaded[u], 16)

            def v_out(t, u, w):
                act.wait_ge(sem["vproj_psum"], t + 1)
                if not (isinstance(t, int) and t < NBUF):
                    act.wait_ge(sem["av_psum"], (t - (NBUF - 1)) * 2)
                nc.scalar.copy(VZ[u][:, :, :].rearrange("p k (a b) -> p k a b", b=40)[:, :, :, 0:HC],
                               proj_bank(t)[:, 0:256].rearrange("p (k a c) -> p k a c", k=8, a=4)).then_inc(sem["vz_ready"], 1)

            def max_out(t):
                act.wait_ge(sem["maxT_psum"], t + 1)
                if not (isinstance(t, int) and t == 0):
                    act.wait_ge(sem["maxrow_done"], t * 32)
                nc.scalar.activation(mxT[:, :], MISC[0:16, 0:256], ACT.Copy, scale=-1.0).then_inc(sem["maxT_ready"], 1)

            def exp(t, u, w, k):
                act.wait_ge(sem["sT_psum"], t * GRANULES + (k + 1))
                if not (isinstance(t, int) and t == 0):
                    act.wait_ge(sem["av_psum"], t * 2 + (k // 4 - 1))
                nc.scalar.activation(PB[:, k, :], EX[k % 2], ACT.Exp, scale=float(HC) ** -0.5).then_inc(sem["exp_ready"], 1)

            def unit(t, b=None):
                if on(t):
                    a1_head(t)
                if on(t - 2):
                    a2_silu(t - 2, 0)
                if on(t):
                    a1_qkv(t)
                if on(t - 2):
                    a2_silu(t - 2, 1)
                if on(t):
                    a1_exp(t)
                if on(t - 2):
                    a2_hT(t - 2, 0)
                if on(t):
                    a1_pT(t)
                    a1_oT(t)
                if on(t - 1):
                    a2_xqT(t - 1)
                    a2_xhT(t - 1)
                if on(t - 2):
                    a2_hT(t - 2, 1)
                if b is not None:
                    v_out(*tile(0, b))
                if on(t + 1):
                    load_unit(t + 1)

            load_unit(0)
            for t in range(3):
                unit(t)
            with act.Fori(3, UNITS - 1) as t:
                unit(t)
            unit(UNITS - 1)
            for t in range(NBUF):
                load_ctx(t, t, 0)
            act.wait_ge(sem["const_ready"], 3)
            unit(UNITS, 0)
            unit(UNITS + 1, 1)

            def slot(turn, off):
                s = tile(turn, off)[0]
                for k in range(GRANULES):
                    if k == 1 and live(s):
                        max_out(s)
                    if k < LAG and live(s - 1):
                        exp(*tile(turn, off - 1), k + GRANULES - LAG)
                    if k >= LAG and live(s):
                        exp(*tile(turn, off), k - LAG)
                    if k == 3 and live(s + 3):
                        load_ctx(*tile(turn, off + 3))
                    if k == 4 and live(s + 2):
                        v_out(*tile(turn, off + 2))

            for s in range(4):
                slot(0, s)
            with act.Fori(1, 4) as i:
                for r in range(1, 4):
                    slot(i, r)
            for s in range(13, NT + 1):
                slot(0, s)
            for g in range(4):
                act.wait_ge(sem["ohT_psum"], g + 1)
                nc.scalar.copy(ohT[:, 4 * g:4 * g + 4, :].rearrange("p n t -> p (n t)"),
                               (bankA if g % 2 == 0 else bankB)[0:NTILE, :]).then_inc(sem["ohT_ready"], 1)
            for g in range(6):
                w = min(3, NT - 3 * g)
                act.wait_ge(sem["look_psum"], g + 1)
                nc.scalar.copy(look[:, 3 * g:3 * g + w, :].rearrange("p n c -> p (n c)"),
                               big[:, g % 4, 0:w * 131]).then_inc(sem["look_ready"], 1)

        @block.tensor
        def _(pe):
            mm = nc.tensor.matmul

            def a1_s1(t):
                pe.wait_ge(sem["xn_ready"], t + 1)
                if not isinstance(t, int) or t > 2:
                    pe.wait_ge(sem["x2_ready"], (t - 2) * 2)
                elif t > 0:
                    pe.wait_ge(sem["oT_ready"], t)
                for c in range(DC):
                    for j in range(2):
                        last = nc.tensor.transpose(bankA[:, c * 256 + j * P:c * 256 + (j + 1) * P],
                                                   xn[:, j, c * P:(c + 1) * P], ident[:, :])
                last.then_inc(sem["xT_psum"], 1)

            def a1_s2(t):
                pe.wait_ge(sem["xT_ready"], t + 1)
                pe.wait_ge(sem["attn_w_loaded"], 48)
                for e in range(DC):
                    for c in range(DC):
                        last = mm(bankA[:, e * 256:(e + 1) * 256], wqT[:, c, e * P:(e + 1) * P], xnT[:, c, :],
                                  start=c == 0, stop=c == DC - 1)
                last.then_inc(sem["q_psum"], 1)
                if not (isinstance(t, int) and t == 0):
                    pe.wait_ge(sem["x1_ready"], t)
                for e in range(DC):
                    for c in range(DC):
                        last = mm(bankB[:, e * 256:(e + 1) * 256], wkT[:, c, e * P:(e + 1) * P], xnT[:, c, :],
                                  start=c == 0, stop=c == DC - 1)
                last.then_inc(sem["k_psum"], 1)
                if not isinstance(t, int) or t > 1:
                    pe.wait_ge(sem["xhT_ready"], t - 1)
                elif t == 1:
                    pe.wait_ge(sem["pT_ready"], 1)
                for j in range(2):
                    for c in range(DC):
                        last = mm(bankC[:, j * 256:(j + 1) * 256], xnT[:, c, j * P:(j + 1) * P], wvT[:, c, :],
                                  start=c == 0, stop=c == DC - 1)
                last.then_inc(sem["v_psum"], 1)

            def a1_s3(t):
                pe.wait_ge(sem["k_ready"], t + 1)
                pe.wait_ge(sem["v_ready"], t + 1)
                pe.wait_ge(sem["ctxT_loaded"], (t + 1) * 32)
                for j in range(2):
                    for b in range(2):
                        for c in range(DC):
                            last = mm(bankC[b * S:(b + 1) * S, j * P:(j + 1) * P],
                                      qT[:, c, j * P + b * S:j * P + (b + 1) * S], kT[:, c, j, b * P:(b + 1) * P],
                                      start=c == 0, stop=c == DC - 1)
                last.then_inc(sem["s_psum"], 1)

            def a1_s4(t):
                pe.wait_ge(sem["probs_ready"], t + 1)
                for j in range(2):
                    last = nc.tensor.transpose(bankC[:, j * P:(j + 1) * P], probs[:, j, :], ident[:, :])
                last.then_inc(sem["pT_psum"], 1)

            def a1_s5(t):
                pe.wait_ge(sem["pT_ready"], t + 1)
                pe.wait_ge(sem["ctxV_loaded"], (t + 1) * 32)
                for c in range(DC):
                    for j in range(2):
                        for b in range(2):
                            at = c * 256 + j * P + b * S
                            last = mm(bankA[:, at:at + S], vb[:, j, b, c * P:(c + 1) * P], pT[:, j, b * S:(b + 1) * S],
                                      start=True, stop=True)
                last.then_inc(sem["oT_psum"], 1)

            def a1_s6(t):
                pe.wait_ge(sem["oT_ready"], t + 1)
                pe.wait_ge(sem["wo_loaded"], 16)
                if not isinstance(t, int) or t > 1:
                    pe.wait_ge(sem["x2_ready"], t * 2 - 3)
                for j in range(2):
                    for c in range(DC):
                        last = mm(bankB[:, j * 256:(j + 1) * 256], oT[:, c, j * P:(j + 1) * P], woT[:, c, :],
                                  start=c == 0, stop=c == DC - 1)
                last.then_inc(sem["y_psum"], 1)

            def a2_r1(t):
                pe.wait_ge(sem["xq_ready"], t + 1)
                if not (isinstance(t, int) and t == 0):
                    pe.wait_ge(sem["hT_ready"], t * 2 - 1)
                for c in range(DC):
                    for j in range(2):
                        last = nc.tensor.transpose(bankDb[:, c * 256 + j * P:c * 256 + (j + 1) * P],
                                                   xq[:, j, c * P:(c + 1) * P], identb[:, :])
                last.then_inc(sem["xqT_psum"], 1)

            def a2_r1h(t):
                pe.wait_ge(sem["xh_ready"], t + 1)
                pe.wait_ge(sem["pT_ready"], t + 2 if on(t + 1) else UNITS)
                for c in range(DC):
                    for j in range(2):
                        last = nc.tensor.transpose(bankC[:, c * 256 + j * P:c * 256 + (j + 1) * P],
                                                   xh[:, j, c * P:(c + 1) * P], ident[:, :])
                last.then_inc(sem["xhT_psum"], 1)

            def a2_r2(t, j):
                pe.wait_ge(sem["xqT_ready"], t + 1)
                pe.wait_ge(sem["w_ready"], 3)
                if not (isinstance(t, int) and t == 0 and j == 0):
                    pe.wait_ge(sem["h_ready"], t * 2 + j)
                pe.wait_ge(sem["xhT_ready"], t + 1)
                for w, src, dst in ((wgT, xqT, G), (wuT, xhT, U)):
                    for f in range(2):
                        for c in range(DC):
                            last = mm(dst[:, f, :], src[:, c, j * P:(j + 1) * P], w[:, c, f * FH:(f + 1) * FH],
                                      start=c == 0, stop=c == DC - 1)
                last.then_inc(sem["gateup_psum"], 1)

            def a2_r4(t, j):
                pe.wait_ge(sem["hq_ready"], t * 2 + (j + 1))
                if j == 0:
                    pe.wait_ge(sem["xqT_ready"], t + 1)
                    if not (isinstance(t, int) and t == 0):
                        pe.wait_ge(sem["hT_ready"], t * 2)
                else:
                    pe.wait_ge(sem["hT_ready"], t * 2 + 1)
                    if on(t + 1):
                        pe.wait_ge(sem["xqT_ready"], t + 2)
                for k in range(FK):
                    last = nc.tensor.transpose(bankDb[0:FP, k * P:(k + 1) * P], hq[:, k * FP:(k + 1) * FP], identb[:, :])
                last.then_inc(sem["hT_psum"], 1)

            def a2_r5(t, j):
                pe.wait_ge(sem["hT_ready"], t * 2 + (j + 1))
                if on(t + 2):
                    pe.wait_ge(sem["oT_ready" if j else "k_ready"], t + 3)
                else:
                    if j == 1:
                        pe.wait_ge(sem["vz_ready"], t - (UNITS - 3))
                    pe.wait_ge(sem["x1_ready"], UNITS)
                    pe.wait_ge(sem["x2_ready"], t * 2 + j - 1)
                for k in range(FK):
                    last = mm((bankA if j else bankB)[:, 0:D], hqT[:, k, :], wdT[:, k, :], start=k == 0, stop=k == FK - 1)
                last.then_inc(sem["down_psum"], 1)

            pe.wait_ge(sem["ident_ready"], 1)
            a1_s1(0)
            a1_s2(0)
            a1_s3(0)
            a1_s4(0)
            a1_s5(0)
            a1_s6(0)
            pe.wait_ge(sem["wsum_ready"], 3)
            for i in range(3):
                n = P if i < 2 else FP
                last = mm(bankD[:, i:i + 1], ones[0:n, :], wsum[0:n, i:i + 1], start=True, stop=True)
            last.then_inc(sem["wtot_ready"], 1)
            pe.wait_ge(sem["wmean_ready"], 1)
            pe.wait_ge(sem["chan_w_loaded"], 7 * 16)
            mm(bankD[:, 8:9], wob[:, :], bias[:, 4:5], start=True, stop=True).then_inc(sem["bo_sum_ready"], 1)
            pe.wait_ge(sem["bo_ready"], 1)
            def proj_q(t):
                if isinstance(t, int) and t == 0:
                    pe.wait_ge(sem["x2_ready"], NT - 4)
                if isinstance(t, int) and t == 1:
                    pe.wait_ge(sem["xhT_ready"], UNITS)
                pe.wait_ge(sem["xn3_ready"], t + 1)
                if not isinstance(t, int) or t > NBUF:
                    pe.wait_ge(sem["x3_ready"], t - NBUF)
                elif t > 0:
                    pe.wait_ge(sem["vz_ready"], t)
                for i in range(2):
                    last = mm(proj_bank(t)[:, i * D:(i + 1) * D], wqb[:, i, :], xn3[:, :], start=True, stop=True)
                last.then_inc(sem["qproj_psum"], 1)

            def proj_k(t, u, w):
                pe.wait_ge(sem["rope_q"], t + 1)
                if not isinstance(t, int) or t >= 2:
                    pe.wait_ge(sem["maxT_ready"], t - 1)
                pe.wait_ge(ctx_loaded[u], (w + 1) * 16)
                for i in range(2):
                    last = mm(proj_bank(t)[:, i * D:(i + 1) * D], wkb[:, i, :], cst[u][:, :], start=True, stop=True)
                last.then_inc(sem["kproj_psum"], 1)

            def proj_v(t, u, w):
                pe.wait_ge(sem["rope_k"], t + 1)
                for st in range(2):
                    last = mm(proj_bank(t)[:, st * P:(st + 1) * P], cst[u][:, st * P:(st + 1) * P], wvb[:, :],
                              start=True, stop=True)
                last.then_inc(sem["vproj_psum"], 1)

            def score_max(t, u, w, m, first=False):
                if m == 0:
                    pe.wait_ge(spread_done[u], (w + 1) * (16 * SPREADS))
                if not (first and m < 2):
                    pe.wait_ge(sem["max_ready"], t * MAXG + (m - 1))
                b, tt, pair = m // 8, m // 4 % 2, m % 4
                for par in range(2):
                    last = mm(MXB[m % 2][:, par * D:(par + 1) * D], QS[u][:, par, b, pair, tt * P:(tt + 1) * P],
                              KS[u][:, b, pair, :], start=True, stop=True)
                last.then_inc(sem["max_psum"], 1)

            def max_turn(t):
                pe.wait_ge(sem["max_ready"], (t + 1) * MAXG)
                if live(t + 2):
                    pe.wait_ge(sem["rope_q"], t + 3)
                else:
                    pe.wait_ge(sem["x3_ready"], t - 1)
                for tt in range(2):
                    last = nc.tensor.transpose(MISC[0:16, tt * P:(tt + 1) * P], mx[:, tt, :], ident[:, :])
                last.then_inc(sem["maxT_psum"], 1)

            def score(t, u, w, k):
                if k == 0:
                    pe.wait_ge(sem["maxrow_done"], (t + 1) * 32)
                if not (isinstance(t, int) and t == 0 and k < 2):
                    pe.wait_ge(sem["exp_ready"], t * GRANULES + (k - 1))
                b, pair = k % 4 // 2, 2 * (k % 2) + k // 4
                for st in range(2):
                    last = mm(EX[k % 2][:, st * 512:(st + 1) * 512], KS[u][:, b, pair, st * P:(st + 1) * P],
                              QS[u][:, :, b, pair, :], start=True, stop=True)
                last.then_inc(sem["sT_psum"], 1)

            def values(t, u, w, half, par):
                if par == 0:
                    pe.wait_ge(sem["exp_ready"], t * GRANULES + (4 * half + 4))
                if half == 0 and par == 0:
                    pe.wait_ge(sem["vz_ready"], t + 1)
                    if not (isinstance(t, int) and t == 0):
                        pe.wait_ge(sem["o_ready"], t)
                for st in range(2):
                    for den in range(2):
                        for g in range(4):
                            slot = 2 * half + par
                            w = OZ[:, 32 * slot:32 * slot + 32] if den else \
                                VZ[u][:, st * 4 + g, 32 * slot:32 * slot + 32]
                            last = mm(AV[32 * g:32 * g + 32, den * D:(den + 1) * D], w,
                                      PB[:, 4 * half + g, st * 512 + par * D:st * 512 + (par + 1) * D],
                                      start=(slot == 0 and st == 0 and den == 0),
                                      stop=(slot == 3 and st == 1), skip_group_check=True)
                if par == 1:
                    last.then_inc(sem["av_psum"], 1)

            def out_proj(t):
                if live(t + 3):
                    pe.wait_ge(sem["vz_ready"], t + 4)
                elif live(t + 1):
                    pe.wait_ge(sem["maxT_ready"], t + 2)
                else:
                    pe.wait_ge(sem["x3_ready"], t)
                pe.wait_ge(sem["o_ready"], t + 1)
                mm(MISC[:, 0:D], wob[:, :], ob[:, :], start=True, stop=True).then_inc(sem["yc_psum"], 1)


            def unit(t, b=None):
                if on(t):
                    a1_s1(t)
                if on(t - 2):
                    a2_r2(t - 2, 0)
                if b is not None:
                    proj_q(b)
                if on(t):
                    a1_s2(t)
                if on(t - 2):
                    a2_r2(t - 2, 1)
                if on(t):
                    a1_s3(t)
                if on(t - 2):
                    a2_r4(t - 2, 0)
                if on(t):
                    a1_s4(t)
                if on(t - 2):
                    a2_r5(t - 2, 0)
                if b is not None:
                    proj_k(*tile(0, b))
                if on(t):
                    a1_s5(t)
                if on(t - 1):
                    a2_r1(t - 1)
                    a2_r1h(t - 1)
                if on(t - 2):
                    a2_r4(t - 2, 1)
                if b is not None:
                    proj_v(*tile(0, b))
                if on(t):
                    a1_s6(t)
                if on(t - 2):
                    a2_r5(t - 2, 1)

            unit(1)
            unit(2)
            with pe.Fori(3, UNITS - 1) as t:
                unit(t)
            unit(UNITS - 1)
            unit(UNITS, 0)
            unit(UNITS + 1, 1)

            pe.wait_ge(sem["x2_ready"], NT)
            pe.wait_ge(sem["ones_row_placed"], 2 * NBUF * 16)

            for m in range(MAXG):
                score_max(*tile(0, 0), m, first=True)
            proj_q(2)

            def slot(turn, off):
                s = tile(turn, off)[0]
                for k in range(GRANULES):
                    if k < LAG and live(s - 1):
                        score(*tile(turn, off - 1), k + GRANULES - LAG)
                    if k >= LAG and live(s):
                        score(*tile(turn, off), k - LAG)
                    if k == 0 and live(s):
                        max_turn(s)
                    if live(s + 1):
                        score_max(*tile(turn, off + 1), 2 * k)
                        score_max(*tile(turn, off + 1), 2 * k + 1)
                    if k == 1 and live(s + 2):
                        proj_k(*tile(turn, off + 2))
                    if k == 2 and live(s + 2):
                        proj_v(*tile(turn, off + 2))
                    if k == 0 and live(s - 1):
                        values(*tile(turn, off - 1), 0, 1)
                    if k in (3, 4) and live(s - 1):
                        values(*tile(turn, off - 1), 1, k - 3)
                    if k == 6 and live(s - 1):
                        out_proj(s - 1)
                    if k == 7 and live(s + 3):
                        proj_q(s + 3)
                    if k == 7 and live(s):
                        values(*tile(turn, off), 0, 0)

            for s in range(4):
                slot(0, s)
            with pe.Fori(1, 4) as i:
                for r in range(1, 4):
                    slot(i, r)
            for s in range(13, NT + 1):
                slot(0, s)
            pe.wait_ge(sem["onehot_ready"], NT)
            for g in range(4):
                if g >= 2:
                    pe.wait_ge(sem["ohT_ready"], g - 1)
                for i in range(4):
                    last = nc.tensor.transpose((bankA if g % 2 == 0 else bankB)[0:NTILE, i * P:(i + 1) * P],
                                               oh[:, 4 * g + i, :], ident[:, :])
                last.then_inc(sem["ohT_psum"], 1)
            pe.wait_ge(sem["max_part"], 1)
            for i in range(2):
                last = nc.tensor.transpose(bankC[0:NTILE, i * P:(i + 1) * P], mpart[:, i, :], ident[:, :])
            last.then_inc(sem["mm_psum"], 1)
            pe.wait_ge(sem["mm_ready"], 1)
            pe.wait_ge(sem["ohT_ready"], 4)
            for g in range(6):
                if g >= 4:
                    pe.wait_ge(sem["look_ready"], g - 3)
                for i in range(min(3, NT - 3 * g)):
                    last = mm(big[:, g % 4, i * 131:(i + 1) * 131], ohT[:, 3 * g + i, :], table[:, :],
                              start=True, stop=True)
                last.then_inc(sem["look_psum"], 1)

        @block.vector
        def _(v):
            V = nc.vector

            def stats(name, srcs, stt, mv, ve, t):
                for j, src in enumerate(srcs):
                    last = V.bn_stats(stt[j], src)
                last.then_inc(sem[name + "_steps"], 1)
                v.wait_ge(sem[name + "_steps"], t * 2 + 1)
                V.memset(hold[:, 0:1], 0.0)
                for j in range(len(srcs)):
                    last = V.bn_aggr(mv[j], stt[j])
                last.then_inc(sem[name + "_steps"], 1)
                v.wait_ge(sem[name + "_steps"], t * 2 + 2)
                for j in range(len(srcs)):
                    last = V.tensor_scalar(ve[j], mv[j][:, 1:2], LN_EPS, None, ALU.add)
                last.then_inc(sem[name + "_var"], 1)

            def ln1_stats(t):
                stats("ln1", [xall[:, t * 2 + j, :] for j in range(2)], [st1[:, j, :] for j in range(2)],
                      [mv1[:, j, :] for j in range(2)], [ve1[:, j:j + 1] for j in range(2)], t)

            def ln1_apply(t):
                v.wait_ge(sem["ln1_rstd"], t + 1)
                if not (isinstance(t, int) and t == 0):
                    v.wait_ge(sem["xT_psum"], t)
                for j in range(2):
                    last = V.tensor_scalar(xn[:, j, :], xall[:, t * 2 + j, :], mv1[:, j, 0:1], rs1[:, j:j + 1],
                                           ALU.subtract, ALU.mult)
                last.then_inc(sem["xn_ready"], 1)

            def a1_max(t):
                v.wait_ge(sem["s_psum"], t + 1)
                V.tensor_reduce(nmax[:, :], bankC[:, 0:2 * P].rearrange("p (j n) -> p j n", j=2), AX,
                                ALU.max).then_inc(sem["s_max"], 1)
                v.wait_ge(sem["s_max"], t + 1)
                V.tensor_scalar(nmaxs[:, :], nmax[:, :], -1.0 / 16.0, None, ALU.mult).then_inc(sem["nmax_ready"], 1)

            def a1_out(t):
                v.wait_ge(sem["probs_ready"], t + 1)
                V.reciprocal(pinv[:, :], psums[:, :]).then_inc(sem["rsum_ready"], 1)
                v.wait_ge(sem["rsum_ready"], t + 1)
                v.wait_ge(sem["y_psum"], t + 1)
                for j in range(2):
                    last = V.scalar_tensor_tensor(out=xall[:, t * 2 + j, :], in0=bankB[:, j * D:(j + 1) * D],
                                                  scalar=pinv[:, j:j + 1], in1=xall[:, t * 2 + j, :],
                                                  op0=ALU.mult, op1=ALU.add)
                last.then_inc(sem["x1_ready"], 1)

            def ln2_stats(t):
                stats("ln2", [xall[:, t * 2 + j, :] for j in range(2)], [st2[:, j, :] for j in range(2)],
                      [mv2[:, j, :] for j in range(2)], [ve2[:, j:j + 1] for j in range(2)], t)

            def a2_quant(t):
                v.wait_ge(sem["ln2_rstd"], t + 1)
                for j in range(2):
                    last = V.tensor_scalar(xn2[:, j, :], xall[:, t * 2 + j, :], mv2[:, j, 0:1], rs2[:, j:j + 1],
                                           ALU.subtract, ALU.mult)
                last.then_inc(sem["xn2_ready"], 1)
                v.wait_ge(sem["xn2_ready"], t + 1)
                V.tensor_reduce(amax[:, :], xn2[:, :, :], AX, ALU.max,
                                apply_absolute_value=True).then_inc(sem["amax_ready"], 1)
                v.wait_ge(sem["amax_ready"], t + 1)
                V.tensor_scalar(amaxc[:, :], amax[:, :], Q_EPS, None, ALU.max).then_inc(sem["amaxc_ready"], 1)
                v.wait_ge(sem["amaxc_ready"], t + 1)
                V.reciprocal(arec[:, :], amaxc[:, :]).then_inc(sem["arec_ready"], 1)
                V.tensor_scalar(ainv[:, :], amaxc[:, :], 1.0 / 127.0, None, ALU.mult).then_inc(sem["act_scale2"], 1)
                v.wait_ge(sem["arec_ready"], t + 1)
                V.tensor_scalar(ascale[:, :], arec[:, :], 127.0, None, ALU.mult).then_inc(sem["ascale_ready"], 1)
                v.wait_ge(sem["ascale_ready"], t + 1)
                for j in range(2):
                    last = V.tensor_scalar(xn2[:, j, :], xn2[:, j, :], ascale[:, j:j + 1], MAGIC, ALU.mult, ALU.add)
                last.then_inc(sem["a_round"], 1)
                v.wait_ge(sem["a_round"], t + 1)
                if not (isinstance(t, int) and t == 0):
                    v.wait_ge(sem["xqT_psum"], t)
                V.tensor_scalar(xq[:, :, :].rearrange("p j d -> p (j d)"), xn2[:, :, :].rearrange("p j d -> p (j d)"),
                                MAGIC, None, ALU.subtract).then_inc(sem["xq_ready"], 1)
                v.wait_ge(sem["act_scale2"], t + 1)
                for j in range(2):
                    last = V.tensor_scalar(xh[:, j, :].rearrange("p (b a) -> p a b", a=16),
                                           xn2[:, j, :].rearrange("p (a b) -> p a b", b=16),
                                           MAGIC, ainv[:, j:j + 1], ALU.subtract, ALU.mult)
                last.then_inc(sem["xh_ready"], 1)

            def a2_scale(t):
                if not (isinstance(t, int) and t == 0):
                    v.wait_ge(sem["up_ready"], t * 2)
                V.tensor_scalar(aG[:, :], amaxc[:, :], wm127[:, 0:1], None, ALU.mult).then_inc(sem["act_scale1"], 1)
                v.wait_ge(sem["act_scale1"], t + 1)
                V.tensor_scalar(aGh[:, :], aG[:, :], 0.5, None, ALU.mult).then_inc(sem["act_scale3"], 1)

            def a2_h(t, j):
                n = t * 2 + j
                v.wait_ge(sem["up_ready"], n + 1)
                if not (isinstance(n, int) and n == 0):
                    v.wait_ge(sem["hq_ready"], n)
                V.scalar_tensor_tensor(out=h1, in0=th, scalar=1.0, in1=us, op0=ALU.add,
                                       op1=ALU.mult).then_inc(sem["h_half"], 1)
                v.wait_ge(sem["h_half"], n + 1)
                V.tensor_tensor(h2.rearrange("p (a n) -> p a n", a=2), G,
                                h1.rearrange("p (a n) -> p a n", a=2), ALU.mult).then_inc(sem["h_ready"], 1)
                v.wait_ge(sem["h_ready"], n + 1)
                V.tensor_reduce(hm[:, 0:1], h2, AX, ALU.max, apply_absolute_value=True).then_inc(sem["hamax_ready"], 1)
                v.wait_ge(sem["hamax_ready"], n + 1)
                V.tensor_scalar(hm[:, 1:2], hm[:, 0:1], Q_EPS, None, ALU.max).then_inc(sem["hamaxc_ready"], 1)
                v.wait_ge(sem["hamaxc_ready"], n + 1)
                V.reciprocal(hm[:, 2:3], hm[:, 1:2]).then_inc(sem["hrec_ready"], 1)
                V.tensor_scalar(bD[:, j:j + 1], hm[:, 1:2], wm127[:, 2:3], None, ALU.mult).then_inc(sem["dscale_ready"], 1)
                v.wait_ge(sem["hrec_ready"], n + 1)
                V.tensor_scalar(hm[:, 3:4], hm[:, 2:3], 127.0, None, ALU.mult).then_inc(sem["hscale_ready"], 1)
                v.wait_ge(sem["hscale_ready"], n + 1)
                V.tensor_scalar(h1, h2, hm[:, 3:4], MAGIC, ALU.mult, ALU.add).then_inc(sem["h_round"], 1)
                v.wait_ge(sem["h_round"], n + 1)
                if not (isinstance(n, int) and n == 0):
                    v.wait_ge(sem["hT_psum"], n)
                V.tensor_scalar(hq[:, :], h1, MAGIC, None, ALU.subtract).then_inc(sem["hq_ready"], 1)

            def a2_out(t, j):
                n = t * 2 + j
                v.wait_ge(sem["dscale_ready"], n + 1)
                v.wait_ge(sem["down_psum"], n + 1)
                V.scalar_tensor_tensor(out=xall[:, n, :], in0=(bankA if j else bankB)[:, 0:D], scalar=bD[:, j:j + 1],
                                       in1=xall[:, n, :], op0=ALU.mult, op1=ALU.add).then_inc(sem["x2_ready"], 1)

            def ternary(i):
                src, dst, n = ((wffn[:, 0, :], wgT[:, :, :], P), (wffn[:, 1, :], wuT, P), (wdn, wdT[:, :, :], FP))[i]
                V.tensor_scalar(src, src, winv[0:n, i:i + 1], 1.0, ALU.mult, ALU.min).then_inc(sem["w_clip"], 1)
                v.wait_ge(sem["w_clip"], i + 1)
                V.tensor_scalar(src, src, -1.0, MAGIC, ALU.max, ALU.add).then_inc(sem["w_round"], 1)
                v.wait_ge(sem["w_round"], i + 1)
                V.tensor_scalar(dst.rearrange("p a b -> p (a b)"), src, MAGIC, wmean[:, 1:2] if i == 1 else 1.0,
                                ALU.subtract, ALU.mult).then_inc(sem["w_ready"], 1)

            V.memset(halfneg[:, :], -0.5)
            V.memset(ones[:, :], 1.0)
            V.memset(OZ[:, :], 0.0).then_inc(sem["oz_ready"], 1)
            v.wait_ge(sem["oz_ready"], 1)
            V.memset(OZ[:, :].rearrange("p (a b) -> p a b", b=40)[:, :, 0:HC], 1.0).then_inc(sem["oz_ready"], 1)
            v.wait_ge(sem["ident_loaded"], 16)
            V.tensor_copy(identb[:, :], ident[:, :]).then_inc(sem["ident_ready"], 1)
            v.wait_ge(sem["x0_loaded"], 16)
            ln1_stats(0)
            ln1_apply(0)
            v.wait_ge(sem["x_loaded"], 32)
            ln1_stats(1)
            ln1_apply(1)
            a1_max(0)
            v.wait_ge(sem["ffn_w_loaded"], 48)
            V.tensor_reduce(wsum[:, 0:2], wffn, AX, ALU.add, apply_absolute_value=True).then_inc(sem["wsum_ready"], 2)
            V.tensor_reduce(wsum[0:FP, 2:3], wdn, AX, ALU.add, apply_absolute_value=True).then_inc(sem["wsum_ready"], 1)
            v.wait_ge(sem["wtot_ready"], 1)
            V.tensor_scalar(wmean[:, 0:3], bankD[:, 0:3], 1.0 / (FF * D), Q_EPS, ALU.mult, ALU.max).then_inc(sem["wmean_ready"], 1)
            v.wait_ge(sem["wmean_ready"], 1)
            V.reciprocal(winv[:, 0:3], wmean[:, 0:3])
            V.tensor_scalar(wm127[:, 0:3], wmean[:, 0:3], 1.0 / 127.0, None, ALU.mult).then_inc(sem["winv_ready"], 1)
            v.wait_ge(sem["winv_ready"], 1)
            v.wait_ge(sem["bo_sum_ready"], 1)
            V.tensor_tensor(boe[:, :], bankD[:, 8:9], bias[:, 5:6], ALU.add).then_inc(sem["bo_ready"], 1)
            a1_out(0)
            def ln3_stats(t):
                stats("ln3", [xall[:, t, :]], [st3[:, :]], [mv3[:, :]], [ve3[:, :]], t)

            def ln3_apply(t):
                v.wait_ge(sem["ln3_rstd"], t + 1)
                if not (isinstance(t, int) and t == 0):
                    v.wait_ge(sem["qproj_psum"], t)
                V.tensor_scalar(xn3[:, :], xall[:, t, :], mv3[:, 0:1], rs3[:, 0:1],
                                ALU.subtract, ALU.mult).then_inc(sem["xn3_ready"], 1)

            def rope_part(t, a, name, psum):
                v.wait_ge(sem[psum], t + 1)
                if not (isinstance(t, int) and t == 0):
                    v.wait_ge(sem["qk_sum"], t * 2 - 1 + a)
                for i, tab in enumerate((cos, sin)):
                    last = V.scalar_tensor_tensor(out=rope[:, a, i, :], in0=proj_bank(t)[:, i * D:(i + 1) * D],
                                                  scalar=bias[:, 2 * a + i:2 * a + i + 1], in1=tab[:, :],
                                                  op0=ALU.add, op1=ALU.mult)
                last.then_inc(sem[name], 1)

            def reduce_max(t, m):
                b, tt, pair = m // 8, m // 4 % 2, m % 4
                if m == 0:
                    v.wait_ge(sem["maxT_psum"], t)
                v.wait_ge(sem["max_psum"], t * MAXG + (m + 1))
                col = mx[:, tt, :].rearrange("p (a c) -> p a c", a=2)[:, :, b * 4 + pair]
                V.tensor_reduce(col, MXB[m % 2][:, :].rearrange("p (a n) -> p a n", a=2), AX,
                                ALU.max).then_inc(sem["max_ready"], 1)

            def normalize(t):
                v.wait_ge(sem["av_psum"], t * 2 + 2)
                V.reciprocal(dinv[:, :], AV[:, D:2 * D]).then_inc(sem["den_inv"], 1)
                v.wait_ge(sem["den_inv"], t + 1)
                v.wait_ge(sem["yc_psum"], t)
                V.tensor_tensor(ob[:, :], AV[:, 0:D], dinv[:, :], ALU.mult).then_inc(sem["o_ready"], 1)

            def residual(t):
                v.wait_ge(sem["yc_psum"], t + 1)
                V.scalar_tensor_tensor(out=xall[:, t, :], in0=MISC[:, 0:D], scalar=boe[:, 0:1],
                                       in1=xall[:, t, :], op0=ALU.add, op1=ALU.add).then_inc(sem["x3_ready"], 1)

            def ln4_stats(t):
                stats("ln4", [xall[:, t, :]], [st4[:, :]], [mv4[:, :]], [ve4[:, 0:1]], t)

            def ln4_apply(t):
                v.wait_ge(sem["ln4_rstd"], t + 1)
                if not (isinstance(t, int) and t == 0):
                    v.wait_ge(sem["x4_ready"], t)
                V.tensor_scalar(xn4, xall[:, t, :], mv4[:, 0:1], rs4[:, 0:1],
                                ALU.subtract, ALU.mult).then_inc(sem["xn4_ready"], 1)
                v.wait_ge(sem["xn4_ready"], t + 1)
                stats("ln5", [xn4], [st5[:, :]], [mv5[:, :]], [ve4[:, 1:2]], t)

            def ln5_apply(t):
                v.wait_ge(sem["ln5_rstd"], t + 1)
                v.wait_ge(sem["gamma_done"], t)
                V.tensor_scalar(xn5, xn4, mv5[:, 0:1], rs4[:, 1:2],
                                ALU.subtract, ALU.mult).then_inc(sem["xn5_ready"], 1)

            def route_scores(t):
                v.wait_ge(sem["xf_ready"], t + 1)
                V.tensor_tensor(wk1, xf, sig[:, :], ALU.mult).then_inc(sem["sgn_prod"], 1)
                v.wait_ge(sem["sgn_prod"], t + 1)
                V.tensor_scalar(wk2[:, :], wk1, 0.0, None, ALU.is_lt).then_inc(sem["sgn_neg"], 1)
                v.wait_ge(sem["sgn_neg"], t + 1)
                V.scalar_tensor_tensor(out=wk1, in0=wk1, scalar=0.0, in1=wk2[:, :], op0=ALU.is_gt,
                                       op1=ALU.subtract).then_inc(sem["sgn_ready"], 1)
                v.wait_ge(sem["sgn_ready"], t + 1)
                V.tensor_reduce(tsc[:, :], wk1.rearrange("p (n j) -> p n j", j=SLICE), AX,
                                ALU.add).then_inc(sem["tile_score"], 1)
                V.tensor_reduce(csc[:, :], wk1.rearrange("p (c n) -> p c n", c=CLUSTERS), AX,
                                ALU.add).then_inc(sem["clus_score"], 1)

            def route_pick(t):
                v.wait_ge(sem["clus_score"], t + 1)
                V.scalar_tensor_tensor(out=key1[:, :].rearrange("p (c n) -> p c n", c=CLUSTERS),
                                       in0=csc[:, :].unsqueeze(2).to_broadcast([P, CLUSTERS, CLUSTERS]),
                                       scalar=1024.0, in1=ckey[:, :].rearrange("p (c n) -> p c n", c=CLUSTERS),
                                       op0=ALU.mult, op1=ALU.add).then_inc(sem["key_c"], 1)
                v.wait_ge(sem["key_c"], t + 1)
                V.scalar_tensor_tensor(out=key2[:, :], in0=tsc[:, :], scalar=8.0, in1=key1[:, :], op0=ALU.mult,
                                       op1=ALU.add).then_inc(sem["key_ready"], 1)
                v.wait_ge(sem["key_ready"], t + 1)
                V.tensor_reduce(kmax[:, :], key2[:, :], AX, ALU.max).then_inc(sem["key_max"], 1)
                v.wait_ge(sem["key_max"], t + 1)
                V.tensor_scalar(oh[:, t, :], key2[:, :], kmax[:, 0:1], None, ALU.is_equal).then_inc(sem["onehot_ready"], 1)

            def route_slice(t):
                v.wait_ge(sem["onehot_ready"], t + 1)
                V.tensor_tensor(wk2[:, :].rearrange("p (n j) -> p n j", j=SLICE),
                                xf.rearrange("p (n j) -> p n j", j=SLICE),
                                oh[:, t, :].unsqueeze(2).to_broadcast([P, NTILE, SLICE]),
                                ALU.mult).then_inc(sem["xf_masked"], 1)
                v.wait_ge(sem["xf_masked"], t + 1)
                V.tensor_reduce(xs[:, t, :], wk2[:, :].rearrange("p (n j) -> p j n", j=SLICE), AX,
                                ALU.add).then_inc(sem["slice_ready"], 1)

            def unit(t, b=None):
                if on(t + 1):
                    ln1_stats(t + 1)
                if b is not None:
                    ln3_stats(b)
                if on(t - 1):
                    v.wait_ge(sem["x1_ready"], t)
                if on(t + 1):
                    ln1_apply(t + 1)
                if on(t - 1):
                    ln2_stats(t - 1)
                    a2_quant(t - 1)
                if isinstance(t, int) and t == 1:
                    ternary(0)
                if b is not None:
                    ln3_apply(b)
                if on(t - 2):
                    a2_h(t - 2, 0)
                if b is not None:
                    rope_part(b, 0, "rope_q", "qproj_psum")
                if on(t):
                    a1_max(t)
                if isinstance(t, int) and t == 1:
                    ternary(1)
                    ternary(2)
                if on(t - 2):
                    a2_h(t - 2, 1)
                if b is not None:
                    rope_part(b, 1, "rope_k", "kproj_psum")
                if on(t - 1):
                    a2_scale(t - 1)
                if on(t - 2):
                    a2_out(t - 2, 0)
                if on(t):
                    a1_out(t)
                if on(t - 2):
                    a2_out(t - 2, 1)

            unit(1)
            unit(2)
            v.wait_ge(sem["ffn2_loaded"], 8 * 16)
            V.tensor_reduce(ssum, slopes, AX, ALU.add).then_inc(sem["slope_sum"], 1)
            v.wait_ge(sem["slope_sum"], 1)
            V.tensor_scalar(sneg, ssum, 0.0, None, ALU.is_lt).then_inc(sem["slope_neg"], 1)
            v.wait_ge(sem["slope_neg"], 1)
            V.scalar_tensor_tensor(out=sig[:, :], in0=ssum, scalar=0.0, in1=sneg, op0=ALU.is_gt,
                                   op1=ALU.subtract).then_inc(sem["sig_ready"], 1)
            with v.Fori(3, UNITS - 1) as t:
                unit(t)
            unit(UNITS - 1)
            v.wait_ge(sem["chan_w_loaded"], 7 * 16)
            unit(UNITS, 0)
            unit(UNITS + 1, 1)

            v.wait_ge(sem["x2_ready"], NT)

            for m in range(MAXG):
                reduce_max(0, m)

            ln3_stats(2)
            ln3_apply(2)

            def slot(s):
                for k in range(GRANULES):
                    if k == 0:
                        if live(s - 2):
                            v.wait_ge(sem["x3_ready"], s - 1)
                        if live(s + 2):
                            rope_part(s + 2, 0, "rope_q", "qproj_psum")
                        if live(s - 2):
                            ln4_stats(s - 2)
                    if k == 1 and live(s - 3):
                        route_scores(s - 3)
                    if k == 2:
                        if live(s + 2):
                            rope_part(s + 2, 1, "rope_k", "kproj_psum")
                        if live(s - 3):
                            route_pick(s - 3)
                    if k == 3:
                        if live(s - 2):
                            ln4_apply(s - 2)
                        if live(s - 3):
                            route_slice(s - 3)
                    if k == 4 and live(s + 3):
                        ln3_stats(s + 3)
                    if k == 5 and live(s - 1):
                        normalize(s - 1)
                    if k == 6 and live(s - 2):
                        ln5_apply(s - 2)
                    if k == 7:
                        if live(s - 1):
                            residual(s - 1)
                        if live(s + 3):
                            ln3_apply(s + 3)
                    if live(s + 1):
                        reduce_max(s + 1, 2 * k)
                        reduce_max(s + 1, 2 * k + 1)

            for s in range(4):
                slot(s)
            with v.Fori(4, 13) as s:
                slot(s)
            for s in range(13, NT + 3):
                slot(s)

            links = [0]

            def link(ins):
                links[0] += 1
                ins.then_inc(sem["spline_step"], 1)
                v.wait_ge(sem["spline_step"], links[0])

            v.wait_ge(sem["slice_ready"], NT)
            v.wait_ge(sem["x4_ready"], NT)
            link(V.tensor_reduce(tmm[:, :, 0], xs[:, :, :], AX, ALU.min))
            link(V.tensor_reduce(tmm[:, :, 1], xs[:, :, :], AX, ALU.max))
            link(V.tensor_scalar(bigm, oh[:, :, :], -BIG, BIG, ALU.mult, ALU.add))
            for i, (name, op, edge) in enumerate((("min", ALU.min, ALU.add), ("max", ALU.max, ALU.subtract))):
                link(V.tensor_tensor(cand, oh[:, :, :], tmm[:, :, i:i + 1].to_broadcast([P, NT, NTILE]),
                                ALU.mult))
                link(V.tensor_tensor(cand, cand, bigm, edge))
                V.tensor_reduce(mpart[:, i, :], cand.rearrange("p n t -> p t n"), AX, op).then_inc(sem[name + "_part"], 1)
                v.wait_ge(sem[name + "_part"], 1)
            v.wait_ge(sem["mm_psum"], 1)
            V.tensor_reduce(table[:, 128:129], bankC[0:NTILE, 0:P], AX, ALU.min)
            V.tensor_reduce(table[:, 129:130], bankC[0:NTILE, P:2 * P], AX, ALU.max).then_inc(sem["mm_ready"], 1)
            v.wait_ge(sem["look_ready"], 6)
            mnb = look[:, :, 128:129].to_broadcast([P, NT, SLICE])
            link(V.tensor_tensor(u0[:, :, :], xs[:, :, :], mnb, ALU.subtract))
            link(V.tensor_tensor(span[:, 0, :], look[:, :, 129], look[:, :, 128], ALU.subtract))
            link(V.tensor_scalar(span[:, 1, :], span[:, 0, :], 1e-8, None, ALU.add))
            link(V.reciprocal(span[:, 2, :], span[:, 1, :]))
            link(V.tensor_tensor(u1[:, :, :], u0[:, :, :], span[:, 2, :].unsqueeze(2).to_broadcast([P, NT, SLICE]),
                            ALU.mult))
            link(V.tensor_scalar(u2[:, :, :], u1[:, :, :], 0.0, 1.0 - 1e-6, ALU.max, ALU.min))
            link(V.tensor_scalar(u3[:, :, :], u2[:, :, :], float(GRID), None, ALU.mult))
            link(V.tensor_scalar(u4[:, :, :], u3[:, :, :], MAGIC, None, ALU.add))
            link(V.tensor_scalar(u5[:, :, :], u4[:, :, :], MAGIC, None, ALU.subtract))
            link(V.tensor_tensor(u0[:, :, :], u5[:, :, :], u3[:, :, :], ALU.is_gt))
            link(V.tensor_tensor(u1[:, :, :], u5[:, :, :], u0[:, :, :], ALU.subtract))
            link(V.tensor_scalar(u2[:, :, :], u1[:, :, :], 0.0, float(GRID - 1), ALU.max, ALU.min))
            link(V.tensor_tensor(u4[:, :, :], u3[:, :, :], u2[:, :, :], ALU.subtract))
            u2m = u2[:, :, :].rearrange("p n j -> p (n j)")
            link(V.tensor_tensor(gmask.rearrange("p (m g) -> p m g", g=GRID),
                            giota[:, :].unsqueeze(1).to_broadcast([P, NT * SLICE, GRID]),
                            u2m.unsqueeze(2).to_broadcast([P, NT * SLICE, GRID]),
                            ALU.is_equal))
            for i, (name, dst) in enumerate((("base", bsel), ("slope", ssel))):
                link(V.tensor_tensor(gprod.rearrange("p (n c) -> p n c", n=NT), gmask.rearrange("p (n c) -> p n c", n=NT),
                                look[:, :, 64 * i:64 * i + 64], ALU.mult))
                link(V.tensor_reduce(dst[:, :, :].rearrange("p n j -> p (n j)"), gprod.rearrange("p (m g) -> p m g", g=GRID),
                                AX, ALU.add))
            link(V.tensor_tensor(u5[:, :, :], ssel[:, :, :], u4[:, :, :], ALU.mult))
            link(V.tensor_tensor(u3[:, :, :], u5[:, :, :], bsel[:, :, :], ALU.add))
            V.tensor_tensor(delta[:, :, :], u3[:, :, :], look[:, :, 130:131].to_broadcast([P, NT, SLICE]),
                            ALU.mult).then_inc(sem["delta_ready"], 1)
            v.wait_ge(sem["delta_ready"], 1)
            for i, q in enumerate((0, 2)):
                for n in range(4 * q, 4 * q + 4):
                    last = V.tensor_tensor(outb[:, n, :].rearrange("p (t j) -> p t j", j=SLICE),
                                           oh[:, n, :].unsqueeze(2).to_broadcast([P, NTILE, SLICE]),
                                           delta[:, n, :].unsqueeze(1).to_broadcast([P, NTILE, SLICE]), ALU.mult)
                last.then_inc(sem["place_dve"], 1)
                v.wait_ge(sem["place_dve"], i + 1)
                V.tensor_tensor(outb[:, 4 * q:4 * q + 4, :], outb[:, 4 * q:4 * q + 4, :], xall[:, 4 * q:4 * q + 4, :],
                                ALU.add).then_inc(sem["out_dve"], 1)


def kernel(**inputs):
    import numpy as np
    import concourse.bacc as bacc
    from concourse.bass_utils import run_bass_kernel_spmd

    a = {k: np.asarray(v) for k, v in inputs.items()}
    f = np.float32

    def turned(w):
        return np.ascontiguousarray(w.T)

    def twice(w):
        z = np.zeros((2 * w.shape[0], 2 * w.shape[1]), f)
        z[:w.shape[0], :w.shape[1]] = w
        z[w.shape[0]:, w.shape[1]:] = w
        return z

    order = [(b, (2 * g + par) * HC + c) for par in range(2) for c in range(HC) for b in range(2) for g in range(PAIRS)]
    rolled = [(b, o // HC * HC + (o % HC + HC // 2) % HC) for b, o in order]
    cols = np.array([b * 64 + o for b, o in order])
    colr = np.array([b * 64 + o for b, o in rolled])

    def stacked(w):
        z = twice(turned(w))
        return np.ascontiguousarray(np.stack([z[:, cols], z[:, colr]], 1))

    def both(v):
        return np.concatenate([v, v])

    bq, bk = both(a["L1_xattn_bq"]), both(a["L1_xattn_bk"])
    bias = np.stack([bq[cols], bq[colr], bk[cols], bk[colr], both(a["L1_xattn_bv"]), both(a["L1_xattn_bo"])], 1)
    inv_freq = f(1.0) / f(10000.0) ** (np.arange(0, HC, 2, dtype=f) / f(HC))
    angle = np.arange(D, dtype=f)[:, None] * inv_freq[None, :]
    ch = np.array([o % HC for _, o in order])
    cos = np.cos(angle)[:, ch % 4].T
    sin = np.sin(angle)[:, ch % 4].T * np.where(ch < HC // 2, f(-1), f(1))[:, None]
    n = np.arange(NTILE)
    ctx = a["ctx_2048"]
    arrays = {
        "x": a["x"], "ctx": ctx,
        "ctxT": np.ascontiguousarray(ctx.reshape(UNITS, 2, 2 * S, D).transpose(3, 0, 1, 2)),
        "wq": turned(a["L0_xattn_wq"]), "wk": turned(a["L0_xattn_wk"]),
        "wv": turned(a["L0_xattn_wv"]), "wo": turned(a["L0_xattn_wo"]),
        "wg": turned(a["L0_ffn_w_gate"]), "wu": np.ascontiguousarray(turned(a["L0_ffn_w_up"]).reshape(16, 16, FF).swapaxes(0, 1)).reshape(D, FF), "wd": turned(a["L0_ffn_w_down"]),
        "wqb": stacked(a["L1_xattn_Wq"]), "wkb": stacked(a["L1_xattn_Wk"]),
        "wvb": twice(turned(a["L1_xattn_Wv"])), "wob": twice(turned(a["L1_xattn_Wo"])),
        "bias": bias, "cos": np.ascontiguousarray(cos, f), "sin": np.ascontiguousarray(sin, f),
        "gamma": a["L1_ffn_ln_gamma"][None, :], "beta": a["L1_ffn_ln_beta"][None, :],
        "bases": a["L1_ffn_spline_bases"].reshape(NTILE, 64), "slopes": a["L1_ffn_spline_slopes"].reshape(NTILE, 64),
        "slopes_row": a["L1_ffn_spline_slopes"].reshape(1, NTILE * 64),
        "oscale": a["L1_ffn_output_scale"][:, None],
        "ident": np.eye(P, dtype=f),
        "ckey": (-(n // 8) * 128 - n % 8).astype(f)[None, :], "giota": np.arange(GRID, dtype=f)[None, :],
    }
    nc = bacc.Bacc("TRN2", target_bir_lowering=False, num_devices=1)
    feed, A = {}, {}
    for name, v in arrays.items():
        v = np.ascontiguousarray(v)
        feed["in_" + name] = v
        A[name] = nc.dram_tensor("in_" + name, v.shape, mybir.dt.from_np(v.dtype), kind="ExternalInput").ap()
    out = nc.dram_tensor("out_x", (B, S, D), F32, kind="ExternalOutput").ap()
    decoder_kernel(nc, A, out)
    r = run_bass_kernel_spmd(nc, [feed], core_ids=[0])
    return r.results[0]["out_x"]
```

```python
from contextlib import ExitStack

import concourse.bass as bass
from concourse import mybir

F32 = mybir.dt.float32
BF16 = mybir.dt.bfloat16
ALU = mybir.AluOpType
ACT = mybir.ActivationFunctionType
AX = mybir.AxisListType.X

P = 128
B, S, D = 32, 64, 256
NT = B * S // P
DC = D // P
UNITS = NT // 2
FF = 832
FH = FF // 2
FK, FP = 8, FF // 8
HEADS, HC = 8, 8
PAIRS = HEADS // 2
NTILE, SLICE, GRID, CLUSTERS = 64, 4, 16, 8
LN_EPS = 1e-5
Q_EPS = 1e-5
MAGIC = 12582912.0
BIG = 3.0e38
NBUF = 3
GRANULES = 8
ROW = 2 * SLICE * GRID + 3
EARLY = NT - 2
OUT_DVE, OUT_POOL = ((0, 4), (4, 8), (8, 10)), ((10, 13), (13, 16))
MAXG = 16
SPREADS = 14
LAG = 3

SEMS = """
x0_loaded x_loaded attn_w_loaded wo_loaded chan_w_loaded ffn_w_loaded ident_loaded ctxT_loaded ctxV_loaded ffn2_loaded
const_ready ident_ready ones_row_placed oz_ready
wsum_ready wtot_ready wmean_ready winv_ready w_clip w_round w_ready
bo_sum_ready bo_ready
ln1_steps ln1_var ln1_rstd xn_ready
xT_psum xT_ready q_psum q_ready k_psum k_ready v_psum v_ready
s_psum s_max nmax_ready probs_ready pT_psum pT_ready rsum_ready oT_psum oT_ready y_psum x1_ready
ln2_steps ln2_var ln2_rstd xn2_ready amax_ready amaxc_ready arec_ready ascale_ready
a_round xq_ready act_scale2 act_scale3
xqT_psum xqT_ready xh_ready xhT_psum xhT_ready gateup_psum gate_ready up_ready
h_half h_ready hamax_ready hamaxc_ready hrec_ready hscale_ready h_round hq_ready dscale_ready
hT_psum hT_ready down_psum x2_ready
ln3_steps ln3_var ln3_rstd xn3_ready
qproj_psum kproj_psum vproj_psum rope_q rope_k qk_sum part1 rest1 part2 parts_ready
parts_stored vz_ready
max_psum max_ready maxT_psum maxT_ready maxrow_done
sT_psum exp_ready av_psum den_inv o_ready yc_psum x3_ready
ln4_steps ln4_var ln4_rstd xn4_ready
ln5_steps ln5_var ln5_rstd xn5_ready gamma_done xf_ready
sgn_prod sgn_neg sgn_ready tile_score clus_score key_c key_ready key_max onehot_ready
xf_masked x4_ready slice_ready
mask_ready slope_picked slope_sum slope_neg sig_ready
max_part
spline_step mm_psum mm_ready mmt_psum ohT_psum ohT_ready look_psum look_ready

delta_ready place_dve place_pool out_pool out_dve out_stored
""".split()


def decoder_kernel(nc, A, out):
    with ExitStack() as ctx:
        def sb(name, shape, dt=F32):
            return ctx.enter_context(nc.sbuf_tensor(name, shape, dt))

        sem = {name: ctx.enter_context(nc.semaphore(name)) for name in SEMS}
        ctx_loaded = [ctx.enter_context(nc.semaphore(f"ctx_loaded{i}")) for i in range(NBUF)]
        spread_done = [ctx.enter_context(nc.semaphore(f"spread_done{i}")) for i in range(NBUF)]

        def tile(turn, off):
            return turn * NBUF + off, off % NBUF, turn + off // NBUF

        def live(t):
            return not isinstance(t, int) or 0 <= t < NT

        def proj_bank(t):
            return (bankA, bankC)[t] if isinstance(t, int) and t < 2 else MISC

        def on(t):
            return not isinstance(t, int) or 0 <= t < UNITS

        xall = sb("xall", [P, NT, D])
        ident = sb("ident", [P, P])
        identb = sb("identb", [P, P], BF16)
        ones = sb("ones", [P, P])
        halfneg = sb("halfneg", [P, 2])
        wattn = sb("wattn", [P, 4 * DC * D])
        wqT, wkT, wvT, woT = (wattn[:, i * DC * D:(i + 1) * DC * D].rearrange("p (c d) -> p c d", c=DC) for i in range(4))
        PB = sb("PB", [P, GRANULES, 4 * D])
        pbf = PB[:, :, :].rearrange("p g n -> p (g n)")
        slopes = pbf[:, 0:D * GRID].rearrange("p (d g) -> p d g", g=GRID)
        wffn = pbf[:, 4096:4096 + 2 * DC * FF].rearrange("p (a n) -> p a n", a=2)
        lookf = sb("lookf", [P, NT * (ROW - 2)])
        look = lookf[:, :].rearrange("p (n c) -> p n c", n=NT)
        wdn = lookf[0:FP, 0:FK * D]
        outf = sb("outf", [P, NT * D])
        outb = outf[:, :].rearrange("p (n d) -> p n d", n=NT)
        wgT = sb("wgT", [P, DC, FF], BF16)
        wuT = wffn[:, 1, :].rearrange("p (c f) -> p c f", c=DC)
        wdT = sb("wdT", [FP, FK, D], BF16)
        wsum = sb("wsum", [P, 4])
        wmean = sb("wmean", [P, 4])
        winv = sb("winv", [P, 4])
        wm127 = sb("wm127", [P, 4])
        st1 = sb("st1", [P, 2, 6])
        mv1 = sb("mv1", [P, 2, 2])
        ve1 = sb("ve1", [P, 2])
        rs1 = sb("rs1", [P, 2])
        xn = sb("xn", [P, 2, D])
        xnT = sb("xnT", [P, DC, 2 * P])
        qT = sb("qT", [P, DC, 2 * P])
        kT = sb("kT", [P, DC, 2, 4 * S])
        vb = sb("vb", [P, 2, 2, D])
        nmax = sb("nmax", [P, 2])
        nmaxs = sb("nmaxs", [P, 2])
        probs = sb("probs", [P, 2, P])
        psums = sb("psums", [P, 2])
        pinv = sb("pinv", [P, 2])
        pT = sb("pT", [P, 2, P])
        oT = sb("oT", [P, DC, 2 * P])
        st2 = sb("st2", [P, 2, 6])
        mv2 = sb("mv2", [P, 2, 2])
        ve2 = sb("ve2", [P, 2])
        rs2 = sb("rs2", [P, 2])
        hold = sb("hold", [P, 2])
        hold2 = sb("hold2", [P, 2])
        xn2 = sb("xn2", [P, 2, D])
        amax = sb("amax", [P, 2])
        amaxc = sb("amaxc", [P, 2])
        arec = sb("arec", [P, 2])
        ascale = sb("ascale", [P, 2])
        xq = sb("xq", [P, 2, D], BF16)
        xh = sb("xh", [P, 2, D])
        xhT = sb("xhT", [P, DC, 2 * P])
        ainv = sb("ainv", [P, 2])
        aGh = sb("aGh", [P, 2])
        xqT = sb("xqT", [P, DC, 2 * P], BF16)
        th = outf[:, 0 * FF:1 * FF]
        us = outf[:, 1 * FF:2 * FF]
        h1 = outf[:, 2 * FF:3 * FF]
        h2 = outf[:, 3 * FF:4 * FF]
        hm = sb("hm", [P, 4])
        hq = sb("hq", [P, FF], BF16)
        bD = sb("bD", [P, 2])
        hqT = sb("hqT", [FP, FK, P], BF16)
        wqb = sb("wqb", [P, 2, P])
        wkb = sb("wkb", [P, 2, P])
        wvb = sb("wvb", [P, P])
        wob = sb("wob", [P, P])
        bias = sb("bias", [P, 8])
        boe = sb("boe", [P, 1])
        cos = sb("cos", [P, D])
        sin = sb("sin", [P, D])
        cst = [sb(f"cst{i}", [P, D]) for i in range(NBUF)]
        st3 = sb("st3", [P, 6])
        mv3 = sb("mv3", [P, 2])
        ve3 = sb("ve3", [P, 1])
        rs3 = sb("rs3", [P, 1])
        xn3 = sb("xn3", [P, D])
        rope = wattn[:, 0:4 * D].rearrange("p (a i d) -> p a i d", a=2, i=2)
        qk = wattn[:, 4 * D:6 * D].rearrange("p (a d) -> p a d", a=2)
        qkr = wattn[:, 6 * D:8 * D].rearrange("p (a d) -> p a d", a=2)
        parts = sb("parts", [P, 2, 3, D], BF16)
        QS = [sb(f"QS{i}", [P, 2, 2, PAIRS, D], BF16) for i in range(NBUF)]
        KS = [sb(f"KS{i}", [P, 2, PAIRS, D], BF16) for i in range(NBUF)]
        VZ = [sb(f"VZ{i}", [P, 8, 160]) for i in range(NBUF)]
        OZ = sb("OZ", [P, 160])
        rows = sb("rows", [33, 2 * PAIRS * D], BF16)
        row1, row0 = rows[0:1, :], rows[32:33, :]
        mx = lookf[:, 0:NT * 16].bitcast(BF16).rearrange("p (n t c) -> p n t c", n=NT, t=2)
        mxT = sb("mxT", [16, D], BF16)
        dinv = sb("dinv", [P, D])
        ob = sb("ob", [P, D])
        gam = sb("gam", [P, D])
        bet = sb("bet", [P, D])
        ssum = pbf[:, 7424:7424 + D]
        sneg = pbf[:, 7424 + D:7424 + 2 * D]
        sig = sb("sig", [P, D])
        ckey = sb("ckey", [P, NTILE])
        giota = sb("giota", [P, GRID])
        table = sb("table", [NTILE, ROW])
        st4 = sb("st4", [P, 6])
        mv4 = sb("mv4", [P, 2])
        ve4 = sb("ve4", [P, 2])
        rs4 = sb("rs4", [P, 2])
        st5 = sb("st5", [P, 6])
        mv5 = sb("mv5", [P, 2])
        kTf = kT[:, :, :, :].rearrange("p c j n -> p (c j n)")
        xn4, xn5, xf, wk1 = (kTf[:, i * D:(i + 1) * D] for i in range(4))
        wk2 = sb("wk2", [P, D])
        wk3 = sb("wk3", [P, D])
        tsc = sb("tsc", [P, NTILE])
        csc = sb("csc", [P, CLUSTERS])
        key1 = sb("key1", [P, NTILE])
        key2 = sb("key2", [P, NTILE])
        kmax = sb("kmax", [P, 1])
        oh = vb[:, :, :, :].rearrange("p a b (c t) -> p (a b c) t", t=NTILE)
        xs = sb("xs", [P, NT, SLICE])
        tmm = sb("tmm", [P, NT, 2])
        bigm, low, high = (outf[:, i * 1024:(i + 1) * 1024].rearrange("p (n t) -> p n t", n=NT) for i in range(3))
        edge = outf[:, 3072:3072 + 6 * NTILE].rearrange("p (i a t) -> p i a t", i=2, a=3)
        mpart = outf[:, 3584:3584 + 2 * NTILE].rearrange("p (a t) -> p a t", a=2)
        ohT = wattn[0:NTILE, :].rearrange("p (n t) -> p n t", n=NT)
        gmask = pbf[:, 0:1024]
        gprod = [pbf[:, 1024 * (i + 1):1024 * (i + 2)] for i in range(2)]
        mmt = sb("mmt", [P, NT, 2])
        u0, u1, u2, u3, u4, u5 = [sb(f"u{i}", [P, NT, SLICE]) for i in range(6)]
        span = sb("span", [P, 4, NT])
        bsel = sb("bsel", [P, NT, SLICE])
        ssel = sb("ssel", [P, NT, SLICE])
        delta = sb("delta", [P, NT, SLICE])

        bk = [ctx.enter_context(nc.psum_tensor(f"bank{i}", [P, 512], F32)) for i in range(4)]
        big = ctx.enter_context(nc.psum_tensor("big", [P, 4, 512], F32))
        bankA, bankB, bankC, bankD = bk
        G = big[:, 0:2, 0:FH]
        U = big[:, 2:4, 0:FH]
        bankDb = bankD[:, :].bitcast(BF16)
        EX = [big[:, 2 * i:2 * i + 2, :].rearrange("p s n -> p (s n)") for i in range(2)]
        MXB = [bankA, bankB]
        AV = bankC
        MISC = bankD

        def place(engine, n0, n1):
            n = n1 - n0
            return engine.tensor_tensor(outb[:, n0:n1, :].rearrange("p n (t j) -> p n t j", j=SLICE),
                                        oh[:, n0:n1, :].unsqueeze(3).to_broadcast([P, n, NTILE, SLICE]),
                                        delta[:, n0:n1, :].unsqueeze(2).to_broadcast([P, n, NTILE, SLICE]), ALU.mult)

        scr = [nc.dram_tensor(f"scr{i}", [6, P, D], BF16).ap() for i in range(NBUF)]

        block = ctx.enter_context(nc.Block())

        @block.sync
        def _(sp):
            sp.dma_start(ident[:, :], A["ident"]).then_inc(sem["ident_loaded"], 16)
            xin = A["x"].rearrange("(n two) s d -> (two s) n d", two=2)
            sp.dma_start(xall[:, 0:2, :], xin[:, 0:2, :]).then_inc(sem["x0_loaded"], 16)
            for dst, name in ((wqT, "wq"), (wkT, "wk"), (wvT, "wv")):
                sp.dma_start(dst[:, :, :], A[name].rearrange("(c p) e -> p c e", p=P)).then_inc(sem["attn_w_loaded"], 16)

            sp.dma_start(xall[:, 2:6, :], xin[:, 2:6, :]).then_inc(sem["x_loaded"], 16)
            sp.dma_start(woT[:, :, :], A["wo"].rearrange("(c p) e -> p c e", p=P)).then_inc(sem["wo_loaded"], 16)
            for i, name in enumerate(("wg", "wu")):
                sp.dma_start(wffn[:, i, :].rearrange("p (c f) -> p c f", c=DC),
                             A[name].rearrange("(c p) f -> p c f", p=P)).then_inc(sem["ffn_w_loaded"], 16)
            sp.dma_start(wdn.rearrange("p (k d) -> p k d", k=FK),
                         A["wd"].rearrange("(k p) d -> p k d", p=FP)).then_inc(sem["ffn_w_loaded"], 16)
            sp.dma_start(xall[:, 6:NT, :], xin[:, 6:NT, :]).then_inc(sem["x_loaded"], 16)
            for dst, name in ((wqb[:, :, :], "wqb"), (wkb[:, :, :], "wkb"), (wvb[:, :], "wvb"),
                              (wob[:, :], "wob"), (bias[:, 0:6], "bias"), (cos[:, :], "cos"), (sin[:, :], "sin")):
                sp.dma_start(dst, A[name]).then_inc(sem["chan_w_loaded"], 16)
            sp.dma_start(gam[:, :], A["gamma"].to_broadcast([P, D])).then_inc(sem["ffn2_loaded"], 16)
            sp.dma_start(bet[:, :], A["beta"].to_broadcast([P, D])).then_inc(sem["ffn2_loaded"], 16)
            sp.dma_start(pbf[:, 0:D * GRID],
                         A["slopes_row"].to_broadcast([P, D * GRID])).then_inc(sem["ffn2_loaded"], 16)
            sp.dma_start(table[:, 0:64], A["bases"]).then_inc(sem["ffn2_loaded"], 16)
            sp.dma_start(table[:, 64:128], A["slopes"]).then_inc(sem["ffn2_loaded"], 16)
            sp.dma_start(table[:, 128:129], A["oscale"]).then_inc(sem["ffn2_loaded"], 16)
            sp.dma_start(ckey[:, :], A["ckey"].to_broadcast([P, NTILE])).then_inc(sem["ffn2_loaded"], 16)
            sp.dma_start(giota[:, :], A["giota"].to_broadcast([P, GRID])).then_inc(sem["ffn2_loaded"], 16)
            sp.wait_ge(sem["const_ready"], 3)
            for i in range(NBUF):
                for par in range(2):
                    r = 64 * par + 48
                    sp.dma_start(KS[i][r:r + 1, :, :, :].rearrange("p b k t -> p (b k t)"),
                                 row1).then_inc(sem["ones_row_placed"], 16)
            def spread(t, u, w):
                sv = scr[u].rearrange("(a r) (par c g) t -> a par r c (g t)", a=2, par=2, c=HC)
                for a in range(2):
                    n = t * 2 + a
                    sp.wait_ge(sem["parts_ready"], n + 1)
                    sp.dma_start(scr[u][3 * a:3 * a + 3].rearrange("r p t -> p r t"),
                                 parts[:, a, :, :]).then_inc(sem["parts_stored"], 16)
                    if a == 0:
                        if not (isinstance(t, int) and t < NBUF):
                            sp.wait_ge(sem["sT_psum"], (t - (NBUF - 1)) * GRANULES)
                        for par in range(2):
                            r = 64 * par + 48
                            sp.dma_start(QS[u][r:r + 1, par, :, :, :].rearrange("p b k t -> p (b k t)"),
                                         row0).then_inc(spread_done[u], 16)
                    sp.wait_ge(sem["parts_stored"], (n + 1) * 16)
                    for par in range(2):
                        q0 = 64 * par
                        for at, m, piece in ((0, 3, 0), (3, 2, 1), (5, 1, 2)):
                            rows = slice(q0 + 8 * at, q0 + 8 * (at + m))
                            if a == 0:
                                sp.dma_start(QS[u][rows, par, :, :, :].rearrange("p b k t -> p (b k t)"),
                                             sv[0, par, 0:m, :, :]).then_inc(spread_done[u], 16)
                            else:
                                sp.dma_start(KS[u][rows, :, :, :].rearrange("p b k t -> p (b k t)"),
                                             sv[1, par, piece:piece + 1, :, :].to_broadcast([m, HC, 2048])
                                             ).then_inc(spread_done[u], 16)

            def max_rows(t, u, w):
                sp.wait_ge(sem["maxT_ready"], t + 1)
                for par in range(2):
                    r = 64 * par + 48
                    sp.dma_start(QS[u][r:r + 1, par, :, :, :].rearrange("p b k t -> p (b k t)"),
                                 mxT[8 * par:8 * par + 8, :]).then_inc(sem["maxrow_done"], 16)

            spread(*tile(0, 0))
            spread(*tile(0, 1))

            def slot(turn, off):
                if live(tile(turn, off)[0]):
                    max_rows(*tile(turn, off))
                if live(tile(turn, off + 2)[0]):
                    spread(*tile(turn, off + 2))

            for s in range(4):
                slot(0, s)
            with sp.Fori(1, 4) as i:
                for r in range(1, 4):
                    slot(i, r)
            for s in range(13, NT):
                slot(0, s)
            ov = out.rearrange("(n two) s d -> (two s) n d", two=2)
            for i in range(3):
                for name, pieces in (("out_dve", OUT_DVE), ("out_pool", OUT_POOL)):
                    if i < len(pieces):
                        n0, n1 = pieces[i]
                        sp.wait_ge(sem[name], i + 1)
                        sp.dma_start(ov[:, n0:n1, :], outb[:, n0:n1, :]).then_inc(sem["out_stored"], 16)
            sp.wait_ge(sem["out_stored"], 5 * 16)

        @block.gpsimd
        def _(pool):
            nc.gpsimd.memset(row1, 1.0).then_inc(sem["const_ready"], 1)
            nc.gpsimd.memset(row0, 0.0).then_inc(sem["const_ready"], 1)
            pool.wait_ge(sem["const_ready"], 2)
            def rstd(name, ve, rs, t):
                pool.wait_ge(sem[name + "_var"], t + 1)
                w = ve.shape[1]
                nc.gpsimd.tensor_tensor(rs, ve, halfneg[:, 0:w], ALU.pow).then_inc(sem[name + "_rstd"], 1)

            pool.wait_ge(sem["ident_ready"], 1)
            rstd("ln1", ve1[:, :], rs1[:, :], 0)
            rstd("ln1", ve1[:, :], rs1[:, :], 1)
            def split(t, a):
                n = t * 2 + a
                pool.wait_ge(sem["rope_k" if a else "rope_q"], t + 1)
                nc.gpsimd.tensor_tensor(qk[:, a, :], rope[:, a, 0, :], rope[:, a, 1, :], ALU.add).then_inc(sem["qk_sum"], 1)
                pool.wait_ge(sem["qk_sum"], n + 1)
                if not (isinstance(t, int) and t == 0):
                    pool.wait_ge(sem["parts_stored"], (n - 1) * 16)
                nc.gpsimd.tensor_tensor(hold2[:, 0:1], halfneg[:, 0:1], halfneg[:, 1:2], ALU.add)
                nc.gpsimd.tensor_scalar(parts[:, a, 0, :], qk[:, a, :], 1.0, None, ALU.mult).then_inc(sem["part1"], 1)
                pool.wait_ge(sem["part1"], n + 1)
                nc.gpsimd.tensor_tensor(qkr[:, a, :], qk[:, a, :], parts[:, a, 0, :], ALU.subtract).then_inc(sem["rest1"], 1)
                pool.wait_ge(sem["rest1"], n + 1)
                nc.gpsimd.tensor_tensor(hold2[:, 1:2], halfneg[:, 0:1], halfneg[:, 1:2], ALU.add)
                nc.gpsimd.tensor_scalar(parts[:, a, 1, :], qkr[:, a, :], 1.0, None, ALU.mult).then_inc(sem["part2"], 1)
                pool.wait_ge(sem["part2"], n + 1)
                nc.gpsimd.tensor_tensor(parts[:, a, 2, :], qkr[:, a, :], parts[:, a, 1, :],
                                        ALU.subtract).then_inc(sem["parts_ready"], 1)

            def affine(t):
                pool.wait_ge(sem["xn5_ready"], t + 1)
                nc.gpsimd.tensor_tensor(wk3[:, :], xn5, gam[:, :], ALU.mult).then_inc(sem["gamma_done"], 1)
                pool.wait_ge(sem["gamma_done"], t + 1)
                if not (isinstance(t, int) and t == 0):
                    pool.wait_ge(sem["xf_masked"], t)
                nc.gpsimd.tensor_tensor(xf, wk3[:, :], bet[:, :], ALU.add).then_inc(sem["xf_ready"], 1)
                pool.wait_ge(sem["xf_ready"], t + 1)
                nc.gpsimd.tensor_tensor(wk1, xf, sig[:, :], ALU.mult).then_inc(sem["sgn_prod"], 1)
                nc.gpsimd.tensor_tensor(xall[:, t, :], xall[:, t, :], xn4, ALU.add).then_inc(sem["x4_ready"], 1)

            def unit(t):
                if on(t - 1):
                    rstd("ln2", ve2[:, :], rs2[:, :], t - 1)
                if on(t + 1):
                    rstd("ln1", ve1[:, :], rs1[:, :], t + 1)

            for i in range(NBUF):
                nc.gpsimd.memset(QS[i][:, :, :, :, :], 0.0)
                nc.gpsimd.memset(VZ[i][:, :, :], 0.0)
                last = nc.gpsimd.memset(KS[i][:, :, :, :], 0.0)
                if i < 2:
                    unit(i + 1)
            last.then_inc(sem["const_ready"], 1)
            with pool.Fori(3, UNITS - 1) as t:
                unit(t)
            unit(UNITS - 1)
            unit(UNITS)

            rstd("ln3", ve3[:, :], rs3[:, :], 0)
            split(0, 0)
            split(0, 1)
            rstd("ln3", ve3[:, :], rs3[:, :], 1)
            split(1, 0)
            split(1, 1)
            pool.wait_ge(sem["ffn2_loaded"], 8 * 16)
            pool.wait_ge(sem["sig_ready"], 1)

            rstd("ln3", ve3[:, :], rs3[:, :], 2)

            def slot(s):
                if live(s + 2):
                    split(s + 2, 0)
                if live(s - 2):
                    rstd("ln4", ve4[:, 0:1], rs4[:, 0:1], s - 2)
                if live(s + 2):
                    split(s + 2, 1)
                if live(s - 2):
                    rstd("ln5", ve4[:, 1:2], rs4[:, 1:2], s - 2)
                if live(s + 3):
                    rstd("ln3", ve3[:, :], rs3[:, :], s + 3)
                if live(s - 2):
                    affine(s - 2)

            for s in range(4):
                slot(s)
            with pool.Fori(4, 13) as s:
                slot(s)
            for s in range(13, NT + 2):
                slot(s)
            pool.wait_ge(sem["look_ready"], 6)
            pool.wait_ge(sem["mask_ready"], 1)
            nc.gpsimd.tensor_tensor(gprod[1].rearrange("p (n c) -> p n c", n=NT),
                                    gmask.rearrange("p (n c) -> p n c", n=NT),
                                    look[:, :, 64:128], ALU.mult).then_inc(sem["slope_picked"], 1)
            pool.wait_ge(sem["delta_ready"], 1)
            for i, (n0, n1) in enumerate(OUT_POOL):
                place(nc.gpsimd, n0, n1).then_inc(sem["place_pool"], 1)
                pool.wait_ge(sem["place_pool"], i + 1)
                nc.gpsimd.tensor_tensor(outb[:, n0:n1, :], outb[:, n0:n1, :],
                                        xall[:, n0:n1, :], ALU.add).then_inc(sem["out_pool"], 1)

        @block.scalar
        def _(act):
            def load_unit(t):
                if not (isinstance(t, int) and t == 0):
                    act.wait_ge(sem["s_psum"], t)
                act.dma_start(kT[:, 0, :, S:3 * S], A["ctxT"][0:P, t, :, :]).then_inc(sem["ctxT_loaded"], 16)
                act.dma_start(kT[:, 1, :, S:3 * S], A["ctxT"][P:D, t, :, :]).then_inc(sem["ctxT_loaded"], 16)
                if not (isinstance(t, int) and t == 0):
                    act.wait_ge(sem["oT_psum"], t)
                cv = A["ctx"].rearrange("(t j b) s d -> t b s j d", j=2, b=2)
                act.dma_start(vb[S:P, :, 0, :], cv[t, 0, :, :, :]).then_inc(sem["ctxV_loaded"], 16)
                act.dma_start(vb[0:S, :, 1, :], cv[t, 1, :, :, :]).then_inc(sem["ctxV_loaded"], 16)

            def a1_head(t):
                act.wait_ge(sem["xT_psum"], t + 1)
                nc.scalar.copy(xnT[:, :, :].rearrange("p c n -> p (c n)"), bankA[:, :]).then_inc(sem["xT_ready"], 1)

            def a1_qkv(t):
                act.wait_ge(sem["q_psum"], t + 1)
                nc.scalar.copy(qT[:, :, :].rearrange("p c n -> p (c n)"), bankA[:, :]).then_inc(sem["q_ready"], 1)
                act.wait_ge(sem["k_psum"], t + 1)
                nc.scalar.copy(kT[:, :, :, 0:S],
                               bankB[:, :].rearrange("p (c j n) -> p c j n", c=2, j=2)[:, :, :, 0:S])
                nc.scalar.copy(kT[:, :, :, 3 * S:4 * S],
                               bankB[:, :].rearrange("p (c j n) -> p c j n", c=2, j=2)[:, :, :, S:P]).then_inc(sem["k_ready"], 1)
                act.wait_ge(sem["v_psum"], t + 1)
                nc.scalar.copy(vb[0:S, :, 0, :], bankC[0:S, :].rearrange("p (j d) -> p j d", j=2))
                nc.scalar.copy(vb[S:P, :, 1, :], bankC[S:P, :].rearrange("p (j d) -> p j d", j=2)).then_inc(sem["v_ready"], 1)

            def a1_exp(t):
                act.wait_ge(sem["nmax_ready"], t + 1)
                for j in range(2):
                    last = nc.scalar.activation(probs[:, j, :], bankC[:, j * P:(j + 1) * P], ACT.Exp,
                                                bias=nmaxs[:, j:j + 1], scale=1.0 / 16.0, accum_out=psums[:, j:j + 1])
                last.then_inc(sem["probs_ready"], 1)

            def a1_pT(t):
                act.wait_ge(sem["pT_psum"], t + 1)
                nc.scalar.copy(pT[:, :, :].rearrange("p j n -> p (j n)"), bankC[:, 0:2 * P]).then_inc(sem["pT_ready"], 1)

            def a1_oT(t):
                act.wait_ge(sem["oT_psum"], t + 1)
                nc.scalar.copy(oT[:, :, :].rearrange("p c n -> p (c n)"), bankA[:, :]).then_inc(sem["oT_ready"], 1)

            def a2_xqT(t):
                act.wait_ge(sem["xqT_psum"], t + 1)
                nc.scalar.copy(xqT[:, :, :].rearrange("p c n -> p (c n)"), bankDb[:, 0:512]).then_inc(sem["xqT_ready"], 1)

            def a2_xhT(t):
                act.wait_ge(sem["xhT_psum"], t + 1)
                nc.scalar.copy(xhT[:, :, :].rearrange("p c n -> p (c n)"), bankC[:, :]).then_inc(sem["xhT_ready"], 1)

            def a2_silu(t, j):
                act.wait_ge(sem["act_scale3"], t + 1)
                act.wait_ge(sem["gateup_psum"], t * 2 + (j + 1))
                if not (isinstance(t, int) and t == 0 and j == 0):
                    act.wait_ge(sem["h_half"], t * 2 + j)
                nc.scalar.activation(th.rearrange("p (a n) -> p a n", a=2), G, ACT.Tanh,
                                     scale=aGh[:, j:j + 1]).then_inc(sem["gate_ready"], 1)
                nc.scalar.activation(us.rearrange("p (a n) -> p a n", a=2), U, ACT.Copy,
                                     scale=aGh[:, j:j + 1]).then_inc(sem["up_ready"], 1)

            def a2_hT(t, j):
                act.wait_ge(sem["hT_psum"], t * 2 + (j + 1))
                nc.scalar.copy(hqT[:, :, :].rearrange("p k n -> p (k n)"), bankDb[0:FP, :]).then_inc(sem["hT_ready"], 1)

            ctile = A["ctx"].rearrange("(n two) s d -> n (two s) d", two=2)

            def load_ctx(t, u, w):
                if not (isinstance(t, int) and t < NBUF):
                    act.wait_ge(sem["vproj_psum"], t - (NBUF - 1))
                act.dma_start(cst[u][:, :], ctile[t, :, :]).then_inc(ctx_loaded[u], 16)

            def v_out(t, u, w):
                act.wait_ge(sem["vproj_psum"], t + 1)
                if not (isinstance(t, int) and t < NBUF):
                    act.wait_ge(sem["av_psum"], (t - (NBUF - 1)) * 2)
                nc.scalar.copy(VZ[u][:, :, :].rearrange("p k (a b) -> p k a b", b=40)[:, :, :, 0:HC],
                               proj_bank(t)[:, 0:256].rearrange("p (k a c) -> p k a c", k=8, a=4)).then_inc(sem["vz_ready"], 1)

            def max_out(t):
                act.wait_ge(sem["maxT_psum"], t + 1)
                if not (isinstance(t, int) and t == 0):
                    act.wait_ge(sem["maxrow_done"], t * 32)
                nc.scalar.activation(mxT[:, :], MISC[0:16, 0:256], ACT.Copy, scale=-1.0).then_inc(sem["maxT_ready"], 1)

            def exp(t, u, w, k):
                act.wait_ge(sem["sT_psum"], t * GRANULES + (k + 1))
                if not (isinstance(t, int) and t == 0):
                    act.wait_ge(sem["av_psum"], t * 2 + (k // 4 - 1))
                nc.scalar.activation(PB[:, k, :], EX[k % 2], ACT.Exp, scale=float(HC) ** -0.5).then_inc(sem["exp_ready"], 1)

            def unit(t, b=None):
                if on(t):
                    a1_head(t)
                if on(t - 2):
                    a2_silu(t - 2, 0)
                if on(t):
                    a1_qkv(t)
                if on(t - 2):
                    a2_silu(t - 2, 1)
                if on(t):
                    a1_exp(t)
                if on(t - 2):
                    a2_hT(t - 2, 0)
                if on(t):
                    a1_pT(t)
                    a1_oT(t)
                if on(t - 1):
                    a2_xqT(t - 1)
                    a2_xhT(t - 1)
                if on(t - 2):
                    a2_hT(t - 2, 1)
                if b is not None:
                    v_out(*tile(0, b))
                if on(t + 1):
                    load_unit(t + 1)

            load_unit(0)
            for t in range(3):
                unit(t)
            with act.Fori(3, UNITS - 1) as t:
                unit(t)
            unit(UNITS - 1)
            for t in range(NBUF):
                load_ctx(t, t, 0)
            act.wait_ge(sem["const_ready"], 3)
            unit(UNITS, 0)
            unit(UNITS + 1, 1)

            def slot(turn, off):
                s = tile(turn, off)[0]
                for k in range(GRANULES):
                    if k == 1 and live(s):
                        max_out(s)
                    if k < LAG and live(s - 1):
                        exp(*tile(turn, off - 1), k + GRANULES - LAG)
                    if k >= LAG and live(s):
                        exp(*tile(turn, off), k - LAG)
                    if k == 3 and live(s + 3):
                        load_ctx(*tile(turn, off + 3))
                    if k == 4 and live(s + 2):
                        v_out(*tile(turn, off + 2))

            for s in range(4):
                slot(0, s)
            with act.Fori(1, 4) as i:
                for r in range(1, 4):
                    slot(i, r)
            for s in range(13, NT):
                slot(0, s)
            def oh_out(g):
                act.wait_ge(sem["ohT_psum"], g + 1)
                nc.scalar.copy(ohT[:, 4 * g:4 * g + 4, :].rearrange("p n t -> p (n t)"),
                               (bankA if g % 2 == 0 else bankB)[0:NTILE, :]).then_inc(sem["ohT_ready"], 1)

            def look_out(g):
                w = min(3, NT - 3 * g)
                act.wait_ge(sem["look_psum"], g + 1)
                nc.scalar.copy(look[:, 3 * g:3 * g + w, :].rearrange("p n c -> p (n c)"),
                               big[:, g % 4, 0:w * (ROW - 2)]).then_inc(sem["look_ready"], 1)

            for g in range(3):
                oh_out(g)
            slot(0, NT)
            for g in range(4):
                look_out(g)
            oh_out(3)
            look_out(4)
            look_out(5)

        @block.tensor
        def _(pe):
            mm = nc.tensor.matmul

            def a1_s1(t):
                pe.wait_ge(sem["xn_ready"], t + 1)
                if not (isinstance(t, int) and t == 0):
                    pe.wait_ge(sem["oT_ready"], t)
                for c in range(DC):
                    for j in range(2):
                        last = nc.tensor.transpose(bankA[:, c * 256 + j * P:c * 256 + (j + 1) * P],
                                                   xn[:, j, c * P:(c + 1) * P], ident[:, :])
                last.then_inc(sem["xT_psum"], 1)

            def a1_s2(t):
                pe.wait_ge(sem["xT_ready"], t + 1)
                pe.wait_ge(sem["attn_w_loaded"], 48)
                for e in range(DC):
                    for c in range(DC):
                        last = mm(bankA[:, e * 256:(e + 1) * 256], wqT[:, c, e * P:(e + 1) * P], xnT[:, c, :],
                                  start=c == 0, stop=c == DC - 1)
                last.then_inc(sem["q_psum"], 1)
                if not (isinstance(t, int) and t == 0):
                    pe.wait_ge(sem["x1_ready"], t)
                for e in range(DC):
                    for c in range(DC):
                        last = mm(bankB[:, e * 256:(e + 1) * 256], wkT[:, c, e * P:(e + 1) * P], xnT[:, c, :],
                                  start=c == 0, stop=c == DC - 1)
                last.then_inc(sem["k_psum"], 1)
                if not isinstance(t, int) or t > 1:
                    pe.wait_ge(sem["xhT_ready"], t - 1)
                elif t == 1:
                    pe.wait_ge(sem["pT_ready"], 1)
                for j in range(2):
                    for c in range(DC):
                        last = mm(bankC[:, j * 256:(j + 1) * 256], xnT[:, c, j * P:(j + 1) * P], wvT[:, c, :],
                                  start=c == 0, stop=c == DC - 1)
                last.then_inc(sem["v_psum"], 1)

            def a1_s3(t):
                pe.wait_ge(sem["q_ready"], t + 1)
                pe.wait_ge(sem["k_ready"], t + 1)
                pe.wait_ge(sem["v_ready"], t + 1)
                pe.wait_ge(sem["ctxT_loaded"], (t + 1) * 32)
                for j in range(2):
                    for b in range(2):
                        for c in range(DC):
                            last = mm(bankC[b * S:(b + 1) * S, j * P:(j + 1) * P],
                                      qT[:, c, j * P + b * S:j * P + (b + 1) * S], kT[:, c, j, b * P:(b + 1) * P],
                                      start=c == 0, stop=c == DC - 1)
                last.then_inc(sem["s_psum"], 1)

            def a1_s4(t):
                pe.wait_ge(sem["probs_ready"], t + 1)
                for j in range(2):
                    last = nc.tensor.transpose(bankC[:, j * P:(j + 1) * P], probs[:, j, :], ident[:, :])
                last.then_inc(sem["pT_psum"], 1)

            def a1_s5(t):
                pe.wait_ge(sem["pT_ready"], t + 1)
                pe.wait_ge(sem["ctxV_loaded"], (t + 1) * 32)
                for c in range(DC):
                    for j in range(2):
                        for b in range(2):
                            at = c * 256 + j * P + b * S
                            last = mm(bankA[:, at:at + S], vb[:, j, b, c * P:(c + 1) * P], pT[:, j, b * S:(b + 1) * S],
                                      start=True, stop=True)
                last.then_inc(sem["oT_psum"], 1)

            def a1_s6(t):
                pe.wait_ge(sem["oT_ready"], t + 1)
                pe.wait_ge(sem["wo_loaded"], 16)
                if not isinstance(t, int) or t > 1:
                    pe.wait_ge(sem["x2_ready"], t * 2 - 3)
                for j in range(2):
                    for c in range(DC):
                        last = mm(bankB[:, j * 256:(j + 1) * 256], oT[:, c, j * P:(j + 1) * P], woT[:, c, :],
                                  start=c == 0, stop=c == DC - 1)
                last.then_inc(sem["y_psum"], 1)

            def a2_r1(t):
                pe.wait_ge(sem["xq_ready"], t + 1)
                if not (isinstance(t, int) and t == 0):
                    pe.wait_ge(sem["hT_ready"], t * 2 - 1)
                for c in range(DC):
                    for j in range(2):
                        last = nc.tensor.transpose(bankDb[:, c * 256 + j * P:c * 256 + (j + 1) * P],
                                                   xq[:, j, c * P:(c + 1) * P], identb[:, :])
                last.then_inc(sem["xqT_psum"], 1)

            def a2_r1h(t):
                pe.wait_ge(sem["xh_ready"], t + 1)
                pe.wait_ge(sem["pT_ready"], t + 2 if on(t + 1) else UNITS)
                for c in range(DC):
                    for j in range(2):
                        last = nc.tensor.transpose(bankC[:, c * 256 + j * P:c * 256 + (j + 1) * P],
                                                   xh[:, j, c * P:(c + 1) * P], ident[:, :])
                last.then_inc(sem["xhT_psum"], 1)

            def a2_r2(t, j):
                pe.wait_ge(sem["xqT_ready"], t + 1)
                pe.wait_ge(sem["w_ready"], 3)
                if not (isinstance(t, int) and t == 0 and j == 0):
                    pe.wait_ge(sem["h_ready"], t * 2 + j)
                pe.wait_ge(sem["xhT_ready"], t + 1)
                for w, src, dst in ((wgT, xqT, G), (wuT, xhT, U)):
                    for f in range(2):
                        for c in range(DC):
                            last = mm(dst[:, f, :], src[:, c, j * P:(j + 1) * P], w[:, c, f * FH:(f + 1) * FH],
                                      start=c == 0, stop=c == DC - 1)
                last.then_inc(sem["gateup_psum"], 1)

            def a2_r4(t, j):
                pe.wait_ge(sem["hq_ready"], t * 2 + (j + 1))
                if j == 0:
                    pe.wait_ge(sem["xqT_ready"], t + 1)
                    if not (isinstance(t, int) and t == 0):
                        pe.wait_ge(sem["x2_ready"], t * 2)
                else:
                    pe.wait_ge(sem["hT_ready"], t * 2 + 1)
                    if on(t + 1):
                        pe.wait_ge(sem["xqT_ready"], t + 2)
                for k in range(FK):
                    last = nc.tensor.transpose(bankDb[0:FP, k * P:(k + 1) * P], hq[:, k * FP:(k + 1) * FP], identb[:, :])
                last.then_inc(sem["hT_psum"], 1)

            def a2_r5(t, j):
                pe.wait_ge(sem["hT_ready"], t * 2 + (j + 1))
                if j == 0:
                    if on(t + 2):
                        pe.wait_ge(sem["k_ready"], t + 3)
                    else:
                        pe.wait_ge(sem["x1_ready"], UNITS)
                        pe.wait_ge(sem["x2_ready"], t * 2 - 1)
                for k in range(FK):
                    last = mm((bankD if j else bankB)[:, 0:D], hqT[:, k, :], wdT[:, k, :], start=k == 0, stop=k == FK - 1)
                last.then_inc(sem["down_psum"], 1)

            pe.wait_ge(sem["ident_ready"], 1)
            a1_s1(0)
            a1_s2(0)
            a1_s3(0)
            a1_s4(0)
            a1_s5(0)
            a1_s6(0)
            pe.wait_ge(sem["wsum_ready"], 3)
            for i in range(3):
                n = P if i < 2 else FP
                last = mm(bankD[:, i:i + 1], ones[0:n, :], wsum[0:n, i:i + 1], start=True, stop=True)
            last.then_inc(sem["wtot_ready"], 1)
            pe.wait_ge(sem["wmean_ready"], 1)
            pe.wait_ge(sem["chan_w_loaded"], 7 * 16)
            mm(bankD[:, 8:9], wob[:, :], bias[:, 4:5], start=True, stop=True).then_inc(sem["bo_sum_ready"], 1)
            pe.wait_ge(sem["bo_ready"], 1)
            def proj_q(t):
                if isinstance(t, int) and t == 0:
                    pe.wait_ge(sem["oT_ready"], UNITS)
                if isinstance(t, int) and t == 1:
                    pe.wait_ge(sem["xhT_ready"], UNITS)
                pe.wait_ge(sem["xn3_ready"], t + 1)
                if not isinstance(t, int) or t > NBUF:
                    pe.wait_ge(sem["x3_ready"], t - NBUF)
                elif t > 0:
                    pe.wait_ge(sem["vz_ready"], t)
                for i in range(2):
                    last = mm(proj_bank(t)[:, i * D:(i + 1) * D], wqb[:, i, :], xn3[:, :], start=True, stop=True)
                last.then_inc(sem["qproj_psum"], 1)

            def proj_k(t, u, w):
                pe.wait_ge(sem["rope_q"], t + 1)
                if not isinstance(t, int) or t >= 2:
                    pe.wait_ge(sem["maxT_ready"], t - 1)
                pe.wait_ge(ctx_loaded[u], (w + 1) * 16)
                for i in range(2):
                    last = mm(proj_bank(t)[:, i * D:(i + 1) * D], wkb[:, i, :], cst[u][:, :], start=True, stop=True)
                last.then_inc(sem["kproj_psum"], 1)

            def proj_v(t, u, w):
                pe.wait_ge(sem["rope_k"], t + 1)
                for st in range(2):
                    last = mm(proj_bank(t)[:, st * P:(st + 1) * P], cst[u][:, st * P:(st + 1) * P], wvb[:, :],
                              start=True, stop=True)
                last.then_inc(sem["vproj_psum"], 1)

            def score_max(t, u, w, m, first=False):
                if m == 0:
                    pe.wait_ge(spread_done[u], (w + 1) * (16 * SPREADS))
                if not (first and m < 2):
                    pe.wait_ge(sem["max_ready"], t * MAXG + (m - 1))
                b, tt, pair = m // 8, m // 4 % 2, m % 4
                for par in range(2):
                    last = mm(MXB[m % 2][:, par * D:(par + 1) * D], QS[u][:, par, b, pair, tt * P:(tt + 1) * P],
                              KS[u][:, b, pair, :], start=True, stop=True)
                last.then_inc(sem["max_psum"], 1)

            def max_turn(t):
                pe.wait_ge(sem["max_ready"], (t + 1) * MAXG)
                if live(t + 2):
                    pe.wait_ge(sem["rope_q"], t + 3)
                else:
                    pe.wait_ge(sem["x3_ready"], t - 1)
                for tt in range(2):
                    last = mm(MISC[0:16, tt * P:(tt + 1) * P], mx[:, t, tt, :], identb[:, :], start=True, stop=True)
                last.then_inc(sem["maxT_psum"], 1)

            def score(t, u, w, k):
                if k == 0:
                    pe.wait_ge(sem["maxrow_done"], (t + 1) * 32)
                if not (isinstance(t, int) and t == 0 and k < 2):
                    pe.wait_ge(sem["exp_ready"], t * GRANULES + (k - 1))
                b, pair = k % 4 // 2, 2 * (k % 2) + k // 4
                for st in range(2):
                    last = mm(EX[k % 2][:, st * 512:(st + 1) * 512], KS[u][:, b, pair, st * P:(st + 1) * P],
                              QS[u][:, :, b, pair, :], start=True, stop=True)
                last.then_inc(sem["sT_psum"], 1)

            def values(t, u, w, first, n):
                for group in range(first, first + n):
                    half, par, st, den = group // 8, group // 4 % 2, group // 2 % 2, group % 2
                    if group % 8 == 0:
                        pe.wait_ge(sem["exp_ready"], t * GRANULES + (4 * half + 4))
                    if group == 0:
                        pe.wait_ge(sem["vz_ready"], t + 1)
                        if not (isinstance(t, int) and t == 0):
                            pe.wait_ge(sem["o_ready"], t)
                    at = 32 * (2 * half + par)
                    for g in range(4):
                        last = mm(AV[32 * g:32 * g + 32, den * D:(den + 1) * D],
                                  OZ[:, at:at + 32] if den else VZ[u][:, st * 4 + g, at:at + 32],
                                  PB[:, 4 * half + g, st * 512 + par * D:st * 512 + (par + 1) * D],
                                  start=group == 0, stop=group >= 14, skip_group_check=True)
                    if group % 8 == 7:
                        last.then_inc(sem["av_psum"], 1)

            def out_proj(t):
                if live(t + 3):
                    pe.wait_ge(sem["vz_ready"], t + 4)
                elif live(t + 1):
                    pe.wait_ge(sem["maxT_ready"], t + 2)
                else:
                    pe.wait_ge(sem["x3_ready"], t)
                pe.wait_ge(sem["o_ready"], t + 1)
                mm(MISC[:, 0:D], wob[:, :], ob[:, :], start=True, stop=True).then_inc(sem["yc_psum"], 1)


            def unit(t, b=None):
                if on(t):
                    a1_s1(t)
                if on(t - 2):
                    a2_r2(t - 2, 0)
                if on(t):
                    a1_s2(t)
                if on(t - 2):
                    a2_r2(t - 2, 1)
                if b is not None:
                    proj_q(b)
                if on(t):
                    a1_s3(t)
                if on(t - 2):
                    a2_r4(t - 2, 0)
                if on(t):
                    a1_s4(t)
                if on(t - 2):
                    a2_r5(t - 2, 0)
                if b is not None:
                    proj_k(*tile(0, b))
                if on(t):
                    a1_s5(t)
                if on(t - 1):
                    a2_r1(t - 1)
                    a2_r1h(t - 1)
                if on(t - 2):
                    a2_r4(t - 2, 1)
                if b is not None:
                    proj_v(*tile(0, b))
                if on(t):
                    a1_s6(t)
                if on(t - 2):
                    a2_r5(t - 2, 1)

            unit(1)
            unit(2)
            with pe.Fori(3, UNITS - 1) as t:
                unit(t)
            unit(UNITS - 1)
            unit(UNITS, 0)
            unit(UNITS + 1, 1)

            pe.wait_ge(sem["x2_ready"], NT)
            pe.wait_ge(sem["ones_row_placed"], 2 * NBUF * 16)

            for m in range(MAXG):
                score_max(*tile(0, 0), m, first=True)
            proj_q(2)

            VALUES = {(7, 0): (0, 2), (7, 1): (2, 2), (0, 0): (4, 1), (0, 1): (5, 1), (1, 0): (6, 1), (1, 1): (7, 1),
                      (3, 0): (8, 2), (3, 1): (10, 2), (4, 0): (12, 2), (4, 1): (14, 2)}

            def values_part(turn, off, k, part):
                at = off if k == 7 else off - 1
                if (k, part) in VALUES and live(tile(turn, at)[0]):
                    values(*tile(turn, at), *VALUES[k, part])

            def slot(turn, off, tail=True):
                s = tile(turn, off)[0]
                for k in range(GRANULES):
                    if k < LAG and live(s - 1):
                        score(*tile(turn, off - 1), k + GRANULES - LAG)
                    if k >= LAG and live(s):
                        score(*tile(turn, off), k - LAG)
                    if live(s + 1):
                        score_max(*tile(turn, off + 1), 2 * k)
                    values_part(turn, off, k, 0)
                    if live(s + 1):
                        score_max(*tile(turn, off + 1), 2 * k + 1)
                    if k == 0 and live(s):
                        max_turn(s)
                    if k == 1 and live(s + 2):
                        proj_k(*tile(turn, off + 2))
                    if k == 2 and live(s + 2):
                        proj_v(*tile(turn, off + 2))
                    if k == 7 and live(s + 3):
                        proj_q(s + 3)
                    values_part(turn, off, k, 1)
                    if k == 6 and live(s - 1) and tail:
                        out_proj(s - 1)

            for s in range(4):
                slot(0, s)
            with pe.Fori(1, 4) as i:
                for r in range(1, 4):
                    slot(i, r)
            for s in range(13, NT):
                slot(0, s)
            def oh_turn(g):
                pe.wait_ge(sem["onehot_ready"], 4 * g + 4)
                if g >= 2:
                    pe.wait_ge(sem["ohT_ready"], g - 1)
                for i in range(4):
                    last = nc.tensor.transpose((bankA if g % 2 == 0 else bankB)[0:NTILE, i * P:(i + 1) * P],
                                               oh[:, 4 * g + i, :], ident[:, :])
                last.then_inc(sem["ohT_psum"], 1)

            def look_up(g):
                pe.wait_ge(sem["ohT_ready"], (3 * g + min(3, NT - 3 * g) - 1) // 4 + 1)
                if g >= 4:
                    pe.wait_ge(sem["look_ready"], g - 3)
                for i in range(min(3, NT - 3 * g)):
                    last = mm(big[:, g % 4, i * (ROW - 2):(i + 1) * (ROW - 2)], ohT[:, 3 * g + i, :],
                              table[:, 0:ROW - 2], start=True, stop=True)
                last.then_inc(sem["look_psum"], 1)

            pe.wait_ge(sem["max_ready"], NT * MAXG)
            for g in range(3):
                oh_turn(g)
            slot(0, NT, tail=False)
            pe.wait_ge(sem["exp_ready"], NT * GRANULES)
            for g in range(4):
                look_up(g)
            out_proj(NT - 1)
            oh_turn(3)
            look_up(4)
            look_up(5)
            pe.wait_ge(sem["max_part"], 1)
            for i in range(2):
                last = nc.tensor.transpose(bankC[0:NTILE, i * P:(i + 1) * P], mpart[:, i, :], ident[:, :])
            last.then_inc(sem["mm_psum"], 1)
            pe.wait_ge(sem["mm_ready"], 1)
            for n in range(NT):
                last = mm(bankA[:, 2 * n:2 * n + 2], ohT[:, n, :], table[:, ROW - 2:ROW], start=True, stop=True)
            last.then_inc(sem["mmt_psum"], 1)

        @block.vector
        def _(v):
            V = nc.vector

            def stats(name, srcs, stt, mv, ve, t):
                for j, src in enumerate(srcs):
                    last = V.bn_stats(stt[j], src)
                last.then_inc(sem[name + "_steps"], 1)
                v.wait_ge(sem[name + "_steps"], t * 2 + 1)
                V.memset(hold[:, 0:1], 0.0)
                for j in range(len(srcs)):
                    last = V.bn_aggr(mv[j], stt[j])
                last.then_inc(sem[name + "_steps"], 1)
                v.wait_ge(sem[name + "_steps"], t * 2 + 2)
                for j in range(len(srcs)):
                    last = V.tensor_scalar(ve[j], mv[j][:, 1:2], LN_EPS, None, ALU.add)
                last.then_inc(sem[name + "_var"], 1)

            def ln1_stats(t):
                stats("ln1", [xall[:, t * 2 + j, :] for j in range(2)], [st1[:, j, :] for j in range(2)],
                      [mv1[:, j, :] for j in range(2)], [ve1[:, j:j + 1] for j in range(2)], t)

            def ln1_apply(t):
                v.wait_ge(sem["ln1_rstd"], t + 1)
                if not (isinstance(t, int) and t == 0):
                    v.wait_ge(sem["xT_psum"], t)
                for j in range(2):
                    last = V.tensor_scalar(xn[:, j, :], xall[:, t * 2 + j, :], mv1[:, j, 0:1], rs1[:, j:j + 1],
                                           ALU.subtract, ALU.mult)
                last.then_inc(sem["xn_ready"], 1)

            def a1_max(t):
                v.wait_ge(sem["s_psum"], t + 1)
                V.tensor_reduce(nmax[:, :], bankC[:, 0:2 * P].rearrange("p (j n) -> p j n", j=2), AX,
                                ALU.max).then_inc(sem["s_max"], 1)
                v.wait_ge(sem["s_max"], t + 1)
                V.tensor_scalar(nmaxs[:, :], nmax[:, :], -1.0 / 16.0, None, ALU.mult).then_inc(sem["nmax_ready"], 1)

            def a1_out(t):
                v.wait_ge(sem["probs_ready"], t + 1)
                V.reciprocal(pinv[:, :], psums[:, :]).then_inc(sem["rsum_ready"], 1)
                v.wait_ge(sem["rsum_ready"], t + 1)
                v.wait_ge(sem["y_psum"], t + 1)
                for j in range(2):
                    last = V.scalar_tensor_tensor(out=xall[:, t * 2 + j, :], in0=bankB[:, j * D:(j + 1) * D],
                                                  scalar=pinv[:, j:j + 1], in1=xall[:, t * 2 + j, :],
                                                  op0=ALU.mult, op1=ALU.add)
                last.then_inc(sem["x1_ready"], 1)

            def ln2_stats(t):
                stats("ln2", [xall[:, t * 2 + j, :] for j in range(2)], [st2[:, j, :] for j in range(2)],
                      [mv2[:, j, :] for j in range(2)], [ve2[:, j:j + 1] for j in range(2)], t)

            def a2_quant(t):
                v.wait_ge(sem["ln2_rstd"], t + 1)
                for j in range(2):
                    last = V.tensor_scalar(xn2[:, j, :], xall[:, t * 2 + j, :], mv2[:, j, 0:1], rs2[:, j:j + 1],
                                           ALU.subtract, ALU.mult)
                last.then_inc(sem["xn2_ready"], 1)
                v.wait_ge(sem["xn2_ready"], t + 1)
                V.tensor_reduce(amax[:, :], xn2[:, :, :], AX, ALU.max,
                                apply_absolute_value=True).then_inc(sem["amax_ready"], 1)
                v.wait_ge(sem["amax_ready"], t + 1)
                V.tensor_scalar(amaxc[:, :], amax[:, :], Q_EPS, None, ALU.max).then_inc(sem["amaxc_ready"], 1)
                v.wait_ge(sem["amaxc_ready"], t + 1)
                V.reciprocal(arec[:, :], amaxc[:, :]).then_inc(sem["arec_ready"], 1)
                V.tensor_scalar(ainv[:, :], amaxc[:, :], 1.0 / 127.0, None, ALU.mult).then_inc(sem["act_scale2"], 1)
                v.wait_ge(sem["arec_ready"], t + 1)
                V.tensor_scalar(ascale[:, :], arec[:, :], 127.0, None, ALU.mult).then_inc(sem["ascale_ready"], 1)

            def a2_round(t):
                v.wait_ge(sem["ascale_ready"], t + 1)
                for j in range(2):
                    last = V.tensor_scalar(xn2[:, j, :], xn2[:, j, :], ascale[:, j:j + 1], MAGIC, ALU.mult, ALU.add)
                last.then_inc(sem["a_round"], 1)
                v.wait_ge(sem["a_round"], t + 1)
                if not (isinstance(t, int) and t == 0):
                    v.wait_ge(sem["xqT_psum"], t)
                V.tensor_scalar(xq[:, :, :].rearrange("p j d -> p (j d)"), xn2[:, :, :].rearrange("p j d -> p (j d)"),
                                MAGIC, None, ALU.subtract).then_inc(sem["xq_ready"], 1)
                v.wait_ge(sem["act_scale2"], t + 1)
                for j in range(2):
                    last = V.tensor_scalar(xh[:, j, :].rearrange("p (b a) -> p a b", a=16),
                                           xn2[:, j, :].rearrange("p (a b) -> p a b", b=16),
                                           MAGIC, ainv[:, j:j + 1], ALU.subtract, ALU.mult)
                last.then_inc(sem["xh_ready"], 1)

            def a2_scale(t):
                if not (isinstance(t, int) and t == 0):
                    v.wait_ge(sem["up_ready"], t * 2)
                V.tensor_scalar(aGh[:, :], amaxc[:, :], wm127[:, 0:1], 0.5, ALU.mult, ALU.mult).then_inc(sem["act_scale3"], 1)

            def a2_h(t, j):
                n = t * 2 + j
                v.wait_ge(sem["gate_ready"], n + 1)
                v.wait_ge(sem["up_ready"], n + 1)
                if not (isinstance(n, int) and n == 0):
                    v.wait_ge(sem["hq_ready"], n)
                V.scalar_tensor_tensor(out=h1, in0=th, scalar=1.0, in1=us, op0=ALU.add,
                                       op1=ALU.mult).then_inc(sem["h_half"], 1)
                v.wait_ge(sem["h_half"], n + 1)
                V.tensor_tensor(h2.rearrange("p (a n) -> p a n", a=2), G,
                                h1.rearrange("p (a n) -> p a n", a=2), ALU.mult).then_inc(sem["h_ready"], 1)

            def a2_hquant(t, j):
                n = t * 2 + j
                v.wait_ge(sem["h_ready"], n + 1)
                V.tensor_reduce(hm[:, 0:1], h2, AX, ALU.max, apply_absolute_value=True).then_inc(sem["hamax_ready"], 1)
                v.wait_ge(sem["hamax_ready"], n + 1)
                V.tensor_scalar(hm[:, 1:2], hm[:, 0:1], Q_EPS, None, ALU.max).then_inc(sem["hamaxc_ready"], 1)
                v.wait_ge(sem["hamaxc_ready"], n + 1)
                V.reciprocal(hm[:, 2:3], hm[:, 1:2]).then_inc(sem["hrec_ready"], 1)
                V.tensor_scalar(bD[:, j:j + 1], hm[:, 1:2], wm127[:, 2:3], None, ALU.mult).then_inc(sem["dscale_ready"], 1)
                v.wait_ge(sem["hrec_ready"], n + 1)
                V.tensor_scalar(hm[:, 3:4], hm[:, 2:3], 127.0, None, ALU.mult).then_inc(sem["hscale_ready"], 1)
                v.wait_ge(sem["hscale_ready"], n + 1)
                V.tensor_scalar(h1, h2, hm[:, 3:4], MAGIC, ALU.mult, ALU.add).then_inc(sem["h_round"], 1)
                v.wait_ge(sem["h_round"], n + 1)
                if not (isinstance(n, int) and n == 0):
                    v.wait_ge(sem["hT_psum"], n)
                V.tensor_scalar(hq[:, :], h1, MAGIC, None, ALU.subtract).then_inc(sem["hq_ready"], 1)

            def a2_out(t, j):
                n = t * 2 + j
                v.wait_ge(sem["dscale_ready"], n + 1)
                v.wait_ge(sem["down_psum"], n + 1)
                V.scalar_tensor_tensor(out=xall[:, n, :], in0=(bankD if j else bankB)[:, 0:D], scalar=bD[:, j:j + 1],
                                       in1=xall[:, n, :], op0=ALU.mult, op1=ALU.add).then_inc(sem["x2_ready"], 1)

            def ternary(i):
                src, dst, n = ((wffn[:, 0, :], wgT[:, :, :], P), (wffn[:, 1, :], wuT, P), (wdn, wdT[:, :, :], FP))[i]
                V.tensor_scalar(src, src, winv[0:n, i:i + 1], 1.0, ALU.mult, ALU.min).then_inc(sem["w_clip"], 1)
                v.wait_ge(sem["w_clip"], i + 1)
                V.tensor_scalar(src, src, -1.0, MAGIC, ALU.max, ALU.add).then_inc(sem["w_round"], 1)
                v.wait_ge(sem["w_round"], i + 1)
                V.tensor_scalar(dst.rearrange("p a b -> p (a b)"), src, MAGIC, wmean[:, 1:2] if i == 1 else 1.0,
                                ALU.subtract, ALU.mult).then_inc(sem["w_ready"], 1)

            V.memset(halfneg[:, :], -0.5)
            V.memset(ones[:, :], 1.0)
            V.memset(OZ[:, :], 0.0).then_inc(sem["oz_ready"], 1)
            v.wait_ge(sem["oz_ready"], 1)
            V.memset(OZ[:, :].rearrange("p (a b) -> p a b", b=40)[:, :, 0:HC], 1.0).then_inc(sem["oz_ready"], 1)
            v.wait_ge(sem["ident_loaded"], 16)
            V.tensor_copy(identb[:, :], ident[:, :]).then_inc(sem["ident_ready"], 1)
            v.wait_ge(sem["x0_loaded"], 16)
            ln1_stats(0)
            ln1_apply(0)
            v.wait_ge(sem["x_loaded"], 32)
            ln1_stats(1)
            ln1_apply(1)
            a1_max(0)
            v.wait_ge(sem["ffn_w_loaded"], 48)
            V.tensor_reduce(wsum[:, 0:2], wffn, AX, ALU.add, apply_absolute_value=True).then_inc(sem["wsum_ready"], 2)
            V.tensor_reduce(wsum[0:FP, 2:3], wdn, AX, ALU.add, apply_absolute_value=True).then_inc(sem["wsum_ready"], 1)
            v.wait_ge(sem["wtot_ready"], 1)
            V.tensor_scalar(wmean[:, 0:3], bankD[:, 0:3], 1.0 / (FF * D), Q_EPS, ALU.mult, ALU.max).then_inc(sem["wmean_ready"], 1)
            v.wait_ge(sem["wmean_ready"], 1)
            V.reciprocal(winv[:, 0:3], wmean[:, 0:3])
            V.tensor_scalar(wm127[:, 0:3], wmean[:, 0:3], 1.0 / 127.0, None, ALU.mult).then_inc(sem["winv_ready"], 1)
            v.wait_ge(sem["winv_ready"], 1)
            v.wait_ge(sem["bo_sum_ready"], 1)
            V.tensor_tensor(boe[:, :], bankD[:, 8:9], bias[:, 5:6], ALU.add).then_inc(sem["bo_ready"], 1)
            a1_out(0)
            norms = {"ln3": (lambda t: xall[:, t, :], st3, mv3, ve3[:, 0:1]),
                     "ln4": (lambda t: xall[:, t, :], st4, mv4, ve4[:, 0:1]),
                     "ln5": (lambda t: xn4, st5, mv5, ve4[:, 1:2])}

            def norm_bn(name, t):
                src, st, mv, ve = norms[name]
                V.bn_stats(st[:, :], src(t)).then_inc(sem[name + "_steps"], 1)

            def norm_aggr(name, t):
                src, st, mv, ve = norms[name]
                v.wait_ge(sem[name + "_steps"], t * 2 + 1)
                V.memset(hold[:, 0:1], 0.0)
                V.bn_aggr(mv[:, :], st[:, :]).then_inc(sem[name + "_steps"], 1)

            def norm_var(name, t):
                src, st, mv, ve = norms[name]
                v.wait_ge(sem[name + "_steps"], t * 2 + 2)
                V.tensor_scalar(ve, mv[:, 1:2], LN_EPS, None, ALU.add).then_inc(sem[name + "_var"], 1)

            def norm_stats(name, t):
                norm_bn(name, t)
                norm_aggr(name, t)
                norm_var(name, t)

            def ln3_apply(t):
                v.wait_ge(sem["ln3_rstd"], t + 1)
                if not (isinstance(t, int) and t == 0):
                    v.wait_ge(sem["qproj_psum"], t)
                V.tensor_scalar(xn3[:, :], xall[:, t, :], mv3[:, 0:1], rs3[:, 0:1],
                                ALU.subtract, ALU.mult).then_inc(sem["xn3_ready"], 1)

            def rope_part(t, a, i):
                if i == 0:
                    v.wait_ge(sem["kproj_psum" if a else "qproj_psum"], t + 1)
                    if not (isinstance(t, int) and t == 0):
                        v.wait_ge(sem["qk_sum"], t * 2 - 1 + a)
                last = V.scalar_tensor_tensor(out=rope[:, a, i, :], in0=proj_bank(t)[:, i * D:(i + 1) * D],
                                              scalar=bias[:, 2 * a + i:2 * a + i + 1], in1=(sin if i else cos)[:, :],
                                              op0=ALU.add, op1=ALU.mult)
                if i == 1:
                    last.then_inc(sem["rope_k" if a else "rope_q"], 1)

            def reduce_max(t, m):
                b, tt, pair = m // 8, m // 4 % 2, m % 4
                v.wait_ge(sem["max_psum"], t * MAXG + (m + 1))
                col = mx[:, t, tt, :].rearrange("p (a c) -> p a c", a=2)[:, :, b * 4 + pair]
                V.tensor_reduce(col, MXB[m % 2][:, :].rearrange("p (a n) -> p a n", a=2), AX,
                                ALU.max).then_inc(sem["max_ready"], 1)

            def den_inverse(t):
                v.wait_ge(sem["av_psum"], t * 2 + 2)
                V.reciprocal(dinv[:, :], AV[:, D:2 * D]).then_inc(sem["den_inv"], 1)

            def normalize(t):
                v.wait_ge(sem["den_inv"], t + 1)
                if not (isinstance(t, int) and t == 0):
                    v.wait_ge(sem["yc_psum"], t)
                V.tensor_tensor(ob[:, :], AV[:, 0:D], dinv[:, :], ALU.mult).then_inc(sem["o_ready"], 1)

            def residual(t):
                v.wait_ge(sem["yc_psum"], t + 1)
                V.scalar_tensor_tensor(out=xall[:, t, :], in0=MISC[:, 0:D], scalar=boe[:, 0:1],
                                       in1=xall[:, t, :], op0=ALU.add, op1=ALU.add).then_inc(sem["x3_ready"], 1)

            def ln4_apply(t):
                v.wait_ge(sem["ln4_rstd"], t + 1)
                if not (isinstance(t, int) and t == 0):
                    v.wait_ge(sem["x4_ready"], t)
                V.tensor_scalar(xn4, xall[:, t, :], mv4[:, 0:1], rs4[:, 0:1],
                                ALU.subtract, ALU.mult).then_inc(sem["xn4_ready"], 1)

            def ln5_bn(t):
                v.wait_ge(sem["xn4_ready"], t + 1)
                norm_bn("ln5", t)

            def ln5_apply(t):
                v.wait_ge(sem["ln5_rstd"], t + 1)
                if not (isinstance(t, int) and t == 0):
                    v.wait_ge(sem["gamma_done"], t)
                V.tensor_scalar(xn5, xn4, mv5[:, 0:1], rs4[:, 1:2],
                                ALU.subtract, ALU.mult).then_inc(sem["xn5_ready"], 1)

            def route_sign(t, step):
                if step == 0:
                    v.wait_ge(sem["sgn_prod"], t + 1)
                    V.tensor_scalar(wk2[:, :], wk1, 0.0, None, ALU.is_lt).then_inc(sem["sgn_neg"], 1)
                else:
                    v.wait_ge(sem["sgn_neg"], t + 1)
                    V.scalar_tensor_tensor(out=wk2[:, :], in0=wk1, scalar=0.0, in1=wk2[:, :], op0=ALU.is_gt,
                                           op1=ALU.subtract).then_inc(sem["sgn_ready"], 1)

            def route_sums(t):
                v.wait_ge(sem["sgn_ready"], t + 1)
                V.tensor_reduce(csc[:, :], wk2[:, :].rearrange("p (c n) -> p c n", c=CLUSTERS), AX,
                                ALU.add).then_inc(sem["clus_score"], 1)
                V.tensor_reduce(tsc[:, :], wk2[:, :].rearrange("p (n j) -> p n j", j=SLICE), AX,
                                ALU.add).then_inc(sem["tile_score"], 1)

            def route_cluster(t):
                v.wait_ge(sem["clus_score"], t + 1)
                V.scalar_tensor_tensor(out=key1[:, :].rearrange("p (c n) -> p c n", c=CLUSTERS),
                                       in0=csc[:, :].unsqueeze(2).to_broadcast([P, CLUSTERS, CLUSTERS]),
                                       scalar=1024.0, in1=ckey[:, :].rearrange("p (c n) -> p c n", c=CLUSTERS),
                                       op0=ALU.mult, op1=ALU.add).then_inc(sem["key_c"], 1)

            def route_key(t):
                v.wait_ge(sem["key_c"], t + 1)
                v.wait_ge(sem["tile_score"], t + 1)
                V.scalar_tensor_tensor(out=key2[:, :], in0=tsc[:, :], scalar=8.0, in1=key1[:, :], op0=ALU.mult,
                                       op1=ALU.add).then_inc(sem["key_ready"], 1)

            def route_best(t):
                v.wait_ge(sem["key_ready"], t + 1)
                V.tensor_reduce(kmax[:, :], key2[:, :], AX, ALU.max).then_inc(sem["key_max"], 1)

            def route_onehot(t):
                v.wait_ge(sem["key_max"], t + 1)
                V.tensor_scalar(oh[:, t, :], key2[:, :], kmax[:, 0:1], None, ALU.is_equal).then_inc(sem["onehot_ready"], 1)

            def route_mask(t):
                v.wait_ge(sem["onehot_ready"], t + 1)
                V.tensor_tensor(wk2[:, :].rearrange("p (n j) -> p n j", j=SLICE),
                                xf.rearrange("p (n j) -> p n j", j=SLICE),
                                oh[:, t, :].unsqueeze(2).to_broadcast([P, NTILE, SLICE]),
                                ALU.mult).then_inc(sem["xf_masked"], 1)

            def route_slice(t):
                v.wait_ge(sem["xf_masked"], t + 1)
                V.tensor_reduce(xs[:, t, :], wk2[:, :].rearrange("p (n j) -> p j n", j=SLICE), AX,
                                ALU.add).then_inc(sem["slice_ready"], 1)

            def unit(t, b=None):
                if on(t - 1):
                    v.wait_ge(sem["x1_ready"], t)
                    ln2_stats(t - 1)
                if b is not None:
                    norm_stats("ln3", b)
                if on(t - 1):
                    a2_quant(t - 1)
                if isinstance(t, int) and t == 1:
                    ternary(0)
                if on(t - 2):
                    a2_h(t - 2, 0)
                if on(t - 1):
                    a2_round(t - 1)
                if b is not None:
                    ln3_apply(b)
                if on(t - 2):
                    a2_hquant(t - 2, 0)
                if b is not None:
                    rope_part(b, 0, 0)
                    rope_part(b, 0, 1)
                if on(t):
                    a1_max(t)
                if isinstance(t, int) and t == 1:
                    ternary(1)
                    ternary(2)
                if on(t - 2):
                    a2_h(t - 2, 1)
                    a2_hquant(t - 2, 1)
                if b is not None:
                    rope_part(b, 1, 0)
                    rope_part(b, 1, 1)
                if on(t - 1):
                    a2_scale(t - 1)
                if on(t - 2):
                    a2_out(t - 2, 0)
                if on(t + 1):
                    ln1_stats(t + 1)
                    ln1_apply(t + 1)
                if on(t):
                    a1_out(t)
                if on(t - 2):
                    a2_out(t - 2, 1)

            unit(1)
            unit(2)
            v.wait_ge(sem["ffn2_loaded"], 8 * 16)
            V.tensor_reduce(ssum, slopes, AX, ALU.add).then_inc(sem["slope_sum"], 1)
            v.wait_ge(sem["slope_sum"], 1)
            V.tensor_scalar(sneg, ssum, 0.0, None, ALU.is_lt).then_inc(sem["slope_neg"], 1)
            v.wait_ge(sem["slope_neg"], 1)
            V.scalar_tensor_tensor(out=sig[:, :], in0=ssum, scalar=0.0, in1=sneg, op0=ALU.is_gt,
                                   op1=ALU.subtract).then_inc(sem["sig_ready"], 1)
            with v.Fori(3, UNITS - 1) as t:
                unit(t)
            unit(UNITS - 1)
            v.wait_ge(sem["chan_w_loaded"], 7 * 16)
            unit(UNITS, 0)
            unit(UNITS + 1, 1)

            v.wait_ge(sem["x2_ready"], NT)

            for m in range(MAXG):
                reduce_max(0, m)

            norm_stats("ln3", 2)
            ln3_apply(2)

            def slot(s):
                ahead, front, mid, back, route = live(s + 3), live(s + 2), live(s - 1), live(s - 2), live(s - 3)

                def maxima(m):
                    if live(s + 1):
                        reduce_max(s + 1, m)

                if back:
                    v.wait_ge(sem["x3_ready"], s - 1)
                if front:
                    rope_part(s + 2, 0, 0)
                if back:
                    norm_bn("ln4", s - 2)
                if front:
                    rope_part(s + 2, 0, 1)
                maxima(0)
                if back:
                    norm_aggr("ln4", s - 2)
                maxima(1)
                if back:
                    norm_var("ln4", s - 2)
                if route:
                    route_sign(s - 3, 0)
                maxima(2)
                if route:
                    route_sign(s - 3, 1)
                maxima(3)
                if front:
                    rope_part(s + 2, 1, 0)
                    rope_part(s + 2, 1, 1)
                if route:
                    route_sums(s - 3)
                maxima(4)
                if route:
                    route_cluster(s - 3)
                maxima(5)
                if route:
                    route_key(s - 3)
                if back:
                    ln4_apply(s - 2)
                maxima(6)
                if route:
                    route_best(s - 3)
                if back:
                    ln5_bn(s - 2)
                maxima(7)
                if route:
                    route_onehot(s - 3)
                if back:
                    norm_aggr("ln5", s - 2)
                if ahead:
                    norm_bn("ln3", s + 3)
                maxima(8)
                if route:
                    route_mask(s - 3)
                if back:
                    norm_var("ln5", s - 2)
                maxima(9)
                if ahead:
                    norm_aggr("ln3", s + 3)
                if route:
                    route_slice(s - 3)
                if mid:
                    den_inverse(s - 1)
                maxima(10)
                if mid:
                    normalize(s - 1)
                if ahead:
                    norm_var("ln3", s + 3)
                maxima(11)
                if back:
                    ln5_apply(s - 2)
                maxima(12)
                maxima(13)
                if mid:
                    residual(s - 1)
                if ahead:
                    ln3_apply(s + 3)
                maxima(14)
                maxima(15)

            for s in range(4):
                slot(s)
            with v.Fori(4, 13) as s:
                slot(s)
            for s in range(13, NT):
                slot(s)

            steps = [0]

            def step(ins):
                ins.then_inc(sem["spline_step"], 1)
                steps[0] += 1

            def settle():
                v.wait_ge(sem["spline_step"], steps[0])

            def extremes(n0, n1, dst):
                step(V.tensor_reduce(tmm[:, n0:n1, 0], xs[:, n0:n1, :], AX, ALU.min))
                step(V.tensor_reduce(tmm[:, n0:n1, 1], xs[:, n0:n1, :], AX, ALU.max))
                step(V.tensor_scalar(bigm[:, n0:n1, :], oh[:, n0:n1, :], -BIG, BIG, ALU.mult, ALU.add))
                settle()
                w = [P, n1 - n0, NTILE]
                for i in range(2):
                    step(V.tensor_tensor(dst[i], oh[:, n0:n1, :], tmm[:, n0:n1, i:i + 1].to_broadcast(w), ALU.mult))
                settle()
                for i in range(2):
                    step(V.tensor_tensor(dst[i], dst[i], bigm[:, n0:n1, :], (ALU.add, ALU.subtract)[i]))
                settle()

            v.wait_ge(sem["x3_ready"], NT - 1)
            norm_bn("ln4", 14)
            route_sign(13, 0)
            norm_aggr("ln4", 14)
            route_sign(13, 1)
            norm_var("ln4", 14)
            route_sums(13)
            route_cluster(13)
            ln4_apply(14)
            route_key(13)
            ln5_bn(14)
            route_best(13)
            norm_aggr("ln5", 14)
            route_onehot(13)
            norm_var("ln5", 14)
            route_mask(13)
            route_slice(13)
            ln5_apply(14)
            v.wait_ge(sem["slice_ready"], EARLY)
            extremes(0, EARLY, (low[:, 0:EARLY, :], high[:, 0:EARLY, :]))
            for i, (src, op) in enumerate(((low, ALU.min), (high, ALU.max))):
                step(V.tensor_reduce(edge[:, i, 2, :], src[:, 0:EARLY, :].rearrange("p n t -> p t n"), AX, op))
            den_inverse(15)
            route_sign(14, 0)
            normalize(15)
            route_sign(14, 1)
            route_sums(14)
            route_cluster(14)
            residual(15)
            route_key(14)
            v.wait_ge(sem["x3_ready"], NT)
            norm_bn("ln4", 15)
            route_best(14)
            norm_aggr("ln4", 15)
            route_onehot(14)
            norm_var("ln4", 15)
            route_mask(14)
            ln4_apply(15)
            route_slice(14)
            ln5_bn(15)
            norm_aggr("ln5", 15)
            norm_var("ln5", 15)
            ln5_apply(15)
            for part in range(2):
                route_sign(15, part)
            route_sums(15)
            route_cluster(15)
            route_key(15)
            route_best(15)
            route_onehot(15)
            route_mask(15)
            route_slice(15)

            v.wait_ge(sem["slice_ready"], NT)
            extremes(EARLY, NT, (edge[:, 0, 0:2, :], edge[:, 1, 0:2, :]))
            for i, op in enumerate((ALU.min, ALU.max)):
                last = V.tensor_reduce(mpart[:, i, :], edge[:, i, :, :].rearrange("p a t -> p t a"), AX, op)
            last.then_inc(sem["max_part"], 1)
            v.wait_ge(sem["mm_psum"], 1)
            V.tensor_reduce(table[:, ROW - 2:ROW - 1], bankC[0:NTILE, 0:P], AX, ALU.min)
            V.tensor_reduce(table[:, ROW - 1:ROW], bankC[0:NTILE, P:2 * P], AX, ALU.max).then_inc(sem["mm_ready"], 1)
            v.wait_ge(sem["mmt_psum"], 1)
            step(V.tensor_copy(mmt[:, :, :].rearrange("p n a -> p (n a)"), bankA[:, 0:2 * NT]))
            settle()
            step(V.tensor_tensor(span[:, 0, :], mmt[:, :, 1], mmt[:, :, 0], ALU.subtract))
            step(V.tensor_tensor(u0[:, :, :], xs[:, :, :], mmt[:, :, 0:1].to_broadcast([P, NT, SLICE]), ALU.subtract))
            settle()
            step(V.tensor_scalar(span[:, 1, :], span[:, 0, :], 1e-8, None, ALU.add))
            settle()
            step(V.reciprocal(span[:, 2, :], span[:, 1, :]))
            settle()
            step(V.tensor_tensor(u1[:, :, :], u0[:, :, :], span[:, 2, :].unsqueeze(2).to_broadcast([P, NT, SLICE]),
                                 ALU.mult))
            settle()
            step(V.tensor_scalar(u2[:, :, :], u1[:, :, :], 0.0, 1.0 - 1e-6, ALU.max, ALU.min))
            settle()
            step(V.tensor_scalar(u3[:, :, :], u2[:, :, :], float(GRID), None, ALU.mult))
            settle()
            step(V.tensor_scalar(u4[:, :, :], u3[:, :, :], MAGIC, None, ALU.add))
            settle()
            step(V.tensor_scalar(u5[:, :, :], u4[:, :, :], MAGIC, None, ALU.subtract))
            settle()
            step(V.tensor_tensor(u0[:, :, :], u5[:, :, :], u3[:, :, :], ALU.is_gt))
            settle()
            step(V.tensor_tensor(u1[:, :, :], u5[:, :, :], u0[:, :, :], ALU.subtract))
            settle()
            step(V.tensor_scalar(u2[:, :, :], u1[:, :, :], 0.0, float(GRID - 1), ALU.max, ALU.min))
            settle()
            u2m = u2[:, :, :].rearrange("p n j -> p (n j)")
            V.tensor_tensor(gmask.rearrange("p (m g) -> p m g", g=GRID),
                            giota[:, :].unsqueeze(1).to_broadcast([P, NT * SLICE, GRID]),
                            u2m.unsqueeze(2).to_broadcast([P, NT * SLICE, GRID]),
                            ALU.is_equal).then_inc(sem["mask_ready"], 1)
            step(V.tensor_tensor(u4[:, :, :], u3[:, :, :], u2[:, :, :], ALU.subtract))
            v.wait_ge(sem["look_ready"], 6)
            v.wait_ge(sem["mask_ready"], 1)
            step(V.tensor_tensor(gprod[0].rearrange("p (n c) -> p n c", n=NT), gmask.rearrange("p (n c) -> p n c", n=NT),
                                 look[:, :, 0:64], ALU.mult))
            settle()
            step(V.tensor_reduce(bsel[:, :, :].rearrange("p n j -> p (n j)"), gprod[0].rearrange("p (m g) -> p m g", g=GRID),
                                 AX, ALU.add))
            v.wait_ge(sem["slope_picked"], 1)
            step(V.tensor_reduce(ssel[:, :, :].rearrange("p n j -> p (n j)"), gprod[1].rearrange("p (m g) -> p m g", g=GRID),
                                 AX, ALU.add))
            settle()
            step(V.tensor_tensor(u5[:, :, :], ssel[:, :, :], u4[:, :, :], ALU.mult))
            settle()
            step(V.tensor_tensor(u3[:, :, :], u5[:, :, :], bsel[:, :, :], ALU.add))
            settle()
            V.tensor_tensor(delta[:, :, :], u3[:, :, :], look[:, :, 128:129].to_broadcast([P, NT, SLICE]),
                            ALU.mult).then_inc(sem["delta_ready"], 1)
            v.wait_ge(sem["delta_ready"], 1)
            v.wait_ge(sem["x4_ready"], NT)
            for i, (n0, n1) in enumerate(OUT_DVE):
                place(V, n0, n1).then_inc(sem["place_dve"], 1)
                v.wait_ge(sem["place_dve"], i + 1)
                V.tensor_tensor(outb[:, n0:n1, :], outb[:, n0:n1, :], xall[:, n0:n1, :],
                                ALU.add).then_inc(sem["out_dve"], 1)


def kernel(**inputs):
    import numpy as np
    import concourse.bacc as bacc
    from concourse.bass_utils import run_bass_kernel_spmd

    a = {k: np.asarray(v) for k, v in inputs.items()}
    f = np.float32

    def turned(w):
        return np.ascontiguousarray(w.T)

    def twice(w):
        z = np.zeros((2 * w.shape[0], 2 * w.shape[1]), f)
        z[:w.shape[0], :w.shape[1]] = w
        z[w.shape[0]:, w.shape[1]:] = w
        return z

    order = [(b, (2 * g + par) * HC + c) for par in range(2) for c in range(HC) for b in range(2) for g in range(PAIRS)]
    rolled = [(b, o // HC * HC + (o % HC + HC // 2) % HC) for b, o in order]
    cols = np.array([b * 64 + o for b, o in order])
    colr = np.array([b * 64 + o for b, o in rolled])

    def stacked(w):
        z = twice(turned(w))
        return np.ascontiguousarray(np.stack([z[:, cols], z[:, colr]], 1))

    def both(v):
        return np.concatenate([v, v])

    bq, bk = both(a["L1_xattn_bq"]), both(a["L1_xattn_bk"])
    bias = np.stack([bq[cols], bq[colr], bk[cols], bk[colr], both(a["L1_xattn_bv"]), both(a["L1_xattn_bo"])], 1)
    inv_freq = f(1.0) / f(10000.0) ** (np.arange(0, HC, 2, dtype=f) / f(HC))
    angle = np.arange(D, dtype=f)[:, None] * inv_freq[None, :]
    ch = np.array([o % HC for _, o in order])
    cos = np.cos(angle)[:, ch % 4].T
    sin = np.sin(angle)[:, ch % 4].T * np.where(ch < HC // 2, f(-1), f(1))[:, None]
    n = np.arange(NTILE)
    ctx = a["ctx_2048"]
    arrays = {
        "x": a["x"], "ctx": ctx,
        "ctxT": np.ascontiguousarray(ctx.reshape(UNITS, 2, 2 * S, D).transpose(3, 0, 1, 2)),
        "wq": turned(a["L0_xattn_wq"]), "wk": turned(a["L0_xattn_wk"]),
        "wv": turned(a["L0_xattn_wv"]), "wo": turned(a["L0_xattn_wo"]),
        "wg": turned(a["L0_ffn_w_gate"]), "wu": np.ascontiguousarray(turned(a["L0_ffn_w_up"]).reshape(16, 16, FF).swapaxes(0, 1)).reshape(D, FF), "wd": turned(a["L0_ffn_w_down"]),
        "wqb": stacked(a["L1_xattn_Wq"]), "wkb": stacked(a["L1_xattn_Wk"]),
        "wvb": twice(turned(a["L1_xattn_Wv"])), "wob": twice(turned(a["L1_xattn_Wo"])),
        "bias": bias, "cos": np.ascontiguousarray(cos, f), "sin": np.ascontiguousarray(sin, f),
        "gamma": a["L1_ffn_ln_gamma"][None, :], "beta": a["L1_ffn_ln_beta"][None, :],
        "bases": a["L1_ffn_spline_bases"].reshape(NTILE, 64), "slopes": a["L1_ffn_spline_slopes"].reshape(NTILE, 64),
        "slopes_row": a["L1_ffn_spline_slopes"].reshape(1, NTILE * 64),
        "oscale": a["L1_ffn_output_scale"][:, None],
        "ident": np.eye(P, dtype=f),
        "ckey": (-(n // 8) * 128 - n % 8).astype(f)[None, :], "giota": np.arange(GRID, dtype=f)[None, :],
    }
    nc = bacc.Bacc("TRN2", target_bir_lowering=False, num_devices=1)
    feed, A = {}, {}
    for name, v in arrays.items():
        v = np.ascontiguousarray(v)
        feed["in_" + name] = v
        A[name] = nc.dram_tensor("in_" + name, v.shape, mybir.dt.from_np(v.dtype), kind="ExternalInput").ap()
    out = nc.dram_tensor("out_x", (B, S, D), F32, kind="ExternalOutput").ap()
    decoder_kernel(nc, A, out)
    r = run_bass_kernel_spmd(nc, [feed], core_ids=[0])
    return r.results[0]["out_x"]
```
